# Optimizing a Trainium2 kernel written in Bass

```python
import numpy as np
import jax
import jax.numpy as jnp

def _softmax(x, axis=-1):
    return jax.nn.softmax(x, axis=axis)

def _gelu(x):
    return jax.nn.gelu(x, approximate=True)

def _silu(x):
    return jax.nn.silu(x)

def _sigmoid(x):
    return jax.nn.sigmoid(x)

def _layernorm(x, axis=-1, eps=1e-05):
    m = jnp.mean(x, axis=axis, keepdims=True)
    v = jnp.var(x, axis=axis, keepdims=True)
    return (x - m) / jnp.sqrt(v + eps)

def _scatter_add(tgt, idx, src, axis=0):
    return tgt.at[idx].add(src)

def _segment_sum(src, seg, n):
    return jax.ops.segment_sum(src, seg, n)
kernel_name = 'mk_gnn_resnorm_d4_gnn_r8_531968'

def setup_inputs(seed: int=0):
    np.random.seed(seed)
    _w = jnp.asarray

    def _rec_inputs():
        import jax
        import jax.numpy as jnp
        _gk = jax.random.key(seed)
        x = -0.0002928 + 1 * jax.random.normal(jax.random.fold_in(_gk, 1), (1024, 512), jnp.float32)
        _s = jax.random.randint(jax.random.fold_in(_gk, 2), (16384,), 0, 1024, jnp.int32)
        _d = jax.random.randint(jax.random.fold_in(_gk, 3), (16384,), 0, 1024, jnp.int32)
        _loop = jnp.arange(1024, dtype=jnp.int32)
        src = jnp.concatenate([_s, _d, _loop])
        dst = jnp.concatenate([_d, _s, _loop])
        _o = jnp.argsort(dst, stable=True)
        src = src[_o]
        dst = dst[_o]
        edge_attr_128 = 0.000283511 + 1.00007 * jax.random.normal(jax.random.fold_in(_gk, 12), (33792, 128), jnp.float32)
        return (x, src, dst, edge_attr_128)
    x, src, dst, edge_attr_128 = _rec_inputs()

    def _L0_gnn_setup():
        import jax, jax.numpy as jnp
        import numpy as np
        N, E, D_IN, D_OUT = (1024, 32768, 512, 512)
        key = jax.random.key(seed)
        k1, k2, k3 = jax.random.split(key, 3)
        x = jax.random.normal(k1, (N, D_IN), dtype=jnp.float32)
        edge_index = jax.random.randint(k2, (2, E), 0, N, dtype=jnp.int64)
        limit = float(np.sqrt(6.0 / (D_IN + D_OUT)))
        weight = jax.random.uniform(k3, (D_IN, D_OUT), dtype=jnp.float32, minval=-limit, maxval=limit)
        bias = jnp.zeros((D_OUT,), dtype=jnp.float32)
        return {'x': x, 'edge_index': edge_index, 'weight': weight, 'bias': bias}
    _L0_gnn_all = _L0_gnn_setup()
    _L0_gnn_in = {k: v for k, v in _L0_gnn_all.items() if k in ('weight', 'bias')}
    del _L0_gnn_all

    def _L1_gnn_setup():
        import jax, jax.numpy as jnp
        import numpy as np
        N, E = (1250, 18750)
        HD, ED = (512, 128)
        BN_EPS = 1e-05
        key = jax.random.key(seed)
        ks = jax.random.split(key, 16)
        s = 0.02
        return {'h': jax.random.normal(ks[0], (N, HD), jnp.float32), 'edge_index': jax.random.randint(ks[1], (2, E), 0, N, jnp.int32), 'edge_attr': jax.random.normal(ks[2], (E, ED), jnp.float32), 'W1': jax.random.normal(ks[3], (HD, HD + ED), jnp.float32) * s, 'b1': jnp.zeros((HD,), jnp.float32), 'W2': jax.random.normal(ks[4], (HD, HD), jnp.float32) * s, 'b2': jnp.zeros((HD,), jnp.float32), 'W_ih': jax.random.normal(ks[5], (3 * HD, HD), jnp.float32) * s, 'W_hh': jax.random.normal(ks[6], (3 * HD, HD), jnp.float32) * s, 'b_ih': jnp.zeros((3 * HD,), jnp.float32), 'b_hh': jnp.zeros((3 * HD,), jnp.float32), 'gamma': jnp.ones((HD,), jnp.float32), 'beta': jnp.zeros((HD,), jnp.float32), 'run_mean': jnp.zeros((HD,), jnp.float32), 'run_var': jnp.ones((HD,), jnp.float32)}
    _L1_gnn_all = _L1_gnn_setup()
    _L1_gnn_in = {k: v for k, v in _L1_gnn_all.items() if k in ('W1', 'b1', 'W2', 'b2', 'W_ih', 'W_hh', 'b_ih', 'b_hh', 'gamma', 'beta', 'run_mean', 'run_var')}
    del _L1_gnn_all

    def _L2_gnn_setup():
        import jax, jax.numpy as jnp
        import numpy as np
        N = 2500
        E = 31250
        B = 128
        Fin = 512
        Fqk = 512
        Fv = 512
        H = 8
        key = jax.random.key(seed)
        k1, k2, k3, k4 = jax.random.split(key, 4)
        x = jax.random.normal(k1, (N, Fin), dtype=jnp.float32)
        batch = jnp.sort(jax.random.randint(k2, (N,), 0, B)).astype(jnp.int32)
        ei = jax.random.randint(k3, (2, E), 0, N).astype(jnp.int32)
        W = jax.random.normal(k4, (Fin, 2 * Fqk + Fv), dtype=jnp.float32) / np.sqrt(Fin).astype(np.float32)
        return {'x': x, 'batch': batch, 'ei': ei, 'W': W}
    _L2_gnn_all = _L2_gnn_setup()
    _L2_gnn_in = {k: v for k, v in _L2_gnn_all.items() if k in ('W',)}
    del _L2_gnn_all

    def _L3_gnn_setup():
        import jax, jax.numpy as jnp
        import numpy as np
        N = 6250
        IN_CH = 512
        OUT_CH = 512
        DEG = 32
        E = N * DEG
        key = jax.random.key(seed)
        kx, kwc, kwn, kb, ke = jax.random.split(key, 5)
        x = jax.random.normal(kx, (N, IN_CH), dtype=jnp.float32)
        bound = 1.0 / np.sqrt(IN_CH)
        wc = jax.random.uniform(kwc, (IN_CH, OUT_CH), minval=-bound, maxval=bound, dtype=jnp.float32)
        wn = jax.random.uniform(kwn, (IN_CH, OUT_CH), minval=-bound, maxval=bound, dtype=jnp.float32)
        bias = jax.random.uniform(kb, (OUT_CH,), minval=-bound, maxval=bound, dtype=jnp.float32)
        src = jnp.repeat(jnp.arange(N, dtype=jnp.int64), DEG)
        dst = jax.random.randint(ke, (E,), 0, N, dtype=jnp.int64)
        edge_index = jnp.stack([src, dst], axis=0)
        return {'x': x, 'wc': wc, 'wn': wn, 'bias': bias, 'edge_index': edge_index}
    _L3_gnn_all = _L3_gnn_setup()
    _L3_gnn_in = {k: v for k, v in _L3_gnn_all.items() if k in ('wc', 'wn', 'bias')}
    del _L3_gnn_all
    return {'x': x, 'src': src, 'dst': dst, 'edge_attr_128': edge_attr_128, 'L0_gnn_weight': _L0_gnn_in['weight'], 'L0_gnn_bias': _L0_gnn_in['bias'], 'L1_gnn_W1': _L1_gnn_in['W1'], 'L1_gnn_b1': _L1_gnn_in['b1'], 'L1_gnn_W2': _L1_gnn_in['W2'], 'L1_gnn_b2': _L1_gnn_in['b2'], 'L1_gnn_W_ih': _L1_gnn_in['W_ih'], 'L1_gnn_W_hh': _L1_gnn_in['W_hh'], 'L1_gnn_b_ih': _L1_gnn_in['b_ih'], 'L1_gnn_b_hh': _L1_gnn_in['b_hh'], 'L1_gnn_gamma': _L1_gnn_in['gamma'], 'L1_gnn_beta': _L1_gnn_in['beta'], 'L1_gnn_run_mean': _L1_gnn_in['run_mean'], 'L1_gnn_run_var': _L1_gnn_in['run_var'], 'L2_gnn_W': _L2_gnn_in['W'], 'L3_gnn_wc': _L3_gnn_in['wc'], 'L3_gnn_wn': _L3_gnn_in['wn'], 'L3_gnn_bias': _L3_gnn_in['bias']}

def reference(x, src, dst, edge_attr_128, L0_gnn_weight, L0_gnn_bias, L1_gnn_W1, L1_gnn_b1, L1_gnn_W2, L1_gnn_b2, L1_gnn_W_ih, L1_gnn_W_hh, L1_gnn_b_ih, L1_gnn_b_hh, L1_gnn_gamma, L1_gnn_beta, L1_gnn_run_mean, L1_gnn_run_var, L2_gnn_W, L3_gnn_wc, L3_gnn_wn, L3_gnn_bias):
    import jax
    import jax.numpy as jnp

    def _L0_gnn_ref(x, edge_index, weight, bias):
        import jax, jax.numpy as jnp
        import numpy as np
        N, E, D_IN, D_OUT = (1024, 32768, 512, 512)
        support = x @ weight
        n = x.shape[0]
        adj = jnp.zeros((n, n), dtype=x.dtype).at[edge_index[0], edge_index[1]].set(1.0)
        adj = adj + jnp.eye(n, dtype=x.dtype)
        degree = adj.sum(axis=1, keepdims=True)
        d_inv_sqrt = jnp.where(degree > 0, jax.lax.rsqrt(degree), 0.0)
        adj_normalized = d_inv_sqrt * adj * d_inv_sqrt.T
        out = adj_normalized @ support + bias
        return out

    def _L1_gnn_ref(h, edge_index, edge_attr, W1, b1, W2, b2, W_ih, W_hh, b_ih, b_hh, gamma, beta, run_mean, run_var):
        import jax, jax.numpy as jnp
        import numpy as np
        N, E = (1250, 18750)
        HD, ED = (512, 128)
        BN_EPS = 1e-05
        src, dst = (edge_index[0], edge_index[1])
        m_in = jnp.concatenate([h[src], edge_attr], axis=1)
        m = jax.nn.relu(m_in @ W1.T + b1) @ W2.T + b2
        agg = jax.ops.segment_sum(m, dst, num_segments=h.shape[0])
        gi = agg @ W_ih.T + b_ih
        gh = h @ W_hh.T + b_hh
        i_r, i_z, i_n = jnp.split(gi, 3, axis=1)
        h_r, h_z, h_n = jnp.split(gh, 3, axis=1)
        r = jax.nn.sigmoid(i_r + h_r)
        z = jax.nn.sigmoid(i_z + h_z)
        n = jnp.tanh(i_n + r * h_n)
        h_new = (1.0 - z) * n + z * h
        bn = gamma * (h_new - run_mean) * jax.lax.rsqrt(run_var + BN_EPS) + beta
        return h + bn

    def _L2_gnn_ref(x, batch, ei, W):
        import jax, jax.numpy as jnp
        import numpy as np
        N = 2500
        E = 31250
        B = 128
        Fin = 512
        Fqk = 512
        Fv = 512
        H = 8
        src, dest = (ei[0], ei[1])
        n = x.shape[0]
        Fh = Fqk // H
        Fhv = Fv // H
        scaling = float(Fh) ** (-0.5)
        qkv = x @ W
        q, k, v = jnp.split(qkv, [Fqk, 2 * Fqk], axis=-1)
        q = (q * scaling).reshape(n, H, Fh)
        k = k.reshape(n, H, Fh)
        v = v.reshape(n, H, Fhv)
        qs = q[src]
        ks = k[dest]
        vs = v[dest]
        aw = jnp.einsum('ehf,ehf->eh', qs, ks)
        m = jax.ops.segment_max(aw, src, num_segments=n)
        e = jnp.exp(aw - m[src])
        denom = jax.ops.segment_sum(e, src, num_segments=n)
        alpha = e / denom[src]
        out = jax.ops.segment_sum(alpha[:, :, None] * vs, src, num_segments=n)
        return out.reshape(n, Fv)

    def _L3_gnn_ref(x, wc, wn, bias, edge_index):
        import jax, jax.numpy as jnp
        import numpy as np
        N = 6250
        IN_CH = 512
        OUT_CH = 512
        DEG = 32
        E = N * DEG
        alpha = x @ wc
        beta = x @ wn
        src, dst = (edge_index[0], edge_index[1])
        sums = jax.ops.segment_sum(beta[dst], src, num_segments=x.shape[0])
        counts = jax.ops.segment_sum(jnp.ones_like(src, dtype=beta.dtype), src, num_segments=x.shape[0])
        gamma = sums / counts[:, None]
        return alpha + gamma + bias
    edge_index = jnp.stack([src, dst])
    batch0 = jnp.zeros((1024,), jnp.int32)
    x = _layernorm(x + _L0_gnn_ref(x, edge_index, L0_gnn_weight, L0_gnn_bias), axis=-1)
    x = _layernorm(x + _L1_gnn_ref(x, edge_index, edge_attr_128, L1_gnn_W1, L1_gnn_b1, L1_gnn_W2, L1_gnn_b2, L1_gnn_W_ih, L1_gnn_W_hh, L1_gnn_b_ih, L1_gnn_b_hh, L1_gnn_gamma, L1_gnn_beta, L1_gnn_run_mean, L1_gnn_run_var), axis=-1)
    x = _layernorm(x + _L2_gnn_ref(x, batch0, edge_index, L2_gnn_W), axis=-1)
    x = _layernorm(x + _L3_gnn_ref(x, L3_gnn_wc, L3_gnn_wn, L3_gnn_bias, edge_index), axis=-1)
    return x

_drawn_inputs = setup_inputs


def setup_inputs(seed=0):
    import zlib

    import numpy as np

    out = dict(_drawn_inputs(seed))
    spreads = {'L0_gnn_bias': (0.0, 0.1),
     'L1_gnn_b1': (0.0, 0.1),
     'L1_gnn_b2': (0.0, 0.1),
     'L1_gnn_b_ih': (0.0, 0.416),
     'L1_gnn_b_hh': (0.0, 0.534),
     'L1_gnn_gamma': (1.0, 0.2),
     'L1_gnn_beta': (0.0, 0.1),
     'L1_gnn_run_mean': (0.0, 0.1),
     'L1_gnn_run_var': (1.0, 0.2)}
    factors = {'L3_gnn_bias': 2.793}
    for name, (base, spread) in spreads.items():
        noise = np.random.default_rng([zlib.crc32(name.encode()), seed]).standard_normal(out[name].shape)
        drawn = base * np.exp(spread * noise) if base else spread * noise
        out[name] = jnp.asarray(drawn.astype(out[name].dtype))
    for name, factor in factors.items():
        out[name] = (out[name] * factor).astype(out[name].dtype)
    return out
```

```python
from contextlib import ExitStack

import concourse.bass as bass
from concourse import mybir

ALU = mybir.AluOpType
ACT = mybir.ActivationFunctionType
F32 = mybir.dt.float32
F16 = mybir.dt.float16
BF16 = mybir.dt.bfloat16
I32 = mybir.dt.int32
U16 = mybir.dt.uint16
AX_X = mybir.AxisListType.X

P = 128
KB = 256
EPS = 1e-5
FAR = 1.0e6
BIG = 1.0e30
TINY = 1.0e-30


def gnn_kernel(nc, x, x_t, src_t, dst_t, attr_t, w0, b0, w1h_t, w1e_t, b1, w2_t, b2, wih_t, whh_t,
               bih, bhh, gamma, beta, run_mean, run_var, wqkv, wc, wn, b3, out):
    N, D = x.shape
    EA, E = attr_t.shape
    NB = N // P
    KD = D // P
    SUPER = 2
    TILES = E // P
    SUPERS = TILES // SUPER
    RING = 4
    NV = -(-(SUPERS + NB - 1) // RING) * RING
    TURNS = NV // RING
    NT = NV * SUPER
    H = 8
    DH = D // H
    assert EA == P and TILES * P == E and TILES % SUPER == 0 and SUPER == 2 and N == 2 * 512 and D == 512

    p_dram = nc.dram_tensor("messages_dram", [N, D], F32, kind="Internal").ap()

    with ExitStack() as ctx:
        def sb(name, shape, dt):
            return ctx.enter_context(nc.sbuf_tensor(name, shape, dt))

        def sem(name):
            return ctx.enter_context(nc.semaphore(name))

        arena = sb("arena", [P, 190 * KB], F32)

        def at(kb, size_kb):
            return arena[:, int(kb * KB):int((kb + size_kb) * KB)]

        def rows(kb, n, width):
            return at(kb, n * width / KB).rearrange("p (a b) -> p a b", a=n)

        ct = rows(0, NB, N)
        xn = rows(32, NB, D)
        b0_s, b1_s = at(48, 2), at(50, 2)
        brz_s, bhh_rz = at(52, 4), at(56, 4)
        bin_s, bhn_s = at(60, 2), at(62, 2)
        bn_a, bn_b = at(64, 2), at(66, 2)
        mean_s, var_s = at(68, 2), at(70, 2)
        y_s = rows(72, 2, D)
        xt = rows(76, KD, N)
        sup = rows(92, NB, D)
        w0_s = rows(108, KD, D)
        adj = rows(116, NB, N)
        oh_src = at(116, 8).bitcast(BF16).rearrange("p (v j n) -> p v j n", v=2, j=SUPER)
        oh_dst = at(124, 1).bitcast(BF16).rearrange("p (v j n) -> p v j n", v=2, j=SUPER)
        iota_i = at(186, 4).bitcast(I32)
        edge_i = at(126, 3)[:, 0:2 * TILES].bitcast(I32).rearrange("p (a t) -> p a t", a=2)
        dst_f, src_f, plan_t = (at(kb, 2)[:, 0:NT].rearrange("p (v j) -> p v j", j=SUPER) for kb in (129, 131, 133))
        tile_f, is_k = at(135, 1)[:, 0:NV], at(136, 1)[:, 0:NV]
        w1h_s = rows(148, KD, D)
        p_s = rows(156, 4, D)
        w1e_s = at(164, 2)
        w2_s = rows(166, KD, D)
        agg = rows(92, NB, D)
        attr_s = rows(108, RING, SUPER * P)
        gath = at(112, 16).rearrange("p (v j n) -> p v j n", v=RING, j=SUPER)
        msg = rows(128, 4, D)
        oh_edge = rows(136, 4, P)
        whh_s = rows(138, KD, 3 * D)
        wih_a = rows(174, 2, 3 * D)
        wih_b = rows(108, 2, 3 * D)
        agg_t = rows(120, KD, N)
        m_t = rows(92, KD, N)
        indeg_row = at(162, 4)[0:1, :]
        rz_s = rows(120, 2, 2 * D)
        n_s = rows(128, 2, D)
        d_s = rows(132, 2, D)
        x2t = rows(76, KD, N)
        q_t = rows(92, KD, N)
        k_t = rows(108, KD, N)
        v_s = rows(124, NB, D)
        wk_s, wv_s, wc_s = rows(140, KD, D), rows(148, KD, D), rows(156, KD, D)
        wq_s, wn_s = rows(164, KD, D), rows(172, KD, D)
        cnt_n = at(48, 16).bitcast(U16).rearrange("p (i n) -> p i n", i=NB)
        no_edge = at(140, 16).bitcast(BF16).rearrange("p (i n) -> p i n", i=NB)
        logit = rows(64, 2, N)
        prob = rows(164, 2, N)
        prob_t = rows(180, 2, N)
        att = rows(76, NB, D)
        x3t = rows(92, KD, N)
        bet = rows(108, NB, D)

        ident = sb("ident", [P, P], F32)
        ones = sb("ones", [P, P], F32)
        node_h = sb("node_h", [P, N], F16)
        node_f = sb("node_f", [P, P], F32)
        visit_f = sb("visit_f", [P, NV], F32)
        dst_v = sb("dst_v", [P, NV, SUPER], F32)
        src_v = sb("src_v", [P, NV, SUPER], F32)
        src_i = sb("src_i", [P, NV, SUPER], I32)
        rel = sb("rel", [P, NV, SUPER], F32)
        blk = sb("blk", [P, NV], F32)
        blk_r = sb("blk_r", [P, NV], F32)
        blk_i = sb("blk_i", [P, NV], I32)
        tile_i = sb("tile_i", [P, NV], I32)
        below = sb("below", [P, NB], F32)
        first_i = sb("first_i", [P, NB], I32)
        first_f = sb("first_f", [P, NB], F32)
        hits = sb("hits", [P, 1], F32)
        covered = sb("covered", [P, 1], F32)
        open_f = sb("open_f", [P, 1], F32)
        open_p = sb("open_p", [P, 1], F32)
        rounds_f = sb("rounds_f", [P, 1], F32)
        rounds_i = sb("rounds_i", [P, 1], I32)
        idx = sb("idx", [P, RING, SUPER], I32)
        eps_s = sb("eps_s", [P, 1], F32)
        dinv = sb("dinv", [P, NB], F32)
        indeg = sb("indeg", [P, NB], F32)
        outdeg = sb("outdeg", [P, NB], F32)
        r_out = sb("r_out", [P, NB], F32)
        stats = sb("stats", [P, 4 * NB, 6], F32)
        mv = sb("mv", [P, 4 * NB, 2], F32)
        std = sb("std", [P, 4 * NB], F32)
        rstd = sb("rstd", [P, 4 * NB], F32)
        b2_row = sb("b2_row", [1, D], F32)
        b3_s = sb("b3_s", [P, D], F32)
        low = sb("low", [P, H * NB], F32)
        den = sb("den", [P, H * NB], F32)
        rden = sb("rden", [P, H * NB], F32)

        ps = ctx.enter_context(nc.psum_tensor("ps", [P, 8, 512], F32))

        phase = sem("phase")
        s_edges, s_x, s_xt, s_w0, s_bias, s_w1h, s_w1e, s_w2 = (sem(f"loaded_{n}") for n in
            ("edges", "x", "xt", "w0", "bias", "w1h", "w1e", "w2"))
        s_whh, s_wih, s_wq, s_wkv, s_wcn = (sem(f"loaded_{n}") for n in ("whh", "wih", "wq", "wkv", "wcn"))
        s_attr = [sem(f"attr_loaded_{u}") for u in range(RING)]
        s_gath = [sem(f"gathered_{u}") for u in range(RING)]
        s_pw = [sem(f"messages_stored_{u}") for u in range(4)]
        s_out = [sem(f"out_stored_{u}") for u in range(2)]
        const_set = sem("const_set")
        dve_step = sem("dve_step")
        act_step = sem("act_step")
        pool_step = sem("pool_step")
        idx_set = sem("idx_set")
        xb_set = sem("xb_set")
        below_set, below_sum, hits_set, hits_sum = (sem(n) for n in ("below_set", "below_sum", "hits_set", "hits_sum"))
        plan_set = sem("plan_set")
        rounds_done = sem("rounds_done")
        sup_mm, sup_out = sem("sup_mm"), sem("sup_out")
        onehot_set, count_mm, count_added, tables_set, edge_tables_set = (sem(n) for n in
            ("onehot_set", "count_mm", "count_added", "tables_set", "edge_tables_set"))
        adj_set, deg_mm, dinv_std, dinv_set, sup_scaled = (sem(n) for n in ("adj_set", "deg_mm", "dinv_std", "dinv_set", "sup_scaled"))
        l0_mm, y_set, var_set, std_set, x_set = (sem(n) for n in ("l0_mm", "y_set", "var_set", "std_set", "x_set"))
        t_mm, t_out, p_mm, p_out = (sem(n) for n in ("t_mm", "t_out", "p_mm", "p_out"))
        attr_mm, pre_set, msg_set, edge_hot, agg_mm, agg_added = (sem(n) for n in
            ("attr_mm", "pre_set", "msg_set", "edge_hot", "agg_mm", "agg_added"))
        row_mm, row_out, mt_mm, mt_out, gate_mm, rz_pre, rz_set, n_pre, n_set, gate_free, bn_std = (sem(n) for n in
            ("row_mm", "row_out", "mt_mm", "mt_out", "gate_mm", "rz_pre", "rz_set", "n_pre", "n_set", "gate_free", "bn_std"))
        qkv_mm, qkv_out, cn_mm, cn_out, mask_out = (sem(n) for n in ("qkv_mm", "qkv_out", "cn_mm", "cn_out", "mask_out"))
        s_mm, s_low, s_exp, s_prob, s_tr, s_tout, s_pv, s_att = (sem(n) for n in
            ("score_mm", "low_set", "exp_set", "prob_set", "prob_tr", "prob_t_set", "pv_mm", "att_set"))
        bet_mm, bet_out, l3_mm, l3_y, x3b_set = (sem(n) for n in ("bet_mm", "bet_out", "l3_mm", "l3_y", "x3b_set"))

        def end_phase(eng, n):
            eng.drain().then_inc(phase, 1)
            eng.wait_ge(phase, 4 * n)

        def rounds(eng, body):
            eng.wait_ge(plan_set, 1)
            n = eng.value_load(rounds_i[0:1, 0:1], min_val=1, max_val=NB)
            with eng.Fori(0, NB) as r:
                with eng.If(r < n):
                    body(r)

        block = ctx.enter_context(nc.Block())

        @block.sync
        def _(sp):
            sp.dma_start(edge_i[:, 0, :], dst_t).then_inc(s_edges, 16)
            sp.dma_start(edge_i[:, 1, :], src_t).then_inc(s_edges, 16)
            sp.dma_start(w0_s, w0.rearrange("(k p) n -> p k n", p=P)).then_inc(s_w0, 16)
            sp.dma_start(xt, x_t.rearrange("(k p) n -> p k n", p=P)).then_inc(s_xt, 16)
            sp.dma_start(xn, x.rearrange("(b p) n -> p b n", p=P)).then_inc(s_x, 16)
            for dest, vec in ((b0_s, b0), (b1_s, b1), (brz_s, bih[0:2 * D]), (bhh_rz, bhh[0:2 * D]),
                              (bin_s, bih[2 * D:3 * D]), (bhn_s, bhh[2 * D:3 * D]), (bn_a, gamma),
                              (bn_b, beta), (mean_s, run_mean), (var_s, run_var), (b3_s[:], b3)):
                sp.dma_start(dest, vec.partition_broadcast(P)).then_inc(s_bias, 16)
            sp.dma_start(b2_row[:], b2.rearrange("(a n) -> a n", a=1)).then_inc(s_bias, 16)
            sp.dma_start(w1h_s, w1h_t.rearrange("(k p) n -> p k n", p=P)).then_inc(s_w1h, 16)
            sp.dma_start(w1e_s, w1e_t).then_inc(s_w1e, 16)
            sp.dma_start(w2_s, w2_t.rearrange("(k p) n -> p k n", p=P)).then_inc(s_w2, 16)
            sp.dma_start(wih_a, wih_t[0:2 * P, :].rearrange("(k p) n -> p k n", p=P)).then_inc(s_wih, 16)
            for i in range(NB):
                sp.wait_ge(p_out, i + 1)
                sp.dma_start(p_dram[i * P:(i + 1) * P, :], p_s[:, i % 4, :]).then_inc(s_pw[i % 4], 16)
            sp.wait_ge(phase, 8)
            for u in range(4):
                sp.wait_ge(s_pw[u], 32)
            sp.dma_start(whh_s, whh_t.rearrange("(k p) n -> p k n", p=P)).then_inc(s_whh, 16)

            def edge_round(r):
                with sp.Fori(0, TURNS) as turn:
                    for u in range(RING):
                        v = turn * RING + u
                        first = sp.value_load(tile_i[0:1, bass.ds(v, 1)], min_val=0, max_val=SUPERS - 1)
                        sp.wait_ge(attr_mm, r * NT + v * SUPER + 2)
                        sp.dma_start(attr_s[:, u, :], attr_t[:, bass.ds(first * (SUPER * P), SUPER * P)])\
                          .then_inc(s_attr[u], 16)
            rounds(sp, edge_round)
            sp.wait_ge(phase, 12)
            sp.dma_start(wih_b, wih_t[2 * P:4 * P, :].rearrange("(k p) n -> p k n", p=P)).then_inc(s_wih, 16)
            sp.wait_ge(mt_mm, 2 * KD)
            sp.dma_start(wq_s, wqkv[:, 0:D].rearrange("(k p) n -> p k n", p=P)).then_inc(s_wq, 16)
            sp.wait_ge(gate_mm, NB)
            sp.dma_start(wk_s, wqkv[:, D:2 * D].rearrange("(k p) n -> p k n", p=P)).then_inc(s_wkv, 16)
            sp.dma_start(wv_s, wqkv[:, 2 * D:3 * D].rearrange("(k p) n -> p k n", p=P)).then_inc(s_wkv, 16)
            sp.dma_start(wc_s, wc.rearrange("(k p) n -> p k n", p=P)).then_inc(s_wcn, 16)
            sp.dma_start(wn_s, wn.rearrange("(k p) n -> p k n", p=P)).then_inc(s_wcn, 16)
            for i in range(NB):
                sp.wait_ge(x_set, 3 * NB + i + 1)
                sp.dma_start(out[i * P:(i + 1) * P, :], xn[:, i, :]).then_inc(s_out[i % 2], 16)
            for u in range(2):
                sp.wait_ge(s_out[u], 16 * (NB // 2))

        @block.gpsimd
        def _(pool):
            pool.memset(ident[:], 0.0).then_inc(pool_step, 1)
            pool.iota(iota_i, pattern=[[1, N]], base=0, channel_multiplier=0).then_inc(pool_step, 1)
            pool.memset(ones[:], 1.0).then_inc(const_set, 1)
            pool.memset(eps_s[:], EPS).then_inc(const_set, 1)
            pool.wait_ge(pool_step, 2)
            pool.affine_select(out=ident[:], in_=ident[:], compare_op=ALU.not_equal, fill=1.0, base=0,
                               pattern=[[-1, P]], channel_multiplier=1).then_inc(const_set, 1)
            pool.tensor_copy(node_f[:], iota_i[:, 0:P]).then_inc(const_set, 1)
            pool.tensor_copy(visit_f[:], iota_i[:, 0:NV]).then_inc(const_set, 1)
            pool.tensor_copy(node_h[:], iota_i).then_inc(const_set, 1)
            pool.wait_ge(s_x, 16)
            pool.wait_ge(s_bias, 12 * 16)
            for i in range(NB):
                pool.tensor_tensor(xn[:, i, :], xn[:, i, :], b0_s, ALU.add).then_inc(xb_set, 1)
            pool.tensor_tensor(brz_s, brz_s, bhh_rz, ALU.add).then_inc(xb_set, 1)
            end_phase(pool, 1)
            end_phase(pool, 2)
            for u in range(4):
                pool.wait_ge(s_pw[u], 32)

            def gather_round(r):
                with pool.Fori(0, TURNS) as turn:
                    for u in range(RING):
                        v = turn * RING + u
                        pool.wait_ge(pre_set, r * NT + v * SUPER + 2)
                        pool.sem_inc(pool_step, 1)
                        pool.tensor_copy(idx[:, u, :], src_i[:, bass.ds(v, 1), :].rearrange("p a j -> p (a j)"))\
                            .then_inc(idx_set, 1)
                        pool.wait_ge(idx_set, r * NV + v + 1)
                        pool.sem_inc(pool_step, 1)
                        for j in range(SUPER):
                            pool.indirect_dma_start(
                                out=gath[:, u, j, :], out_offset=None, in_=p_dram,
                                in_offset=bass.IndirectOffsetOnAxis(ap=idx[:, u, j:j + 1], axis=0),
                            ).then_inc(s_gath[u], 16)
            rounds(pool, gather_round)
            end_phase(pool, 3)
            end_phase(pool, 4)
            end_phase(pool, 5)
            end_phase(pool, 6)

        @block.scalar
        def _(act):
            def layer_std(n):
                act.wait_ge(var_set, n + 1)
                act.activation(std[:, n:n + 1], mv[:, n, 1:2], ACT.Sqrt, bias=eps_s[:, 0:1]).then_inc(std_set, 1)

            def turned(n, dest, bank):
                act.wait_ge(t_mm, n + 1)
                i = n % NB
                act.activation(dest[:, :, i * P:(i + 1) * P],
                               ps[:, bank, :].rearrange("p (k n) -> p k n", k=KD), ACT.Copy).then_inc(t_out, 1)

            for i in range(NB):
                act.wait_ge(sup_mm, i + 1)
                act.activation(sup[:, i, :], ps[:, i % 4, :], ACT.Copy).then_inc(sup_out, 1)
            end_phase(act, 1)
            for b in range(NB):
                if b:
                    act.wait_ge(act_step, b)
                act.activation(rows(156, 1, N)[:, 0, :], ct[:, b, :], ACT.Copy, accum_out=indeg[:, b:b + 1])\
                   .then_inc(act_step, 1)
            act.wait_ge(deg_mm, 1)
            act.activation(dinv[:], ps[:, 7, 0:NB], ACT.Sqrt).then_inc(dinv_std, 1)
            act.wait_ge(dinv_set, 1)
            for b in range(NB):
                act.activation(sup[:, b, :], sup[:, b, :], ACT.Copy, scale=dinv[:, b:b + 1]).then_inc(sup_scaled, 1)
            for i in range(NB + 2):
                if i < NB:
                    layer_std(i)
                if i >= 2:
                    turned(i - 2, xt, 4 + i % 2)
            end_phase(act, 2)

            def relu_round(r):
                with act.Fori(0, TURNS) as turn:
                    for u in range(RING):
                        v = turn * RING + u
                        for j in range(SUPER):
                            t = r * NT + v * SUPER + j
                            n = SUPER * u + j
                            act.wait_ge(pre_set, t + 9)
                            act.activation(msg[:, n % 4, :], msg[:, n % 4, :], ACT.Relu).then_inc(msg_set, 1)
            rounds(act, relu_round)
            end_phase(act, 3)
            for b in range(NB):
                turned(NB + b, agg_t, b % 2)
            act.activation(var_s, var_s, ACT.Sqrt, bias=eps_s[:, 0:1]).then_inc(bn_std, 1)
            for c in range(2):
                act.wait_ge(row_mm, c + 1)
                act.activation(indeg_row[0:1, c * 512:(c + 1) * 512], ps[0:1, 2 + c, :], ACT.Copy).then_inc(row_out, 1)
            for g in range(2 * KD):
                act.wait_ge(mt_mm, g + 1)
                act.activation(m_t[:, g % KD, (g // KD) * 512:(g // KD + 1) * 512], ps[:, 4 + g % 4, :], ACT.Copy)\
                   .then_inc(mt_out, 1)
            for i in range(NB + 1):
                if i < NB:
                    act.wait_ge(rz_pre, i + 1)
                    act.activation(rz_s[:, i % 2, :], rz_s[:, i % 2, :], ACT.Sigmoid).then_inc(rz_set, 1)
                    act.wait_ge(n_pre, i + 1)
                    act.activation(n_s[:, i % 2, :], n_s[:, i % 2, :], ACT.Tanh).then_inc(n_set, 1)
                if i:
                    layer_std(NB + i - 1)
            end_phase(act, 4)
            for i in range(NB):
                turned(2 * NB + i, x2t, i % 2)
            for i in range(NB):
                act.wait_ge(cn_mm, i + 1)
                act.activation(cnt_n[:, i, :], ps[:, 2 + 2 * (i % 2):4 + 2 * (i % 2), :].rearrange("p a n -> p (a n)"),
                               ACT.Copy, accum_out=outdeg[:, i:i + 1]).then_inc(cn_out, 1)
            for g in range(4 * KD + NB):
                act.wait_ge(qkv_mm, g + 1)
                bank = ps[:, 6 + g % 2, :]
                if g < 2 * KD:
                    act.activation(q_t[:, g % KD, (g // KD) * 512:(g // KD + 1) * 512], bank, ACT.Copy,
                                   scale=-float(DH) ** -0.5).then_inc(qkv_out, 1)
                elif g < 4 * KD:
                    n = g - 2 * KD
                    act.activation(k_t[:, n % KD, (n // KD) * 512:(n // KD + 1) * 512], bank, ACT.Copy)\
                       .then_inc(qkv_out, 1)
                else:
                    act.activation(v_s[:, g - 4 * KD, :], bank, ACT.Copy).then_inc(qkv_out, 1)
            end_phase(act, 5)

            def exps(u):
                act.wait_ge(s_low, u + 1)
                act.activation(logit[:, u % 2, :], logit[:, u % 2, :], ACT.Exp, bias=low[:, u:u + 1], scale=-1.0)\
                   .then_inc(s_exp, 1)

            def prob_out(u):
                act.wait_ge(s_tr, u + 1)
                if u >= 2:
                    act.wait_ge(s_pv, u - 1)
                act.activation(prob_t[:, u % 2, :], ps[:, 4:6, :].rearrange("p a n -> p (a n)"), ACT.Copy)\
                   .then_inc(s_tout, 1)
            U = H * NB
            for u in range(U + 2):
                if u < U:
                    exps(u)
                if u >= 2:
                    prob_out(u - 2)
            end_phase(act, 6)
            for i in range(NB + 2):
                if i < NB:
                    layer_std(2 * NB + i)
                if 1 <= i <= NB:
                    turned(3 * NB + i - 1, x3t, (i - 1) % 2)
                if i >= 2:
                    act.wait_ge(bet_mm, i - 1)
                    act.activation(bet[:, i - 2, :], ps[:, 2 + i % 2, :], ACT.Copy).then_inc(bet_out, 1)
            for i in range(NB):
                layer_std(3 * NB + i)

        @block.tensor
        def _(pe):
            def turn_block(n, source, bank, free=None):
                for k in range(KD):
                    mm = pe.transpose(ps[:, bank, k * P:(k + 1) * P], source[:, n % NB, k * P:(k + 1) * P], ident[:])
                mm.then_inc(t_mm, 1)

            pe.wait_ge(const_set, 6)
            pe.wait_ge(below_set, NB - 1)
            pe.matmul(ps[:, 6, 0:NB - 1], ones[:], below[:, 0:NB - 1], start=True, stop=True).then_inc(below_sum, 1)
            pe.wait_ge(s_w0, 16)
            pe.wait_ge(s_xt, 16)
            for i in range(NB):
                if i >= 4:
                    pe.wait_ge(sup_out, i - 3)
                for k in range(KD):
                    mm = pe.matmul(ps[:, i % 4, :], xt[:, k, i * P:(i + 1) * P], w0_s[:, k, :],
                                   start=(k == 0), stop=(k == KD - 1))
                mm.then_inc(sup_mm, 1)
            pe.wait_ge(hits_set, 1)
            pe.matmul(ps[:, 7, 0:1], ones[:], hits[:], start=True, stop=True).then_inc(hits_sum, 1)
            pe.sem_inc(count_mm, 2)
            pe.wait_ge(sup_out, NB)

            def count_round(r):
                with pe.Fori(0, TURNS) as turn:
                    for u in range(RING):
                        g = r * NV + turn * RING + u
                        pe.wait_ge(onehot_set, g + 1)
                        pe.wait_ge(count_added, g + 1)
                        for j in range(SUPER):
                            for c in range(2):
                                mm = pe.matmul(ps[:, 2 * (u % 2) + c, :], oh_dst[:, u % 2, j, :],
                                               oh_src[:, u % 2, j, c * 512:(c + 1) * 512],
                                               start=(j == 0), stop=(j == SUPER - 1))
                        mm.then_inc(count_mm, 1)
            rounds(pe, count_round)
            end_phase(pe, 1)

            pe.wait_ge(adj_set, NB)
            for i in range(NB):
                for b in range(NB):
                    mm = pe.matmul(ps[:, 7, i:i + 1], adj[:, b, i * P:(i + 1) * P], ones[:, 0:1],
                                   start=(b == 0), stop=(b == NB - 1))
            mm.then_inc(deg_mm, 1)
            pe.wait_ge(s_w1h, 16)
            for i in range(NB + 4):
                if i < NB:
                    if i >= 4:
                        pe.wait_ge(y_set, i - 3)
                    for b in range(NB):
                        if i == 0:
                            pe.wait_ge(sup_scaled, b + 1)
                        mm = pe.matmul(ps[:, i % 4, :], adj[:, b, i * P:(i + 1) * P], sup[:, b, :],
                                       start=(b == 0), stop=(b == NB - 1))
                    mm.then_inc(l0_mm, 1)
                if 2 <= i < NB + 2:
                    n = i - 2
                    pe.wait_ge(x_set, n + 1)
                    if n >= 2:
                        pe.wait_ge(t_out, n - 1)
                    turn_block(n, xn, 4 + n % 2)
                if i >= 4:
                    n = i - 4
                    pe.wait_ge(t_out, n + 1)
                    if n >= 2:
                        pe.wait_ge(p_out, n - 1)
                    for k in range(KD):
                        mm = pe.matmul(ps[:, 6 + n % 2, :], xt[:, k, n * P:(n + 1) * P], w1h_s[:, k, :],
                                       start=(k == 0), stop=(k == KD - 1))
                    mm.then_inc(p_mm, 1)
            end_phase(pe, 2)

            pe.sem_inc(attr_mm, 8)
            pe.sem_inc(agg_mm, 4)
            pe.wait_ge(s_w1e, 16)

            def edge_round(r):
                def attr_products(turn, n):
                    t = r * NT + turn * (RING * SUPER) + n
                    slot = n // SUPER % RING
                    if n % SUPER == 0:
                        pe.wait_ge(s_attr[slot], (r * TURNS + turn + n // (RING * SUPER)) * 16 + 16)
                    pe.wait_ge(pre_set, t + 5)
                    pe.matmul(ps[:, n % 4, :], attr_s[:, slot, (n % SUPER) * P:(n % SUPER + 1) * P], w1e_s,
                              start=True, stop=True).then_inc(attr_mm, 1)

                def body(turn, last):
                    for n in range(RING * SUPER):
                        if n + 3 < RING * SUPER or not last:
                            attr_products(turn, n + 3)
                        t = r * NT + turn * (RING * SUPER) + n
                        u, j = n // SUPER, n % SUPER
                        g = r * NV + turn * RING + u
                        pe.wait_ge(edge_hot, t + 1)
                        pe.wait_ge(msg_set, t + 1)
                        if j == 0:
                            pe.wait_ge(agg_added, g + 1)
                        pe.matmul(ps[:, 4 + u % 2, :], oh_edge[:, n % 4, :], msg[:, n % 4, :],
                                  start=(j == 0), stop=(j == SUPER - 1)).then_inc(agg_mm, 1)
                for n in range(3):
                    attr_products(0, n)
                with pe.Fori(0, TURNS - 1) as turn:
                    body(turn, False)
                body(TURNS - 1, True)
            rounds(pe, edge_round)
            end_phase(pe, 3)

            for b in range(NB):
                if b >= 2:
                    pe.wait_ge(t_out, NB + b - 1)
                turn_block(NB + b, agg, b % 2)
            for b in range(NB):
                mm = pe.transpose(ps[0:1, 2 + b // 4, (b % 4) * P:(b % 4 + 1) * P], indeg[:, b:b + 1], ident[:])
                if b % 4 == 3:
                    mm.then_inc(row_mm, 1)
            pe.wait_ge(s_w2, 16)
            pe.wait_ge(s_bias, 12 * 16)
            pe.wait_ge(t_out, 2 * NB)
            for g in range(2 * KD):
                c, m = g // KD, g % KD
                if g >= 4:
                    pe.wait_ge(mt_out, g - 3)
                for k in range(KD):
                    pe.matmul(ps[:, 4 + g % 4, :], w2_s[:, k, m * P:(m + 1) * P], agg_t[:, k, c * 512:(c + 1) * 512],
                              start=(k == 0), stop=False)
                pe.wait_ge(row_out, c + 1)
                pe.matmul(ps[:, 4 + g % 4, :], b2_row[0:1, m * P:(m + 1) * P], indeg_row[0:1, c * 512:(c + 1) * 512],
                          start=False, stop=True).then_inc(mt_mm, 1)
            pe.wait_ge(s_whh, 16)
            pe.wait_ge(s_wih, 32)
            pe.wait_ge(mt_out, 2 * KD)
            for i in range(NB):
                if i >= 2:
                    pe.wait_ge(gate_free, i - 1)
                q = 4 * (i % 2)
                s = slice(i * P, (i + 1) * P)
                for k in range(KD):
                    pe.matmul(ps[:, q + 3, :], xt[:, k, s], whh_s[:, k, 2 * D:3 * D], start=(k == 0), stop=(k == KD - 1))
                for k in range(KD):
                    for c in range(2):
                        pe.matmul(ps[:, q + c, :], xt[:, k, s], whh_s[:, k, c * D:(c + 1) * D],
                                  start=(k == 0), stop=False)
                for k in range(KD):
                    wih = wih_a if k < 2 else wih_b
                    for c in range(3):
                        mm = pe.matmul(ps[:, q + c, :], m_t[:, k, s], wih[:, k % 2, c * D:(c + 1) * D],
                                       start=(k == 0 and c == 2), stop=(k == KD - 1))
                mm.then_inc(gate_mm, 1)
            end_phase(pe, 4)

            for i in range(NB):
                if i >= 2:
                    pe.wait_ge(t_out, 2 * NB + i - 1)
                turn_block(2 * NB + i, xn, i % 2)
            for i in range(NB):
                if i >= 2:
                    pe.wait_ge(cn_out, i - 1)
                for b in range(NB):
                    mm = pe.transpose(ps[:, 2 + 2 * (i % 2) + b // 4, (b % 4) * P:(b % 4 + 1) * P],
                                      ct[:, b, i * P:(i + 1) * P], ident[:])
                mm.then_inc(cn_mm, 1)
            pe.wait_ge(t_out, 3 * NB)
            pe.wait_ge(s_wq, 16)
            for g in range(4 * KD + NB):
                if g >= 2:
                    pe.wait_ge(qkv_out, g - 1)
                if g == 2 * KD:
                    pe.wait_ge(s_wkv, 32)
                for k in range(KD):
                    if g < 4 * KD:
                        w = wq_s if g < 2 * KD else wk_s
                        n = g % (2 * KD)
                        mm = pe.matmul(ps[:, 6 + g % 2, :], w[:, k, (n % KD) * P:(n % KD + 1) * P],
                                       x2t[:, k, (n // KD) * 512:(n // KD + 1) * 512], start=(k == 0), stop=(k == KD - 1))
                    else:
                        i = g - 4 * KD
                        mm = pe.matmul(ps[:, 6 + g % 2, :], x2t[:, k, i * P:(i + 1) * P], wv_s[:, k, :],
                                       start=(k == 0), stop=(k == KD - 1))
                mm.then_inc(qkv_mm, 1)
            end_phase(pe, 5)

            def scores(u):
                h, i = u // NB, u % NB
                if u >= 2:
                    pe.wait_ge(s_low, u - 1)
                o = DH * (h % 2)
                for c in range(2):
                    mm = pe.matmul(ps[:, 2 * (u % 2) + c, :], q_t[o:o + DH, h // 2, i * P:(i + 1) * P],
                                   k_t[o:o + DH, h // 2, c * 512:(c + 1) * 512], start=True, stop=True)
                mm.then_inc(s_mm, 1)

            def turn_probs(u):
                pe.wait_ge(s_prob, u + 1)
                if u >= 1:
                    pe.wait_ge(s_tout, u)
                for b in range(NB):
                    mm = pe.transpose(ps[:, 4 + b // 4, (b % 4) * P:(b % 4 + 1) * P],
                                      prob[:, u % 2, b * P:(b + 1) * P], ident[:])
                mm.then_inc(s_tr, 1)

            def weigh(u):
                h, i = u // NB, u % NB
                pe.wait_ge(s_tout, u + 1)
                if i == 0 and h >= 2:
                    pe.wait_ge(s_att, h - 1)
                for b in range(NB):
                    mm = pe.matmul(ps[:, 6 + h % 2, i * DH:(i + 1) * DH], prob_t[:, u % 2, b * P:(b + 1) * P],
                                   v_s[:, b, h * DH:(h + 1) * DH], start=(b == 0), stop=(b == NB - 1))
                mm.then_inc(s_pv, 1)
            U = H * NB
            for u in range(U + 3):
                if u < U:
                    scores(u)
                if 2 <= u < U + 2:
                    turn_probs(u - 2)
                if u >= 3:
                    weigh(u - 3)
            end_phase(pe, 6)

            pe.wait_ge(s_wcn, 32)
            for i in range(NB + 1):
                if i < NB:
                    pe.wait_ge(x_set, 2 * NB + i + 1)
                    if i >= 2:
                        pe.wait_ge(t_out, 3 * NB + i - 1)
                    turn_block(3 * NB + i, xn, i % 2)
                if i:
                    n = i - 1
                    pe.wait_ge(t_out, 3 * NB + n + 1)
                    if n >= 2:
                        pe.wait_ge(bet_out, n - 1)
                    for k in range(KD):
                        mm = pe.matmul(ps[:, 2 + n % 2, :], x3t[:, k, n * P:(n + 1) * P], wn_s[:, k, :],
                                       start=(k == 0), stop=(k == KD - 1))
                    mm.then_inc(bet_mm, 1)
            for i in range(NB):
                if i >= 2:
                    pe.wait_ge(l3_y, i - 1)
                for k in range(KD):
                    pe.matmul(ps[:, 4 + 2 * (i % 2), :], x3t[:, k, i * P:(i + 1) * P], wc_s[:, k, :],
                              start=(k == 0), stop=(k == KD - 1))
                for b in range(NB):
                    if i == 0:
                        pe.wait_ge(bet_out, b + 1)
                    mm = pe.matmul(ps[:, 5 + 2 * (i % 2), :], ct[:, b, i * P:(i + 1) * P], bet[:, b, :],
                                   start=(b == 0), stop=(b == NB - 1))
                mm.then_inc(l3_mm, 1)

        @block.vector
        def _(dve):
            done = [0]

            def link(ins):
                done[0] += 1
                ins.then_inc(dve_step, 1)
                dve.wait_ge(dve_step, done[0])

            def norm_stats(n):
                link(dve.bn_stats(stats[:, n, :], y_s[:, n % 2, :]))
                dve.bn_aggr(mv[:, n, :], stats[:, n, :]).then_inc(var_set, 1)

            def norm_apply(n):
                dve.wait_ge(std_set, n + 1)
                link(dve.reciprocal(rstd[:, n:n + 1], std[:, n:n + 1]))
                dve.tensor_scalar(xn[:, n % NB, :], y_s[:, n % 2, :], mv[:, n, 0:1], rstd[:, n:n + 1],
                                  ALU.subtract, ALU.mult).then_inc(x_set, 1)

            flat = lambda t: t[:, :, :].rearrange("p v j -> p (v j)")
            dve.memset(flat(dst_f)[:, TILES:NT], FAR)
            dve.memset(flat(src_f)[:, TILES:NT], 0.0)
            dve.wait_ge(s_edges, 32)
            link(dve.tensor_copy(flat(dst_f)[:, 0:TILES], edge_i[:, 0, :]))
            link(dve.tensor_copy(flat(src_f)[:, 0:TILES], edge_i[:, 1, :]))
            for b in range(1, NB):
                dve.tensor_scalar(flat(rel), flat(dst_f), float(b * P), 0.0, ALU.is_lt, ALU.add,
                                  accum_out=below[:, b - 1:b]).then_inc(below_set, 1)
                dve.wait_ge(below_set, b)
            dve.wait_ge(below_sum, 1)
            link(dve.tensor_copy(first_i[:, 0:NB - 1], ps[:, 6, 0:NB - 1]))
            link(dve.tensor_scalar(first_i[:, 0:NB - 1], first_i[:, 0:NB - 1], (SUPER * P).bit_length() - 1, None,
                                   ALU.logical_shift_right))
            link(dve.tensor_copy(first_f[:, 0:NB - 1], first_i[:, 0:NB - 1]))
            dve.wait_ge(const_set, 6)
            for b in range(1, NB):
                link(dve.tensor_scalar(first_f[:, b - 1:b], first_f[:, b - 1:b], float(SUPERS - 1), float(b),
                                       ALU.min, ALU.add))
            link(dve.tensor_scalar(blk[:], visit_f[:], first_f[:, 0:1], None, ALU.is_ge))
            for b in range(2, NB):
                link(dve.scalar_tensor_tensor(blk[:], visit_f[:], first_f[:, b - 1:b], blk[:], ALU.is_ge, ALU.add))
            link(dve.memset(dst_v[:], 0.0))
            link(dve.memset(src_v[:], 0.0))
            for b in range(NB):
                link(dve.tensor_scalar(is_k, blk[:], float(b), None, ALU.is_equal))
                mask = is_k[:, b:NV].unsqueeze(2).broadcast_to([P, NV - b, SUPER])
                for a_f, a_v in ((dst_f, dst_v), (src_f, src_v)):
                    link(dve.tensor_tensor(plan_t[:, b:NV, :], a_f[:, 0:NV - b, :], mask, ALU.mult))
                    link(dve.tensor_tensor(a_v[:, b:NV, :], a_v[:, b:NV, :], plan_t[:, b:NV, :], ALU.add))
            blk_b = blk[:].unsqueeze(2).broadcast_to([P, NV, SUPER])
            link(dve.scalar_tensor_tensor(rel[:], blk_b, -float(P), dst_v[:], ALU.mult, ALU.add))
            link(dve.tensor_scalar(flat(plan_t), flat(rel), 0.0, None, ALU.is_ge))
            dve.scalar_tensor_tensor(flat(plan_t), flat(rel), float(P), flat(plan_t), ALU.is_lt, ALU.mult,
                                     accum_out=hits[:]).then_inc(hits_set, 1)
            dve.wait_ge(hits_sum, 1)
            link(dve.tensor_scalar(covered[:], ps[:, 7, 0:1], float(E), None, ALU.is_equal))
            link(dve.tensor_scalar(open_f[:], covered[:], -1.0, 1.0, ALU.mult, ALU.add))
            link(dve.tensor_scalar(open_p[:], open_f[:], -float(P), None, ALU.mult))
            link(dve.tensor_scalar(rounds_f[:], open_f[:], float(NB - 1), 1.0, ALU.mult, ALU.add))
            link(dve.tensor_copy(rounds_i[:], rounds_f[:]))
            for a_f, a_v in ((dst_f, dst_v), (src_f, src_v)):
                link(dve.tensor_scalar(flat(a_v), flat(a_v), covered[:, 0:1], None, ALU.mult))
                link(dve.scalar_tensor_tensor(flat(a_v), flat(a_f), open_f[:, 0:1], flat(a_v), ALU.mult, ALU.add))
            link(dve.tensor_scalar(blk[:], blk[:], covered[:, 0:1], None, ALU.mult))
            link(dve.tensor_tensor(tile_f, visit_f[:], blk[:], ALU.subtract))
            link(dve.tensor_scalar(tile_f, tile_f, float(SUPERS - 1), None, ALU.min))
            link(dve.tensor_copy(tile_i[:], tile_f))
            link(dve.tensor_copy(src_i[:], src_v[:]))

            def start_tables():
                link(dve.scalar_tensor_tensor(rel[:], blk_b, -float(P), dst_v[:], ALU.mult, ALU.add))
                link(dve.tensor_copy(blk_r[:], blk[:]))
                link(dve.tensor_copy(blk_i[:], blk_r[:]))

            def next_tables(tables_set, steps):
                dve.tensor_scalar(rel[:], rel[:], open_p[:, 0:1], None, ALU.add).then_inc(tables_set, 1)
                dve.tensor_scalar(blk_r[:], blk_r[:], open_f[:, 0:1], None, ALU.add).then_inc(tables_set, 1)
                dve.wait_ge(tables_set, steps + 2)
                dve.tensor_copy(blk_i[:], blk_r[:]).then_inc(tables_set, 1)
                dve.wait_ge(tables_set, steps + 3)
                dve.sem_inc(rounds_done, 1)

            start_tables()
            dve.memset(ct, 0.0).then_inc(count_added, 2)
            dve.sem_inc(plan_set, 1)

            def count_round(r):
                def one_hots(turn, n):
                    v = turn * RING + n
                    dve.wait_ge(count_mm, r * NV + v + 1)
                    for j in range(SUPER):
                        dve.tensor_scalar(oh_dst[:, n % 2, j, :], node_h[:, 0:P], rel[:, bass.ds(v, 1), j], None,
                                          ALU.is_equal)
                        ins = dve.tensor_scalar(oh_src[:, n % 2, j, :], node_h[:], src_v[:, bass.ds(v, 1), j], None,
                                                ALU.is_equal)
                    ins.then_inc(onehot_set, 1)

                def body(turn, last):
                    for n in range(RING):
                        if n + 1 < RING or not last:
                            one_hots(turn, n + 1)
                        v = turn * RING + n
                        b = dve.value_load(blk_i[0:1, bass.ds(v, 1)], min_val=0, max_val=NB - 1)
                        dve.wait_ge(count_mm, r * NV + v + 3)
                        dve.wait_ge(count_added, r * NV + v + 2)
                        place = arena[:, bass.ds(b * N, N)]
                        dve.tensor_tensor(place, place, ps[:, 2 * (n % 2):2 * (n % 2) + 2, :].rearrange("p a n -> p (a n)"),
                                          ALU.add).then_inc(count_added, 1)
                one_hots(0, 0)
                with dve.Fori(0, TURNS - 1) as turn:
                    body(turn, False)
                body(TURNS - 1, True)
                next_tables(tables_set, r * 3)
            rounds(dve, count_round)
            end_phase(dve, 1)

            for b in range(NB):
                dve.tensor_scalar(adj[:, b, :], ct[:, b, :], 1.0, None, ALU.min).then_inc(dve_step, 1)
                done[0] += 1
                dve.wait_ge(dve_step, done[0])
                diag = adj[:, b, b * P:(b + 1) * P]
                dve.tensor_tensor(diag, diag, ident[:], ALU.add).then_inc(adj_set, 1)
            dve.wait_ge(dinv_std, 1)
            dve.reciprocal(dinv[:], dinv[:]).then_inc(dinv_set, 1)
            dve.wait_ge(dinv_set, 1)
            dve.wait_ge(xb_set, NB + 1)

            def messages(n):
                dve.wait_ge(p_mm, n + 1)
                if n >= 4:
                    dve.wait_ge(s_pw[n % 4], 16)
                dve.tensor_tensor(p_s[:, n % 4, :], ps[:, 6 + n % 2, :], b1_s, ALU.add).then_inc(p_out, 1)

            for i in range(NB + 4):
                if i < NB:
                    dve.wait_ge(l0_mm, i + 1)
                    if i >= 2:
                        dve.wait_ge(x_set, i - 1)
                    dve.scalar_tensor_tensor(y_s[:, i % 2, :], ps[:, i % 4, :], dinv[:, i:i + 1], xn[:, i, :],
                                             ALU.mult, ALU.add).then_inc(y_set, 1)
                    dve.wait_ge(y_set, i + 1)
                    norm_stats(i)
                if 1 <= i <= NB:
                    norm_apply(i - 1)
                if i >= 4:
                    messages(i - 4)
            end_phase(dve, 2)

            start_tables()
            dve.sem_inc(pre_set, 8)
            dve.memset(agg, 0.0).then_inc(agg_added, 2)

            def edge_round(r):
                def tiles(turn, w):
                    v = turn * RING + w
                    for j in range(SUPER):
                        n = (SUPER * w + j) % (RING * SUPER)
                        t = r * NT + v * SUPER + j
                        dve.wait_ge(agg_mm, t + 1)
                        dve.tensor_scalar(oh_edge[:, n % 4, :], node_f[:], rel[:, bass.ds(v, 1), j], None,
                                          ALU.is_equal).then_inc(edge_hot, 1)
                        dve.wait_ge(attr_mm, t + 9)
                        if j == 0:
                            dve.wait_ge(s_gath[w % RING], (r * TURNS + turn + w // RING) * 32 + 32)
                        dve.tensor_tensor(msg[:, n % 4, :], ps[:, n % 4, :], gath[:, w % RING, j, :], ALU.add)\
                           .then_inc(pre_set, 1)

                def body(turn, last):
                    for n in range(RING):
                        if n + 1 < RING or not last:
                            tiles(turn, n + 1)
                        v = turn * RING + n
                        b = dve.value_load(blk_i[0:1, bass.ds(v, 1)], min_val=0, max_val=NB - 1)
                        dve.wait_ge(agg_mm, r * NT + v * SUPER + 6)
                        dve.wait_ge(agg_added, r * NV + v + 2)
                        place = arena[:, bass.ds(b * D + 92 * KB, D)]
                        dve.tensor_tensor(place, place, ps[:, 4 + n % 2, :], ALU.add).then_inc(agg_added, 1)
                tiles(0, 0)
                with dve.Fori(0, TURNS - 1) as turn:
                    body(turn, False)
                body(TURNS - 1, True)
                next_tables(edge_tables_set, r * 3)

            rounds(dve, edge_round)
            end_phase(dve, 3)

            dve.wait_ge(bn_std, 1)
            link(dve.reciprocal(var_s, var_s))
            link(dve.tensor_tensor(bn_a, bn_a, var_s, ALU.mult))
            link(dve.tensor_tensor(mean_s, mean_s, bn_a, ALU.mult))
            link(dve.tensor_tensor(bn_b, bn_b, mean_s, ALU.subtract))
            for i in range(NB + 1):
                if i < NB:
                    q = 4 * (i % 2)
                    rz, new, dif = rz_s[:, i % 2, :], n_s[:, i % 2, :], d_s[:, i % 2, :]
                    dve.wait_ge(gate_mm, i + 1)
                    dve.tensor_tensor(rz, ps[:, q:q + 2, :].rearrange("p a n -> p (a n)"), brz_s, ALU.add)\
                       .then_inc(rz_pre, 1)
                    link(dve.tensor_tensor(new, ps[:, q + 3, :], bhn_s, ALU.add))
                    link(dve.tensor_tensor(dif, ps[:, q + 2, :], bin_s, ALU.add))
                    dve.sem_inc(gate_free, 1)
                    dve.wait_ge(rz_set, i + 1)
                    link(dve.tensor_tensor(new, new, rz[:, 0:D], ALU.mult))
                    dve.tensor_tensor(new, new, dif, ALU.add).then_inc(n_pre, 1)
                    dve.wait_ge(n_set, i + 1)
                    link(dve.tensor_tensor(dif, xn[:, i, :], new, ALU.subtract))
                    link(dve.tensor_tensor(dif, dif, rz[:, D:2 * D], ALU.mult))
                    link(dve.tensor_tensor(dif, dif, new, ALU.add))
                    link(dve.tensor_tensor(dif, dif, bn_a, ALU.mult))
                    link(dve.tensor_tensor(dif, dif, bn_b, ALU.add))
                    link(dve.scalar_tensor_tensor(y_s[:, i % 2, :], xn[:, i, :], 2.0, dif, ALU.mult, ALU.add))
                    norm_stats(NB + i)
                if i:
                    norm_apply(NB + i - 1)
            end_phase(dve, 4)

            dve.wait_ge(cn_out, NB)
            dve.wait_ge(qkv_mm, 4 * KD + NB)
            for i in range(NB):
                dve.tensor_scalar(no_edge[:, i, :], cnt_n[:, i, :], 0.0, BIG, ALU.is_equal, ALU.mult).then_inc(mask_out, 1)
            end_phase(dve, 5)

            def lowest(u):
                dve.wait_ge(s_mm, u + 1)
                if u >= 2:
                    dve.wait_ge(s_prob, u - 1)
                dve.tensor_tensor_reduce(out=logit[:, u % 2, :],
                                         in0=ps[:, 2 * (u % 2):2 * (u % 2) + 2, :].rearrange("p a n -> p (a n)"),
                                         in1=no_edge[:, u % NB, :], scale=1.0, scalar=3.0e38, op0=ALU.add,
                                         op1=ALU.min, accum_out=low[:, u:u + 1]).then_inc(s_low, 1)

            def probs(u):
                dve.wait_ge(s_exp, u + 1)
                if u >= 2:
                    dve.wait_ge(s_tr, u - 1)
                dve.scalar_tensor_tensor(prob[:, u % 2, :], logit[:, u % 2, :], 1.0, cnt_n[:, u % NB, :], ALU.mult,
                                         ALU.mult, accum_out=den[:, u:u + 1]).then_inc(s_prob, 1)

            def head_out(h):
                dve.wait_ge(s_pv, NB * (h + 1))
                c = slice(h * NB, (h + 1) * NB)
                link(dve.tensor_scalar(rden[:, c], den[:, c], TINY, None, ALU.max))
                link(dve.reciprocal(rden[:, c], rden[:, c]))
                dve.tensor_tensor(att[:, :, h * DH:(h + 1) * DH], ps[:, 6 + h % 2, :].rearrange("p (i f) -> p i f", i=NB),
                                  rden[:, c].unsqueeze(2).broadcast_to([P, NB, DH]), ALU.mult).then_inc(s_att, 1)
            U = H * NB
            for u in range(U + 1):
                if u < U:
                    lowest(u)
                if u >= 1:
                    probs(u - 1)
                if u >= NB + 4 and (u - 4) % NB == 0:
                    head_out((u - 4) // NB - 1)
            head_out(H - 1)
            dve.wait_ge(s_att, H)
            end_phase(dve, 6)

            for i in range(NB + 1):
                if i < NB:
                    n = 2 * NB + i
                    if i >= 2:
                        dve.wait_ge(x_set, n - 1)
                    link(dve.tensor_tensor(y_s[:, i % 2, :], xn[:, i, :], att[:, i, :], ALU.add))
                    norm_stats(n)
                if i:
                    norm_apply(2 * NB + i - 1)
            link(dve.reciprocal(r_out[:], outdeg[:]))
            for i in range(NB + 1):
                if i < NB:
                    n = 3 * NB + i
                    dve.wait_ge(l3_mm, i + 1)
                    if i >= 2:
                        dve.wait_ge(x_set, n - 1)
                    y = y_s[:, i % 2, :]
                    dve.wait_ge(x_set, 2 * NB + i + 1)
                    link(dve.scalar_tensor_tensor(y, ps[:, 5 + 2 * (i % 2), :], r_out[:, i:i + 1], xn[:, i, :],
                                                  ALU.mult, ALU.add))
                    link(dve.tensor_tensor(y, y, b3_s[:], ALU.add))
                    dve.tensor_tensor(y, y, ps[:, 4 + 2 * (i % 2), :], ALU.add).then_inc(l3_y, 1)
                    dve.wait_ge(l3_y, i + 1)
                    norm_stats(n)
                if i:
                    norm_apply(3 * NB + i - 1)


def build(nc, aps, out):
    gnn_kernel(nc, *aps, out)


def kernel(**inputs):
    import numpy as _np
    import concourse.bacc as _bacc
    from concourse import mybir as _mybir
    from concourse.bass_utils import run_bass_kernel_spmd as _run

    def a(name):
        return _np.asarray(inputs[name])

    def c(v):
        return _np.ascontiguousarray(v)

    x, w1 = a("x"), a("L1_gnn_W1")
    hd = x.shape[1]
    tiles = a("src").shape[0] // 128
    laid = {
        "x": c(x),
        "x_t": c(x.T),
        "src_t": c(a("src").reshape(tiles, 128).T),
        "dst_t": c(a("dst").reshape(tiles, 128).T),
        "attr_t": c(a("edge_attr_128").T),
        "w0": c(a("L0_gnn_weight")),
        "b0": c(a("L0_gnn_bias")),
        "w1h_t": c(w1[:, :hd].T),
        "w1e_t": c(w1[:, hd:].T),
        "b1": c(a("L1_gnn_b1")),
        "w2_t": c(a("L1_gnn_W2").T),
        "b2": c(a("L1_gnn_b2")),
        "wih_t": c(a("L1_gnn_W_ih").T),
        "whh_t": c(a("L1_gnn_W_hh").T),
        "bih": c(a("L1_gnn_b_ih")),
        "bhh": c(a("L1_gnn_b_hh")),
        "gamma": c(a("L1_gnn_gamma")),
        "beta": c(a("L1_gnn_beta")),
        "run_mean": c(a("L1_gnn_run_mean")),
        "run_var": c(a("L1_gnn_run_var")),
        "wqkv": c(a("L2_gnn_W")),
        "wc": c(a("L3_gnn_wc")),
        "wn": c(a("L3_gnn_wn")),
        "b3": c(a("L3_gnn_bias")),
    }
    nc = _bacc.Bacc("TRN2", target_bir_lowering=False, num_devices=1)
    arrays, aps = {}, []
    for name, value in laid.items():
        arrays[f"in_{name}_dram"] = value
        aps.append(nc.dram_tensor(f"in_{name}_dram", value.shape, _mybir.dt.from_np(value.dtype),
                                  kind="ExternalInput").ap())
    out = nc.dram_tensor("out_0_dram", x.shape, _mybir.dt.float32, kind="ExternalOutput").ap()
    build(nc, aps, out)
    r = _run(nc, [arrays], core_ids=[0])
    return r.results[0]["out_0_dram"]
```

```python
from contextlib import ExitStack

import concourse.bass as bass
from concourse import mybir

ALU = mybir.AluOpType
ACT = mybir.ActivationFunctionType
F32 = mybir.dt.float32
F32R = mybir.dt.float32r
F16 = mybir.dt.float16
BF16 = mybir.dt.bfloat16
I32 = mybir.dt.int32
U16 = mybir.dt.uint16
AX_X = mybir.AxisListType.X

P = 128
KB = 256
EPS = 1e-5
FAR = 1.0e6
BIG = 1.0e30
TINY = 1.0e-30


def gnn_kernel(nc, x, x_t, src_t, dst_t, attr_t, w0, b0, w1h_t, w1e_t, b1, w2_t, b2, wih_t, whh_t,
               bih, bhh, gamma, beta, run_mean, run_var, wqkv, wc, wn, b3, out):
    N, D = x.shape
    EA, E = attr_t.shape
    NB = N // P
    KD = D // P
    SUPER = 2
    TILES = E // P
    SUPERS = TILES // SUPER
    RING = 4
    NV = -(-(SUPERS + NB - 1) // RING) * RING
    TURNS = NV // RING
    NT = NV * SUPER
    CLEARED = 4 ** RING
    H = 8
    DH = D // H
    assert EA == P and TILES * P == E and TILES % SUPER == 0 and SUPER == 2 and N == 2 * 512 and D == 512

    p_dram = nc.dram_tensor("messages_dram", [N, D], F32, kind="Internal").ap()

    qk_dram = nc.dram_tensor("queries_keys_dram", [4, D, N], F32, kind="Internal").ap()

    with ExitStack() as ctx:
        def sb(name, shape, dt):
            return ctx.enter_context(nc.sbuf_tensor(name, shape, dt))

        def sem(name):
            return ctx.enter_context(nc.semaphore(name))

        base = -(-nc.sbuf_base // 64) * 64
        arena = sb("arena", [P, 190 * KB], F32)

        def fast(name, kb, shape):
            return nc.alloc_sbuf_tensor_at(name, shape, F32R, offset=base + int(kb * 1024))

        def at(kb, size_kb):
            return arena[:, int(kb * KB):int((kb + size_kb) * KB)]

        def rows(kb, n, width):
            return at(kb, n * width / KB).rearrange("p (a b) -> p a b", a=n)

        ct = rows(0, NB, N)
        xn = rows(32, NB, D)
        b0_s, b1_s = at(48, 2), at(50, 2)
        brz_s, bhh_rz = at(52, 4), at(56, 4)
        bin_s, bhn_s = at(60, 2), at(62, 2)
        bn_a, bn_b = at(64, 2), at(66, 2)
        mean_s, var_s = at(68, 2), at(70, 2)
        y_s = rows(72, 2, D)
        xt = rows(76, KD, N)
        sup = rows(92, NB, D)
        w0_s = rows(108, KD, D)
        adj_r = fast("adj_r", 116, [P, NB, N])
        sup_hi = fast("sup_hi", 164, [P, NB, D])
        sup_lo = fast("sup_lo", 92, [P, NB, D])
        oh_src = at(164, 16).bitcast(BF16).rearrange("p (v j n) -> p v j n", v=RING, j=SUPER)
        oh_dst = at(180, 2).bitcast(BF16).rearrange("p (k t n) -> p k t n", k=2, t=4)
        iota_i = at(186, 4).bitcast(I32)
        edge_i = at(126, 3)[:, 0:2 * TILES].bitcast(I32).rearrange("p (a t) -> p a t", a=2)
        dst_f, src_f, plan_t = (at(kb, 2)[:, 0:NT].rearrange("p (v j) -> p v j", j=SUPER) for kb in (129, 131, 133))
        tile_f, is_k = at(135, 1)[:, 0:NV], at(136, 1)[:, 0:NV]
        w1h_s = rows(148, KD, D)
        p_s = rows(156, 4, D)
        w1e_s = at(186, 2)
        w2_s = rows(166, KD, D)
        agg = rows(92, NB, D)
        attr_s = rows(108, RING, SUPER * P)
        gath = at(112, 16).rearrange("p (v j n) -> p v j n", v=RING, j=SUPER)
        msg = rows(128, 4, D)
        msg_hi = fast("msg_hi", 136, [P, 4, D])
        msg_lo = fast("msg_lo", 144, [P, 4, D])
        oh_edge = fast("oh_edge", 152, [P, 2, 4, P])
        whh_s = rows(138, KD, 3 * D)
        wih_a = rows(174, 2, 3 * D)
        wih_b = rows(108, 2, 3 * D)
        agg_t = rows(120, KD, N)
        m_t = rows(92, KD, N)
        indeg_row = at(162, 4)[0:1, :]
        rz_s = rows(120, 2, 2 * D)
        n_s = rows(128, 2, D)
        d_s = rows(132, 2, D)
        x2t = rows(76, KD, N)
        stage = [fast(f"stage_{n}", kb, [P, 2, 2, 512]) for n, kb in enumerate((64, 116))]
        q_h = [fast(f"q_h{n}", 92 + 12 * n, [P, N]) for n in range(2)]
        k_h = [fast(f"k_h{n}", 96 + 12 * n, [P, 2, N]) for n in range(2)]
        v_s = rows(124, NB, D)
        wk_s, wv_s, wc_s = rows(140, KD, D), rows(148, KD, D), rows(156, KD, D)
        wq_s, wn_s = rows(164, KD, D), rows(172, KD, D)
        cnt_n = at(48, 16).bitcast(U16).rearrange("p (i n) -> p i n", i=NB)
        no_edge = at(140, 16).bitcast(BF16).rearrange("p (i n) -> p i n", i=NB)
        logit = rows(64, 2, N)
        prob = rows(164, 2, N)
        prob_t = rows(180, 2, N)
        att = rows(76, NB, D)
        x3t = rows(92, KD, N)
        bet = rows(108, NB, D)

        ident = sb("ident", [P, P], F32)
        ones = sb("ones", [P, P], F32)
        node_h = sb("node_h", [P, N], F16)
        node_f = sb("node_f", [P, P], F32)
        visit_f = sb("visit_f", [P, NV], F32)
        dst_v = sb("dst_v", [P, NV, SUPER], F32)
        src_v = sb("src_v", [P, NV, SUPER], F32)
        src_i = sb("src_i", [P, NV, SUPER], I32)
        rel = sb("rel", [P, NV, SUPER], F32)
        blk = sb("blk", [P, NV], F32)
        end_f = sb("end_f", [P, NB], F32)
        end_i = sb("end_i", [P, NB], I32)
        turn_f = sb("turn_f", [P, TURNS], F32)
        turn_i = sb("turn_i", [P, TURNS], I32)
        last_i = sb("last_i", [P, NV], I32)
        ends_s = sb("ends_s", [P, 2, 2, 4], F32)
        zero_s = sb("zero_s", [P, 1], F32)
        ones_r = sb("ones_r", [P, 2], F32R)
        blk_i = sb("blk_i", [P, NV], I32)
        tile_i = sb("tile_i", [P, NV], I32)
        below = sb("below", [P, NB], F32)
        first_i = sb("first_i", [P, NB], I32)
        first_f = sb("first_f", [P, NB], F32)
        hits = sb("hits", [P, 1], F32)
        covered = sb("covered", [P, 1], F32)
        open_f = sb("open_f", [P, 1], F32)
        open_p = sb("open_p", [P, 1], F32)
        rounds_f = sb("rounds_f", [P, 1], F32)
        rounds_i = sb("rounds_i", [P, 1], I32)
        idx = sb("idx", [P, RING, SUPER], I32)
        eps_s = sb("eps_s", [P, 1], F32)
        dinv = sb("dinv", [P, NB], F32)
        indeg = sb("indeg", [P, NB], F32)
        outdeg = sb("outdeg", [P, NB], F32)
        r_out = sb("r_out", [P, NB], F32)
        stats = sb("stats", [P, 4 * NB, 6], F32)
        mv = sb("mv", [P, 4 * NB, 2], F32)
        std = sb("std", [P, 4 * NB], F32)
        rstd = sb("rstd", [P, 4 * NB], F32)
        b2_row = sb("b2_row", [1, D], F32)
        b3_s = sb("b3_s", [P, D], F32)
        low = sb("low", [P, H * NB], F32)
        den = sb("den", [P, H * NB], F32)
        rden = sb("rden", [P, H * NB], F32)

        ps = ctx.enter_context(nc.psum_tensor("ps", [P, 8, 512], F32))

        ps_flat = ps[:, :, :].rearrange("p a n -> p (a n)")

        phase = sem("phase")
        s_edges, s_x, s_xt, s_w0, s_bias, s_w1h, s_w1e, s_w2 = (sem(f"loaded_{n}") for n in
            ("edges", "x", "xt", "w0", "bias", "w1h", "w1e", "w2"))
        s_whh, s_wih, s_wq, s_wkv, s_wcn = (sem(f"loaded_{n}") for n in ("whh", "wih", "wq", "wkv", "wcn"))
        s_attr = [sem(f"attr_loaded_{u}") for u in range(RING)]
        s_gath = [sem(f"gathered_{u}") for u in range(RING)]
        s_pw = [sem(f"messages_stored_{u}") for u in range(4)]
        s_out = [sem(f"out_stored_{u}") for u in range(2)]
        const_set = sem("const_set")
        dve_step = sem("dve_step")
        act_step = sem("act_step")
        pool_step = sem("pool_step")
        idx_set = sem("idx_set")
        xb_set = sem("xb_set")
        below_set, below_sum, hits_set, hits_sum = (sem(n) for n in ("below_set", "below_sum", "hits_set", "hits_sum"))
        plan_set = sem("plan_set")
        rounds_done = sem("rounds_done")
        ends_set = sem("ends_set")
        gather_step, hot_step, dst_hot = sem("gather_step"), sem("hot_step"), sem("dst_hot")
        act_round = sem("act_round")
        sup_mm, sup_out = sem("sup_mm"), sem("sup_out")
        seed_mm, onehot_set, count_mm, count_free, ct_set, tables_set, edge_tables_set = (sem(n) for n in
            ("seed_mm", "onehot_set", "count_mm", "count_free", "ct_set", "tables_set", "edge_tables_set"))
        adj_set, deg_mm, dinv_std, dinv_set, sup_scaled = (sem(n) for n in ("adj_set", "deg_mm", "dinv_std", "dinv_set", "sup_scaled"))
        sup_split = sem("sup_split")
        l0_mm, y_set, var_set, std_set, x_set = (sem(n) for n in ("l0_mm", "y_set", "var_set", "std_set", "x_set"))
        t_mm, t_out, p_mm, p_out = (sem(n) for n in ("t_mm", "t_out", "p_mm", "p_out"))
        attr_mm, pre_set, hi_set, lo_set, edge_hot, agg_mm, agg_free, agg_out = (sem(n) for n in
            ("attr_mm", "pre_set", "hi_set", "lo_set", "edge_hot", "agg_mm", "agg_free", "agg_out"))
        row_mm, row_out, mt_mm, mt_out, gate_mm, rz_pre, rz_set, n_pre, n_set, gate_free, bn_std = (sem(n) for n in
            ("row_mm", "row_out", "mt_mm", "mt_out", "gate_mm", "rz_pre", "rz_set", "n_pre", "n_set", "gate_free", "bn_std"))
        qkv_mm, qkv_out, cn_mm, cn_out, mask_out = (sem(n) for n in ("qkv_mm", "qkv_out", "cn_mm", "cn_out", "mask_out"))
        qk_hi, qk_lo = sem("qk_hi"), sem("qk_lo")
        s_qk = [sem(f"queries_keys_stored_{n}") for n in range(4)]
        s_head = [sem(f"head_loaded_{n}") for n in range(2)]
        s_mm, s_low, s_exp, s_prob, s_tr, s_tout, s_pv, s_att = (sem(n) for n in
            ("score_mm", "low_set", "exp_set", "prob_set", "prob_tr", "prob_t_set", "pv_mm", "att_set"))
        bet_mm, bet_out, l3_mm, l3_y, x3b_set = (sem(n) for n in ("bet_mm", "bet_out", "l3_mm", "l3_y", "x3b_set"))

        def end_phase(eng, n):
            eng.drain().then_inc(phase, 1)
            eng.wait_ge(phase, 4 * n)

        def rounds(eng, body):
            eng.wait_ge(plan_set, 1)
            n = eng.value_load(rounds_i[0:1, 0:1], min_val=1, max_val=NB)
            with eng.Fori(0, NB) as r:
                with eng.If(r < n):
                    body(r)

        block = ctx.enter_context(nc.Block())

        @block.sync
        def _(sp):
            sp.dma_start(edge_i[:, 0, :], dst_t).then_inc(s_edges, 16)
            sp.dma_start(edge_i[:, 1, :], src_t).then_inc(s_edges, 16)
            sp.dma_start(w0_s, w0.rearrange("(k p) n -> p k n", p=P)).then_inc(s_w0, 16)
            sp.dma_start(xt, x_t.rearrange("(k p) n -> p k n", p=P)).then_inc(s_xt, 16)
            sp.dma_start(xn, x.rearrange("(b p) n -> p b n", p=P)).then_inc(s_x, 16)
            for dest, vec in ((b0_s, b0), (b1_s, b1), (brz_s, bih[0:2 * D]), (bhh_rz, bhh[0:2 * D]),
                              (bin_s, bih[2 * D:3 * D]), (bhn_s, bhh[2 * D:3 * D]), (bn_a, gamma),
                              (bn_b, beta), (mean_s, run_mean), (var_s, run_var), (b3_s[:], b3)):
                sp.dma_start(dest, vec.partition_broadcast(P)).then_inc(s_bias, 16)
            sp.dma_start(b2_row[:], b2.rearrange("(a n) -> a n", a=1)).then_inc(s_bias, 16)
            sp.dma_start(w1h_s, w1h_t.rearrange("(k p) n -> p k n", p=P)).then_inc(s_w1h, 16)
            sp.wait_ge(const_set, 7)
            sp.dma_start(w1e_s, w1e_t).then_inc(s_w1e, 16)
            for i in range(NB):
                sp.wait_ge(p_out, i + 1)
                sp.dma_start(p_dram[i * P:(i + 1) * P, :], p_s[:, i % 4, :]).then_inc(s_pw[i % 4], 16)
            sp.wait_ge(phase, 8)

            def edge_round(r):
                with sp.Fori(0, TURNS) as turn:
                    for u in range(RING):
                        v = turn * RING + u
                        first = sp.value_load(tile_i[0:1, bass.ds(v, 1)], min_val=0, max_val=SUPERS - 1)
                        sp.wait_ge(attr_mm, r * NT + v * SUPER + 2)
                        sp.dma_start(attr_s[:, u, :], attr_t[:, bass.ds(first * (SUPER * P), SUPER * P)])\
                          .then_inc(s_attr[u], 16)
            rounds(sp, edge_round)
            sp.dma_start(w2_s, w2_t.rearrange("(k p) n -> p k n", p=P)).then_inc(s_w2, 16)
            sp.dma_start(wih_a, wih_t[0:2 * P, :].rearrange("(k p) n -> p k n", p=P)).then_inc(s_wih, 16)
            sp.wait_ge(phase, 12)
            sp.dma_start(whh_s, whh_t.rearrange("(k p) n -> p k n", p=P)).then_inc(s_whh, 16)
            sp.dma_start(wih_b, wih_t[2 * P:4 * P, :].rearrange("(k p) n -> p k n", p=P)).then_inc(s_wih, 16)
            sp.wait_ge(mt_mm, 2 * KD)
            sp.dma_start(wq_s, wqkv[:, 0:D].rearrange("(k p) n -> p k n", p=P)).then_inc(s_wq, 16)
            sp.wait_ge(gate_mm, NB)
            sp.dma_start(wk_s, wqkv[:, D:2 * D].rearrange("(k p) n -> p k n", p=P)).then_inc(s_wkv, 16)
            sp.dma_start(wv_s, wqkv[:, 2 * D:3 * D].rearrange("(k p) n -> p k n", p=P)).then_inc(s_wkv, 16)
            sp.dma_start(wc_s, wc.rearrange("(k p) n -> p k n", p=P)).then_inc(s_wcn, 16)
            sp.dma_start(wn_s, wn.rearrange("(k p) n -> p k n", p=P)).then_inc(s_wcn, 16)
            for g in range(4 * KD):
                n = g % (2 * KD)
                sp.wait_ge(qk_lo, g + 1)
                a = 2 * (g // (2 * KD))
                sp.dma_start(qk_dram[a:a + 2, (n % KD) * P:(n % KD + 1) * P, (n // KD) * 512:(n // KD + 1) * 512]
                             .rearrange("a p n -> p a n"), stage[g % 4 // 2][:, g % 2].bitcast(F32)).then_inc(s_qk[g % 4], 16)
            for n in range(4):
                sp.wait_ge(s_qk[n], 16 * KD)
            for h in range(H):
                if h >= 2:
                    sp.wait_ge(s_mm, NB * (h - 1))
                f = slice(h * DH, (h + 1) * DH)
                for a in range(2):
                    half = slice(a * DH, (a + 1) * DH)
                    sp.dma_start(q_h[h % 2][half, :].bitcast(F32), qk_dram[a, f, :]).then_inc(s_head[h % 2], 16)
                    sp.dma_start(k_h[h % 2][half, :, :].bitcast(F32), qk_dram[2:4, f, :].rearrange("a p n -> p a n"))\
                      .then_inc(s_head[h % 2], 16)
            for i in range(NB):
                sp.wait_ge(x_set, 3 * NB + i + 1)
                sp.dma_start(out[i * P:(i + 1) * P, :], xn[:, i, :]).then_inc(s_out[i % 2], 16)
            for u in range(2):
                sp.wait_ge(s_out[u], 16 * (NB // 2))

        @block.gpsimd
        def _(pool):
            pool.memset(ident[:], 0.0).then_inc(pool_step, 1)
            pool.iota(iota_i, pattern=[[1, N]], base=0, channel_multiplier=0).then_inc(pool_step, 1)
            pool.memset(ones[:], 1.0).then_inc(const_set, 1)
            pool.memset(eps_s[:], EPS).then_inc(const_set, 1)
            pool.memset(zero_s[:], 0.0).then_inc(const_set, 1)
            pool.wait_ge(pool_step, 2)
            pool.affine_select(out=ident[:], in_=ident[:], compare_op=ALU.not_equal, fill=1.0, base=0,
                               pattern=[[-1, P]], channel_multiplier=1).then_inc(const_set, 1)
            pool.tensor_copy(node_f[:], iota_i[:, 0:P]).then_inc(const_set, 1)
            pool.tensor_copy(visit_f[:], iota_i[:, 0:NV]).then_inc(const_set, 1)
            pool.tensor_copy(node_h[:], iota_i).then_inc(const_set, 1)
            pool.wait_ge(s_x, 16)
            pool.wait_ge(s_bias, 12 * 16)
            for i in range(NB):
                pool.tensor_tensor(xn[:, i, :], xn[:, i, :], b0_s, ALU.add).then_inc(xb_set, 1)
            pool.tensor_tensor(brz_s, brz_s, bhh_rz, ALU.add).then_inc(xb_set, 1)

            def hot_round(r):
                pool.wait_ge(tables_set, r + 1)
                pool.sem_inc(hot_step, 1)

                with pool.Fori(0, TURNS) as turn:
                    for k in range(2):
                        v = turn * RING + 2 * k
                        pool.wait_ge(count_mm, r * NV + v + 2)
                        pool.sem_inc(hot_step, 1)
                        pool.tensor_copy(ends_s[:, k, 0, :], rel[:, bass.ds(v, 2), :].rearrange("p v j -> p (v j)"))
                        pool.tensor_copy(ends_s[:, k, 1, :], src_v[:, bass.ds(v, 2), :].rearrange("p v j -> p (v j)"))\
                            .then_inc(ends_set, 1)
                        pool.wait_ge(ends_set, (r * TURNS + turn) * 2 + k + 1)
                        pool.sem_inc(hot_step, 1)
                        for n in range(SUPER):
                            ins = pool.tensor_scalar(oh_dst[:, k, n, :], node_h[:, 0:P], ends_s[:, k, 0, n:n + 1], None,
                                                     ALU.is_equal)
                        ins.then_inc(dst_hot, 2)
            rounds(pool, hot_round)
            end_phase(pool, 1)
            end_phase(pool, 2)
            for u in range(4):
                pool.wait_ge(s_pw[u], 32)

            def gather_round(r):
                with pool.Fori(0, TURNS) as turn:
                    for u in range(RING):
                        v = turn * RING + u
                        pool.wait_ge(pre_set, r * NT + v * SUPER + 2)
                        pool.sem_inc(gather_step, 1)
                        pool.tensor_copy(idx[:, u, :], src_i[:, bass.ds(v, 1), :].rearrange("p a j -> p (a j)"))\
                            .then_inc(idx_set, 1)
                        pool.wait_ge(idx_set, r * NV + v + 1)
                        pool.sem_inc(gather_step, 1)
                        for j in range(SUPER):
                            pool.indirect_dma_start(
                                out=gath[:, u, j, :], out_offset=None, in_=p_dram,
                                in_offset=bass.IndirectOffsetOnAxis(ap=idx[:, u, j:j + 1], axis=0),
                            ).then_inc(s_gath[u], 16)
            rounds(pool, gather_round)
            end_phase(pool, 3)
            end_phase(pool, 4)
            end_phase(pool, 5)
            end_phase(pool, 6)

        @block.scalar
        def _(act):
            def layer_std(n):
                act.wait_ge(var_set, n + 1)
                act.activation(std[:, n:n + 1], mv[:, n, 1:2], ACT.Sqrt, bias=eps_s[:, 0:1]).then_inc(std_set, 1)

            def turned(n, dest, bank):
                act.wait_ge(t_mm, n + 1)
                i = n % NB
                act.activation(dest[:, :, i * P:(i + 1) * P],
                               ps[:, bank, :].rearrange("p (k n) -> p k n", k=KD), ACT.Copy).then_inc(t_out, 1)

            for i in range(NB):
                act.wait_ge(sup_mm, i + 1)
                act.activation(sup[:, i, :], ps[:, i % 4, :], ACT.Copy).then_inc(sup_out, 1)
            def place(b):
                return ps[:, 2 * (b % 4):2 * (b % 4) + 2, :].rearrange("p a n -> p (a n)")

            act.wait_ge(seed_mm, 1)
            for b in range(4):
                act.activation(place(b), zero_s[:, 0:1].broadcast_to([P, N]), ACT.Copy).then_inc(count_free, 1)
            act.wait_ge(plan_set, 1)
            for b in range(NB):
                end = act.value_load(end_i[0:1, b:b + 1], min_val=0, max_val=NB * NV)
                act.wait_ge(count_mm, end + RING)
                act.activation(ct[:, b, :], place(b), ACT.Copy, accum_out=indeg[:, b:b + 1]).then_inc(ct_set, 1)
                act.activation(adj_r[:, b, :], place(b), ACT.Sign).then_inc(adj_set, 1)
                if b < 4:
                    act.wait_ge(ct_set, b + 1)
                    act.wait_ge(adj_set, b + 1)
                    act.activation(place(b), zero_s[:, 0:1].broadcast_to([P, N]), ACT.Copy).then_inc(count_free, 1)
            end_phase(act, 1)
            act.wait_ge(deg_mm, 1)
            act.activation(dinv[:], ps[:, 7, 0:2 * NB].rearrange("p (i c) -> p i c", c=2)[:, :, 0], ACT.Sqrt)\
               .then_inc(dinv_std, 1)
            act.wait_ge(dinv_set, 1)
            for b in range(NB):
                act.activation(sup_hi[:, b, :], sup[:, b, :], ACT.Copy, scale=dinv[:, b:b + 1]).then_inc(sup_scaled, 1)
            for i in range(NB + 2):
                if i < NB:
                    layer_std(i)
                if i >= 2:
                    turned(i - 2, xt, 4 + i % 2)
            end_phase(act, 2)

            act.wait_ge(seed_mm, 2)
            for b in range(4):
                act.activation(ps[:, 4 + b, :], zero_s[:, 0:1].broadcast_to([P, D]), ACT.Copy).then_inc(agg_free, 1)

            def relu_round(r):
                def flush(v, b):
                    act.wait_ge(agg_mm, r * NT + v * SUPER + SUPER + 8)
                    act.sem_inc(act_round, 1)
                    bank = ps[:, bass.ds(b % 4 + 4, 1), :].rearrange("p a n -> p (a n)")
                    act.activation(arena[:, bass.ds(b * D + 92 * KB, D)], bank, ACT.Copy).then_inc(agg_out, 1)
                    act.wait_ge(agg_out, b + 1)
                    act.sem_inc(act_round, 1)
                    act.activation(bank, zero_s[:, 0:1].broadcast_to([P, D]), ACT.Copy).then_inc(agg_free, 1)

                with act.Fori(0, TURNS) as turn:
                    for u in range(RING):
                        v = turn * RING + u
                        for j in range(SUPER):
                            t = r * NT + v * SUPER + j
                            n = SUPER * u + j
                            act.wait_ge(pre_set, t + 9)
                            act.wait_ge(agg_mm, t + 5)
                            act.activation(msg_hi[:, n % 4, :], msg[:, n % 4, :], ACT.Relu).then_inc(hi_set, 1)
                        ended = act.value_load(last_i[0:1, bass.ds(v, 1)], min_val=0, max_val=NB)
                        with act.If(ended > 0):
                            flush(v - 2, ended - 1)
                final = act.value_load(blk_i[0:1, NV - 1:NV], min_val=0, max_val=NB - 1)
                flush(NV - 1, final + r)
            rounds(act, relu_round)
            end_phase(act, 3)
            for b in range(NB):
                turned(NB + b, agg_t, b % 2)
            act.activation(var_s, var_s, ACT.Sqrt, bias=eps_s[:, 0:1]).then_inc(bn_std, 1)
            for c in range(2):
                act.wait_ge(row_mm, c + 1)
                act.activation(indeg_row[0:1, c * 512:(c + 1) * 512], ps[0:1, 2 + c, :], ACT.Copy).then_inc(row_out, 1)
            for g in range(2 * KD):
                act.wait_ge(mt_mm, g + 1)
                act.activation(m_t[:, g % KD, (g // KD) * 512:(g // KD + 1) * 512], ps[:, 4 + g % 4, :], ACT.Copy)\
                   .then_inc(mt_out, 1)
            for i in range(NB + 1):
                if i < NB:
                    act.wait_ge(rz_pre, i + 1)
                    act.activation(rz_s[:, i % 2, :], rz_s[:, i % 2, :], ACT.Sigmoid).then_inc(rz_set, 1)
                    act.wait_ge(n_pre, i + 1)
                    act.activation(n_s[:, i % 2, :], n_s[:, i % 2, :], ACT.Tanh).then_inc(n_set, 1)
                if i:
                    layer_std(NB + i - 1)
            end_phase(act, 4)
            for i in range(NB):
                turned(2 * NB + i, x2t, i % 2)
            for i in range(NB):
                act.wait_ge(cn_mm, i + 1)
                act.activation(cnt_n[:, i, :], ps[:, 2 + 2 * (i % 2):4 + 2 * (i % 2), :].rearrange("p a n -> p (a n)"),
                               ACT.Copy, accum_out=outdeg[:, i:i + 1]).then_inc(cn_out, 1)
            for g in range(4 * KD + NB):
                act.wait_ge(qkv_mm, g + 1)
                bank = ps[:, 6 + g % 2, :]
                if g < 4 * KD:
                    if g >= 4:
                        act.wait_ge(s_qk[g % 4], 16 * (g // 4))
                    act.activation(stage[g % 4 // 2][:, g % 2, 0, :], bank, ACT.Copy,
                                   scale=-float(DH) ** -0.5 if g < 2 * KD else 1.0).then_inc(qk_hi, 1)
                else:
                    act.activation(v_s[:, g - 4 * KD, :], bank, ACT.Copy).then_inc(qkv_out, 1)
            end_phase(act, 5)

            def exps(u):
                act.wait_ge(s_low, u + 1)
                act.activation(logit[:, u % 2, :], logit[:, u % 2, :], ACT.Exp, bias=low[:, u:u + 1], scale=-1.0)\
                   .then_inc(s_exp, 1)

            def prob_out(u):
                for c in range(2):
                    act.wait_ge(s_tr, 2 * u + c + 1)
                    if u >= 2:
                        act.wait_ge(s_pv, u - 1)
                    act.activation(prob_t[:, u % 2, c * 512:(c + 1) * 512], ps[:, 4 + c, :], ACT.Copy)\
                       .then_inc(s_tout, 1)
            U = H * NB
            for u in range(U + 2):
                if u < U:
                    exps(u)
                if u >= 2:
                    prob_out(u - 2)
            end_phase(act, 6)
            for i in range(NB + 2):
                if i < NB:
                    layer_std(2 * NB + i)
                if 1 <= i <= NB:
                    turned(3 * NB + i - 1, x3t, (i - 1) % 2)
                if i >= 2:
                    act.wait_ge(bet_mm, i - 1)
                    act.activation(bet[:, i - 2, :], ps[:, 2 + i % 2, :], ACT.Copy).then_inc(bet_out, 1)
            for i in range(NB):
                layer_std(3 * NB + i)

        @block.tensor
        def _(pe):
            def turn_block(n, source, bank, free=None):
                for k in range(KD):
                    mm = pe.transpose(ps[:, bank, k * P:(k + 1) * P], source[:, n % NB, k * P:(k + 1) * P], ident[:])
                mm.then_inc(t_mm, 1)

            pe.wait_ge(const_set, 7)
            pe.wait_ge(below_set, NB - 1)
            pe.matmul(ps[:, 6, 0:NB - 1], ones[:], below[:, 0:NB - 1], start=True, stop=True).then_inc(below_sum, 1)
            pe.wait_ge(s_w0, 16)
            pe.wait_ge(s_xt, 16)
            for i in range(NB):
                if i >= 4:
                    pe.wait_ge(sup_out, i - 3)
                for k in range(KD):
                    mm = pe.matmul(ps[:, i % 4, :], xt[:, k, i * P:(i + 1) * P], w0_s[:, k, :],
                                   start=(k == 0), stop=(k == KD - 1))
                mm.then_inc(sup_mm, 1)
            pe.wait_ge(hits_set, 1)
            pe.matmul(ps[:, 7, 0:1], ones[:], hits[:], start=True, stop=True).then_inc(hits_sum, 1)
            pe.sem_inc(count_mm, RING)
            pe.wait_ge(sup_out, NB)
            pe.wait_ge(hits_sum, 2)
            for bank in range(8):
                mm = pe.matmul(ps[:, bank, :], ident[:], w0_s[:, 0, :], start=True, stop=True)
            mm.then_inc(seed_mm, 1)

            def count_round(r):
                ahead = pe.snap(r * CLEARED + r % 4 * sum(4 ** u for u in range(RING)))
                with pe.Fori(0, TURNS) as turn:
                    turn_plan = pe.snap(pe.value_load(turn_i[0:1, bass.ds(turn, 1)], min_val=CLEARED,
                                                      max_val=CLEARED * NB + CLEARED - 1) + ahead)
                    g = pe.snap((r * TURNS + turn) * RING)
                    pe.wait_ge(count_free, turn_plan // CLEARED)
                    for u in range(RING):
                        place = pe.snap(turn_plan // (4 ** u) % 4 * N)
                        pe.wait_ge(onehot_set, g + (u + 1))
                        if u % 2 == 0:
                            pe.wait_ge(dst_hot, g + (u + 2))
                        for j in range(SUPER):
                            for c in range(2):
                                mm = pe.matmul(ps_flat[:, bass.ds(place + c * 512, 512)],
                                               oh_dst[:, u // 2, u % 2 * SUPER + j, :],
                                               oh_src[:, u, j, c * 512:(c + 1) * 512],
                                               start=False, stop=False, skip_group_check=True)
                        mm.then_inc(count_mm, 1)
            rounds(pe, count_round)
            end_phase(pe, 1)

            pe.wait_ge(adj_set, 2 * NB)
            for i in range(NB):
                for b in range(NB):
                    mm = pe.matmul(ps[:, 7, 2 * i:2 * i + 2], adj_r[:, b, i * P:(i + 1) * P], ones_r[:],
                                   start=(b == 0), stop=(b == NB - 1))
            mm.then_inc(deg_mm, 1)
            pe.wait_ge(s_w1h, 16)
            for i in range(NB + 4):
                if i < NB:
                    if i >= 4:
                        pe.wait_ge(y_set, i - 3)
                    for b in range(NB):
                        if i == 0:
                            pe.wait_ge(sup_split, b + 1)
                        for part in (sup_hi, sup_lo):
                            mm = pe.matmul(ps[:, i % 4, :], adj_r[:, b, i * P:(i + 1) * P], part[:, b, :],
                                           start=(b == 0 and part is sup_hi), stop=(b == NB - 1 and part is sup_lo))
                    mm.then_inc(l0_mm, 1)
                if 2 <= i < NB + 2:
                    n = i - 2
                    pe.wait_ge(x_set, n + 1)
                    if n >= 2:
                        pe.wait_ge(t_out, n - 1)
                    turn_block(n, xn, 4 + n % 2)
                if i >= 4:
                    n = i - 4
                    pe.wait_ge(t_out, n + 1)
                    if n >= 2:
                        pe.wait_ge(p_out, n - 1)
                    for k in range(KD):
                        mm = pe.matmul(ps[:, 6 + n % 2, :], xt[:, k, n * P:(n + 1) * P], w1h_s[:, k, :],
                                       start=(k == 0), stop=(k == KD - 1))
                    mm.then_inc(p_mm, 1)
            end_phase(pe, 2)

            pe.sem_inc(attr_mm, 8)
            pe.sem_inc(agg_mm, 8)
            pe.wait_ge(s_w1e, 16)
            for bank in range(4, 8):
                mm = pe.matmul(ps[:, bank, :], ident[:], xt[:, 0, 0:512], start=True, stop=True)
            mm.then_inc(seed_mm, 1)

            def edge_round(r):
                def attr_products(turn, n):
                    t = r * NT + turn * (RING * SUPER) + n
                    slot = n // SUPER % RING
                    if n % SUPER == 0:
                        pe.wait_ge(s_attr[slot], (r * TURNS + turn + n // (RING * SUPER)) * 16 + 16)
                    pe.wait_ge(pre_set, t + 5)
                    pe.matmul(ps[:, n % 4, :], attr_s[:, slot, (n % SUPER) * P:(n % SUPER + 1) * P], w1e_s,
                              start=True, stop=True).then_inc(attr_mm, 1)

                def body(turn, last):
                    for n in range(RING * SUPER):
                        if n + 3 < RING * SUPER or not last:
                            attr_products(turn, n + 3)
                        t = r * NT + turn * (RING * SUPER) + n
                        if n % SUPER == 0:
                            v = turn * RING + n // SUPER
                            b = pe.snap(pe.value_load(blk_i[0:1, bass.ds(v, 1)], min_val=0, max_val=NB - 1) + r)
                            pe.wait_ge(agg_free, b + 1)
                        if n % 4 == 0:
                            pe.wait_ge(edge_hot, (r * TURNS + turn) * 2 + n // 4 + 1)
                        pe.wait_ge(lo_set, t + 1)
                        for part in (msg_hi, msg_lo):
                            mm = pe.matmul(ps[:, bass.ds(b % 4 + 4, 1), :].rearrange("p a n -> p (a n)"),
                                           oh_edge[:, n // 4, n % 4, :], part[:, n % 4, :], start=False, stop=False,
                                           skip_group_check=True)
                        mm.then_inc(agg_mm, 1)
                for n in range(3):
                    attr_products(0, n)
                with pe.Fori(0, TURNS - 1) as turn:
                    body(turn, False)
                body(TURNS - 1, True)
            rounds(pe, edge_round)
            end_phase(pe, 3)

            for b in range(NB):
                if b >= 2:
                    pe.wait_ge(t_out, NB + b - 1)
                turn_block(NB + b, agg, b % 2)
            for b in range(NB):
                mm = pe.transpose(ps[0:1, 2 + b // 4, (b % 4) * P:(b % 4 + 1) * P], indeg[:, b:b + 1], ident[:])
                if b % 4 == 3:
                    mm.then_inc(row_mm, 1)
            pe.wait_ge(s_w2, 16)
            pe.wait_ge(s_bias, 12 * 16)
            pe.wait_ge(t_out, 2 * NB)
            for g in range(2 * KD):
                c, m = g // KD, g % KD
                if g >= 4:
                    pe.wait_ge(mt_out, g - 3)
                for k in range(KD):
                    pe.matmul(ps[:, 4 + g % 4, :], w2_s[:, k, m * P:(m + 1) * P], agg_t[:, k, c * 512:(c + 1) * 512],
                              start=(k == 0), stop=False)
                pe.wait_ge(row_out, c + 1)
                pe.matmul(ps[:, 4 + g % 4, :], b2_row[0:1, m * P:(m + 1) * P], indeg_row[0:1, c * 512:(c + 1) * 512],
                          start=False, stop=True).then_inc(mt_mm, 1)
            pe.wait_ge(s_whh, 16)
            pe.wait_ge(s_wih, 32)
            pe.wait_ge(mt_out, 2 * KD)
            for i in range(NB):
                if i >= 2:
                    pe.wait_ge(gate_free, i - 1)
                q = 4 * (i % 2)
                s = slice(i * P, (i + 1) * P)
                for k in range(KD):
                    pe.matmul(ps[:, q + 3, :], xt[:, k, s], whh_s[:, k, 2 * D:3 * D], start=(k == 0), stop=(k == KD - 1))
                for k in range(KD):
                    for c in range(2):
                        pe.matmul(ps[:, q + c, :], xt[:, k, s], whh_s[:, k, c * D:(c + 1) * D],
                                  start=(k == 0), stop=False)
                for k in range(KD):
                    wih = wih_a if k < 2 else wih_b
                    for c in range(3):
                        mm = pe.matmul(ps[:, q + c, :], m_t[:, k, s], wih[:, k % 2, c * D:(c + 1) * D],
                                       start=(k == 0 and c == 2), stop=(k == KD - 1))
                mm.then_inc(gate_mm, 1)
            end_phase(pe, 4)

            for i in range(NB):
                if i >= 2:
                    pe.wait_ge(t_out, 2 * NB + i - 1)
                turn_block(2 * NB + i, xn, i % 2)
            for i in range(NB):
                if i >= 2:
                    pe.wait_ge(cn_out, i - 1)
                for b in range(NB):
                    mm = pe.transpose(ps[:, 2 + 2 * (i % 2) + b // 4, (b % 4) * P:(b % 4 + 1) * P],
                                      ct[:, b, i * P:(i + 1) * P], ident[:])
                mm.then_inc(cn_mm, 1)
            pe.wait_ge(t_out, 3 * NB)
            pe.wait_ge(s_wq, 16)
            for g in range(4 * KD + NB):
                if 2 <= g < 4 * KD + 2:
                    pe.wait_ge(qk_lo, g - 1)
                if g >= 4 * KD + 2:
                    pe.wait_ge(qkv_out, g - 4 * KD - 1)
                if g == 2 * KD:
                    pe.wait_ge(s_wkv, 32)
                for k in range(KD):
                    if g < 4 * KD:
                        w = wq_s if g < 2 * KD else wk_s
                        n = g % (2 * KD)
                        mm = pe.matmul(ps[:, 6 + g % 2, :], w[:, k, (n % KD) * P:(n % KD + 1) * P],
                                       x2t[:, k, (n // KD) * 512:(n // KD + 1) * 512], start=(k == 0), stop=(k == KD - 1))
                    else:
                        i = g - 4 * KD
                        mm = pe.matmul(ps[:, 6 + g % 2, :], x2t[:, k, i * P:(i + 1) * P], wv_s[:, k, :],
                                       start=(k == 0), stop=(k == KD - 1))
                mm.then_inc(qkv_mm, 1)
            end_phase(pe, 5)

            def scores(u):
                h, i = u // NB, u % NB
                if u >= 2:
                    pe.wait_ge(s_low, u - 1)
                if i == 0:
                    pe.wait_ge(s_head[h % 2], 64 * (h // 2 + 1))
                for c in range(2):
                    for a in range(2):
                        mm = pe.matmul(ps[:, 2 * (u % 2) + c, :], q_h[h % 2][:, i * P:(i + 1) * P],
                                       k_h[h % 2][:, a, c * 512:(c + 1) * 512], start=(a == 0), stop=(a == 1))
                mm.then_inc(s_mm, 1)

            def turn_probs(u):
                pe.wait_ge(s_prob, u + 1)
                for b in range(NB):
                    if b % 4 == 0 and u >= 1:
                        pe.wait_ge(s_tout, 2 * u - 1 + b // 4)
                    mm = pe.transpose(ps[:, 4 + b // 4, (b % 4) * P:(b % 4 + 1) * P],
                                      prob[:, u % 2, b * P:(b + 1) * P], ident[:])
                    if b % 4 == 3:
                        mm.then_inc(s_tr, 1)

            def weigh(u):
                h, i = u // NB, u % NB
                if i == 0 and h >= 2:
                    pe.wait_ge(s_att, h - 1)
                for b in range(NB):
                    if b % 4 == 0:
                        pe.wait_ge(s_tout, 2 * u + 1 + b // 4)
                    mm = pe.matmul(ps[:, 6 + h % 2, i * DH:(i + 1) * DH], prob_t[:, u % 2, b * P:(b + 1) * P],
                                   v_s[:, b, h * DH:(h + 1) * DH], start=(b == 0), stop=(b == NB - 1))
                mm.then_inc(s_pv, 1)
            U = H * NB
            for u in range(U + 3):
                if u < U:
                    scores(u)
                if 2 <= u < U + 2:
                    turn_probs(u - 2)
                if u >= 3:
                    weigh(u - 3)
            end_phase(pe, 6)

            pe.wait_ge(s_wcn, 32)
            for i in range(NB + 1):
                if i < NB:
                    pe.wait_ge(x_set, 2 * NB + i + 1)
                    if i >= 2:
                        pe.wait_ge(t_out, 3 * NB + i - 1)
                    turn_block(3 * NB + i, xn, i % 2)
                if i:
                    n = i - 1
                    pe.wait_ge(t_out, 3 * NB + n + 1)
                    if n >= 2:
                        pe.wait_ge(bet_out, n - 1)
                    for k in range(KD):
                        mm = pe.matmul(ps[:, 2 + n % 2, :], x3t[:, k, n * P:(n + 1) * P], wn_s[:, k, :],
                                       start=(k == 0), stop=(k == KD - 1))
                    mm.then_inc(bet_mm, 1)
            for i in range(NB):
                if i >= 2:
                    pe.wait_ge(l3_y, i - 1)
                for k in range(KD):
                    pe.matmul(ps[:, 4 + 2 * (i % 2), :], x3t[:, k, i * P:(i + 1) * P], wc_s[:, k, :],
                              start=(k == 0), stop=(k == KD - 1))
                for b in range(NB):
                    if i == 0:
                        pe.wait_ge(bet_out, b + 1)
                    mm = pe.matmul(ps[:, 5 + 2 * (i % 2), :], ct[:, b, i * P:(i + 1) * P], bet[:, b, :],
                                   start=(b == 0), stop=(b == NB - 1))
                mm.then_inc(l3_mm, 1)

        @block.vector
        def _(dve):
            done = [0]

            def link(ins):
                done[0] += 1
                ins.then_inc(dve_step, 1)
                dve.wait_ge(dve_step, done[0])

            def norm_stats(n):
                link(dve.bn_stats(stats[:, n, :], y_s[:, n % 2, :]))
                dve.bn_aggr(mv[:, n, :], stats[:, n, :]).then_inc(var_set, 1)

            def norm_apply(n):
                dve.wait_ge(std_set, n + 1)
                link(dve.reciprocal(rstd[:, n:n + 1], std[:, n:n + 1]))
                dve.tensor_scalar(xn[:, n % NB, :], y_s[:, n % 2, :], mv[:, n, 0:1], rstd[:, n:n + 1],
                                  ALU.subtract, ALU.mult).then_inc(x_set, 1)

            flat = lambda t: t[:, :, :].rearrange("p v j -> p (v j)")
            dve.memset(flat(dst_f)[:, TILES:NT], FAR)
            dve.memset(flat(src_f)[:, TILES:NT], 0.0)
            dve.wait_ge(s_edges, 32)
            link(dve.tensor_copy(flat(dst_f)[:, 0:TILES], edge_i[:, 0, :]))
            link(dve.tensor_copy(flat(src_f)[:, 0:TILES], edge_i[:, 1, :]))
            for b in range(1, NB):
                dve.tensor_scalar(flat(rel), flat(dst_f), float(b * P), 0.0, ALU.is_lt, ALU.add,
                                  accum_out=below[:, b - 1:b]).then_inc(below_set, 1)
                dve.wait_ge(below_set, b)
            dve.wait_ge(below_sum, 1)
            link(dve.tensor_copy(first_i[:, 0:NB - 1], ps[:, 6, 0:NB - 1]))
            link(dve.tensor_scalar(first_i[:, 0:NB - 1], first_i[:, 0:NB - 1], (SUPER * P).bit_length() - 1, None,
                                   ALU.logical_shift_right))
            link(dve.tensor_copy(first_f[:, 0:NB - 1], first_i[:, 0:NB - 1]))
            dve.wait_ge(const_set, 7)
            for b in range(1, NB):
                link(dve.tensor_scalar(first_f[:, b - 1:b], first_f[:, b - 1:b], float(SUPERS - 1), float(b),
                                       ALU.min, ALU.add))
            link(dve.tensor_scalar(blk[:], visit_f[:], first_f[:, 0:1], None, ALU.is_ge))
            for b in range(2, NB):
                link(dve.scalar_tensor_tensor(blk[:], visit_f[:], first_f[:, b - 1:b], blk[:], ALU.is_ge, ALU.add))
            link(dve.memset(dst_v[:], 0.0))
            link(dve.memset(src_v[:], 0.0))
            for b in range(NB):
                link(dve.tensor_scalar(is_k, blk[:], float(b), None, ALU.is_equal))
                mask = is_k[:, b:NV].unsqueeze(2).broadcast_to([P, NV - b, SUPER])
                for a_f, a_v in ((dst_f, dst_v), (src_f, src_v)):
                    link(dve.tensor_tensor(plan_t[:, b:NV, :], a_f[:, 0:NV - b, :], mask, ALU.mult))
                    link(dve.tensor_tensor(a_v[:, b:NV, :], a_v[:, b:NV, :], plan_t[:, b:NV, :], ALU.add))
            blk_b = blk[:].unsqueeze(2).broadcast_to([P, NV, SUPER])
            link(dve.scalar_tensor_tensor(rel[:], blk_b, -float(P), dst_v[:], ALU.mult, ALU.add))
            link(dve.tensor_scalar(flat(plan_t), flat(rel), 0.0, None, ALU.is_ge))
            dve.scalar_tensor_tensor(flat(plan_t), flat(rel), float(P), flat(plan_t), ALU.is_lt, ALU.mult,
                                     accum_out=hits[:]).then_inc(hits_set, 1)
            dve.wait_ge(hits_sum, 1)
            link(dve.tensor_scalar(covered[:], ps[:, 7, 0:1], float(E), None, ALU.is_equal))
            link(dve.tensor_scalar(open_f[:], covered[:], -1.0, 1.0, ALU.mult, ALU.add))
            link(dve.tensor_scalar(open_p[:], open_f[:], -float(P), None, ALU.mult))
            link(dve.tensor_scalar(rounds_f[:], open_f[:], float(NB - 1), 1.0, ALU.mult, ALU.add))
            link(dve.tensor_copy(rounds_i[:], rounds_f[:]))
            for a_f, a_v in ((dst_f, dst_v), (src_f, src_v)):
                link(dve.tensor_scalar(flat(a_v), flat(a_v), covered[:, 0:1], None, ALU.mult))
                link(dve.scalar_tensor_tensor(flat(a_v), flat(a_f), open_f[:, 0:1], flat(a_v), ALU.mult, ALU.add))
            link(dve.tensor_scalar(end_f[:, 0:NB - 1], first_f[:, 0:NB - 1], covered[:, 0:1], None, ALU.mult))
            link(dve.tensor_scalar(end_f[:, NB - 1:NB], covered[:], float(NV), None, ALU.mult))
            for b in range(NB):
                link(dve.scalar_tensor_tensor(end_f[:, b:b + 1], open_f[:], float((b + 1) * NV), end_f[:, b:b + 1],
                                              ALU.mult, ALU.add))
            link(dve.tensor_copy(end_i[:], end_f[:]))
            link(dve.tensor_scalar(blk[:], blk[:], covered[:, 0:1], None, ALU.mult))
            link(dve.memset(is_k[:, 0:2], 0.0))
            link(dve.tensor_tensor(is_k[:, 2:NV], blk[:, 1:NV - 1], blk[:, 0:NV - 2], ALU.subtract))
            link(dve.tensor_scalar(tile_f, blk[:], 1.0, None, ALU.add))
            link(dve.tensor_tensor(is_k[:, 2:NV], is_k[:, 2:NV], tile_f[:, 0:NV - 2], ALU.mult))
            link(dve.tensor_copy(last_i[:], is_k))
            link(dve.tensor_copy(blk_i[:], blk[:]))
            by_turn = lambda t: t[:, 0:NV].rearrange("p (n u) -> p n u", u=RING)
            link(dve.tensor_scalar(tile_f, blk[:], 4.0, -4.0, ALU.is_ge, ALU.mult))
            link(dve.tensor_tensor(tile_f, tile_f, blk[:], ALU.add))
            link(dve.tensor_scalar(turn_f[:], by_turn(blk)[:, :, RING - 1], 1.0, float(CLEARED), ALU.add, ALU.mult))
            for u in range(RING):
                link(dve.scalar_tensor_tensor(turn_f[:], by_turn(tile_f)[:, :, u], float(4 ** u), turn_f[:],
                                              ALU.mult, ALU.add))
            link(dve.tensor_copy(turn_i[:], turn_f[:]))
            link(dve.tensor_copy(ones_r[:], ones[:, 0:2]))
            link(dve.tensor_tensor(tile_f, visit_f[:], blk[:], ALU.subtract))
            link(dve.tensor_scalar(tile_f, tile_f, float(SUPERS - 1), None, ALU.min))
            link(dve.tensor_copy(tile_i[:], tile_f))
            link(dve.tensor_copy(src_i[:], src_v[:]))

            def start_tables():
                link(dve.scalar_tensor_tensor(rel[:], blk_b, -float(P), dst_v[:], ALU.mult, ALU.add))

            def next_tables(tables_set, steps):
                dve.tensor_scalar(rel[:], rel[:], open_p[:, 0:1], None, ALU.add).then_inc(tables_set, 1)
                dve.wait_ge(tables_set, steps + 2)
                dve.sem_inc(rounds_done, 1)

            start_tables()
            dve.sem_inc(hits_sum, 1)
            dve.sem_inc(tables_set, 1)
            dve.sem_inc(plan_set, 1)

            def count_round(r):
                with dve.Fori(0, TURNS) as turn:
                    for n in range(RING):
                        if n % 2 == 0:
                            dve.wait_ge(ends_set, (r * TURNS + turn) * 2 + n // 2 + 1)
                        dve.wait_ge(count_mm, r * NV + turn * RING + n + 1)
                        for j in range(SUPER):
                            t = n % 2 * SUPER + j
                            if n % 2:
                                dve.tensor_scalar(oh_dst[:, n // 2, t, :], node_h[:, 0:P],
                                                  ends_s[:, n // 2, 0, t:t + 1], None, ALU.is_equal)
                            ins = dve.tensor_scalar(oh_src[:, n, j, :], node_h[:], ends_s[:, n // 2, 1, t:t + 1], None,
                                                    ALU.is_equal)
                        ins.then_inc(onehot_set, 1)
                dve.wait_ge(dst_hot, r * NV + NV)
                dve.wait_ge(onehot_set, r * NV + NV)
                next_tables(tables_set, r)
            rounds(dve, count_round)
            end_phase(dve, 1)

            for b in range(NB):
                diag = adj_r[:, b, b * P:(b + 1) * P]
                dve.tensor_tensor(diag, diag.bitcast(F32), ident[:], ALU.add).then_inc(adj_set, 1)
            dve.wait_ge(dinv_std, 1)
            dve.reciprocal(dinv[:], dinv[:]).then_inc(dinv_set, 1)
            dve.wait_ge(dinv_set, 1)
            for b in range(NB):
                dve.wait_ge(sup_scaled, b + 1)
                dve.scalar_tensor_tensor(sup_lo[:, b, :], sup[:, b, :], dinv[:, b:b + 1], sup_hi[:, b, :].bitcast(F32),
                                         ALU.mult, ALU.subtract).then_inc(sup_split, 1)
            dve.wait_ge(xb_set, NB + 1)

            def messages(n):
                dve.wait_ge(p_mm, n + 1)
                if n >= 4:
                    dve.wait_ge(s_pw[n % 4], 16)
                dve.tensor_tensor(p_s[:, n % 4, :], ps[:, 6 + n % 2, :], b1_s, ALU.add).then_inc(p_out, 1)

            for i in range(NB + 4):
                if i < NB:
                    dve.wait_ge(l0_mm, i + 1)
                    if i >= 2:
                        dve.wait_ge(x_set, i - 1)
                    dve.scalar_tensor_tensor(y_s[:, i % 2, :], ps[:, i % 4, :], dinv[:, i:i + 1], xn[:, i, :],
                                             ALU.mult, ALU.add).then_inc(y_set, 1)
                    dve.wait_ge(y_set, i + 1)
                    norm_stats(i)
                if 1 <= i <= NB:
                    norm_apply(i - 1)
                if i >= 4:
                    messages(i - 4)
            end_phase(dve, 2)

            start_tables()
            dve.sem_inc(edge_tables_set, 1)
            dve.sem_inc(pre_set, 8)

            def edge_round(r):
                def one_hots(turn, k):
                    t = r * NT + turn * (RING * SUPER) + 4 * k
                    dve.wait_ge(agg_mm, t + 4)
                    where = rel[:, bass.ds(turn * RING + k * (4 // SUPER), 4 // SUPER), :]
                    dve.tensor_tensor(oh_edge[:, k % 2, :, :], node_f[:].unsqueeze(1).broadcast_to([P, 4, P]),
                                      where.rearrange("p v j -> p (v j)").unsqueeze(2).broadcast_to([P, 4, P]),
                                      ALU.is_equal).then_inc(edge_hot, 1)

                def add(turn, n):
                    t = r * NT + turn * (RING * SUPER) + n
                    w = n // SUPER
                    dve.wait_ge(attr_mm, t + 9)
                    if n % SUPER == 0:
                        dve.wait_ge(s_gath[w % RING], (r * TURNS + turn + w // RING) * 32 + 32)
                    dve.tensor_tensor(msg[:, n % 4, :], ps[:, n % 4, :], gath[:, w % RING, n % SUPER, :], ALU.add)\
                       .then_inc(pre_set, 1)

                def low_part(turn, n):
                    t = r * NT + turn * (RING * SUPER) + n
                    dve.wait_ge(hi_set, t + 1)
                    dve.scalar_tensor_tensor(msg_lo[:, n % 4, :], msg[:, n % 4, :], 0.0, msg_hi[:, n % 4, :].bitcast(F32),
                                             ALU.max, ALU.subtract).then_inc(lo_set, 1)

                def body(turn, last):
                    for n in range(RING * SUPER):
                        if n % 4 == 0:
                            one_hots(turn, n // 4)
                        if n + 1 < RING * SUPER or not last:
                            add(turn, n + 1)
                        low_part(turn, n)
                add(0, 0)
                with dve.Fori(0, TURNS - 1) as turn:
                    body(turn, False)
                body(TURNS - 1, True)
                dve.wait_ge(edge_hot, r * (TURNS * 2) + TURNS * 2)
                next_tables(edge_tables_set, r)

            rounds(dve, edge_round)
            end_phase(dve, 3)

            dve.wait_ge(bn_std, 1)
            link(dve.reciprocal(var_s, var_s))
            link(dve.tensor_tensor(bn_a, bn_a, var_s, ALU.mult))
            link(dve.tensor_tensor(mean_s, mean_s, bn_a, ALU.mult))
            link(dve.tensor_tensor(bn_b, bn_b, mean_s, ALU.subtract))
            for i in range(NB + 1):
                if i < NB:
                    q = 4 * (i % 2)
                    rz, new, dif = rz_s[:, i % 2, :], n_s[:, i % 2, :], d_s[:, i % 2, :]
                    dve.wait_ge(gate_mm, i + 1)
                    dve.tensor_tensor(rz, ps[:, q:q + 2, :].rearrange("p a n -> p (a n)"), brz_s, ALU.add)\
                       .then_inc(rz_pre, 1)
                    link(dve.tensor_tensor(new, ps[:, q + 3, :], bhn_s, ALU.add))
                    link(dve.tensor_tensor(dif, ps[:, q + 2, :], bin_s, ALU.add))
                    dve.sem_inc(gate_free, 1)
                    dve.wait_ge(rz_set, i + 1)
                    link(dve.tensor_tensor(new, new, rz[:, 0:D], ALU.mult))
                    dve.tensor_tensor(new, new, dif, ALU.add).then_inc(n_pre, 1)
                    dve.wait_ge(n_set, i + 1)
                    link(dve.tensor_tensor(dif, xn[:, i, :], new, ALU.subtract))
                    link(dve.tensor_tensor(dif, dif, rz[:, D:2 * D], ALU.mult))
                    link(dve.tensor_tensor(dif, dif, new, ALU.add))
                    link(dve.tensor_tensor(dif, dif, bn_a, ALU.mult))
                    link(dve.tensor_tensor(dif, dif, bn_b, ALU.add))
                    link(dve.scalar_tensor_tensor(y_s[:, i % 2, :], xn[:, i, :], 2.0, dif, ALU.mult, ALU.add))
                    norm_stats(NB + i)
                if i:
                    norm_apply(NB + i - 1)
            end_phase(dve, 4)

            for g in range(4 * KD):
                dve.wait_ge(qk_hi, g + 1)
                part = stage[g % 4 // 2][:, g % 2]
                dve.scalar_tensor_tensor(part[:, 1, :], ps[:, 6 + g % 2, :], -float(DH) ** -0.5 if g < 2 * KD else 1.0,
                                         part[:, 0, :].bitcast(F32), ALU.mult, ALU.subtract).then_inc(qk_lo, 1)
            dve.wait_ge(cn_out, NB)
            dve.wait_ge(qkv_mm, 4 * KD + NB)
            for i in range(NB):
                dve.tensor_scalar(no_edge[:, i, :], cnt_n[:, i, :], 0.0, BIG, ALU.is_equal, ALU.mult).then_inc(mask_out, 1)
            end_phase(dve, 5)

            def lowest(u):
                dve.wait_ge(s_mm, u + 1)
                if u >= 2:
                    dve.wait_ge(s_prob, u - 1)
                dve.tensor_tensor_reduce(out=logit[:, u % 2, :],
                                         in0=ps[:, 2 * (u % 2):2 * (u % 2) + 2, :].rearrange("p a n -> p (a n)"),
                                         in1=no_edge[:, u % NB, :], scale=1.0, scalar=3.0e38, op0=ALU.add,
                                         op1=ALU.min, accum_out=low[:, u:u + 1]).then_inc(s_low, 1)

            def probs(u):
                dve.wait_ge(s_exp, u + 1)
                if u >= 2:
                    dve.wait_ge(s_tr, 2 * u - 2)
                dve.scalar_tensor_tensor(prob[:, u % 2, :], logit[:, u % 2, :], 1.0, cnt_n[:, u % NB, :], ALU.mult,
                                         ALU.mult, accum_out=den[:, u:u + 1]).then_inc(s_prob, 1)

            def head_out(h):
                dve.wait_ge(s_pv, NB * (h + 1))
                c = slice(h * NB, (h + 1) * NB)
                link(dve.tensor_scalar(rden[:, c], den[:, c], TINY, None, ALU.max))
                link(dve.reciprocal(rden[:, c], rden[:, c]))
                dve.tensor_tensor(att[:, :, h * DH:(h + 1) * DH], ps[:, 6 + h % 2, :].rearrange("p (i f) -> p i f", i=NB),
                                  rden[:, c].unsqueeze(2).broadcast_to([P, NB, DH]), ALU.mult).then_inc(s_att, 1)
            U = H * NB
            for u in range(U + 1):
                if u < U:
                    lowest(u)
                if u >= 1:
                    probs(u - 1)
                if u >= NB + 4 and (u - 4) % NB == 0:
                    head_out((u - 4) // NB - 1)
            head_out(H - 1)
            dve.wait_ge(s_att, H)
            end_phase(dve, 6)

            for i in range(NB + 1):
                if i < NB:
                    n = 2 * NB + i
                    if i >= 2:
                        dve.wait_ge(x_set, n - 1)
                    link(dve.tensor_tensor(y_s[:, i % 2, :], xn[:, i, :], att[:, i, :], ALU.add))
                    norm_stats(n)
                if i:
                    norm_apply(2 * NB + i - 1)
            link(dve.reciprocal(r_out[:], outdeg[:]))
            for i in range(NB + 1):
                if i < NB:
                    n = 3 * NB + i
                    dve.wait_ge(l3_mm, i + 1)
                    if i >= 2:
                        dve.wait_ge(x_set, n - 1)
                    y = y_s[:, i % 2, :]
                    dve.wait_ge(x_set, 2 * NB + i + 1)
                    link(dve.scalar_tensor_tensor(y, ps[:, 5 + 2 * (i % 2), :], r_out[:, i:i + 1], xn[:, i, :],
                                                  ALU.mult, ALU.add))
                    link(dve.tensor_tensor(y, y, b3_s[:], ALU.add))
                    dve.tensor_tensor(y, y, ps[:, 4 + 2 * (i % 2), :], ALU.add).then_inc(l3_y, 1)
                    dve.wait_ge(l3_y, i + 1)
                    norm_stats(n)
                if i:
                    norm_apply(3 * NB + i - 1)


def build(nc, aps, out):
    gnn_kernel(nc, *aps, out)


def kernel(**inputs):
    import numpy as _np
    import concourse.bacc as _bacc
    from concourse import mybir as _mybir
    from concourse.bass_utils import run_bass_kernel_spmd as _run

    def a(name):
        return _np.asarray(inputs[name])

    def c(v):
        return _np.ascontiguousarray(v)

    x, w1 = a("x"), a("L1_gnn_W1")
    hd = x.shape[1]
    tiles = a("src").shape[0] // 128
    laid = {
        "x": c(x),
        "x_t": c(x.T),
        "src_t": c(a("src").reshape(tiles, 128).T),
        "dst_t": c(a("dst").reshape(tiles, 128).T),
        "attr_t": c(a("edge_attr_128").T),
        "w0": c(a("L0_gnn_weight")),
        "b0": c(a("L0_gnn_bias")),
        "w1h_t": c(w1[:, :hd].T),
        "w1e_t": c(w1[:, hd:].T),
        "b1": c(a("L1_gnn_b1")),
        "w2_t": c(a("L1_gnn_W2").T),
        "b2": c(a("L1_gnn_b2")),
        "wih_t": c(a("L1_gnn_W_ih").T),
        "whh_t": c(a("L1_gnn_W_hh").T),
        "bih": c(a("L1_gnn_b_ih")),
        "bhh": c(a("L1_gnn_b_hh")),
        "gamma": c(a("L1_gnn_gamma")),
        "beta": c(a("L1_gnn_beta")),
        "run_mean": c(a("L1_gnn_run_mean")),
        "run_var": c(a("L1_gnn_run_var")),
        "wqkv": c(a("L2_gnn_W")),
        "wc": c(a("L3_gnn_wc")),
        "wn": c(a("L3_gnn_wn")),
        "b3": c(a("L3_gnn_bias")),
    }
    nc = _bacc.Bacc("TRN2", target_bir_lowering=False, num_devices=1)
    arrays, aps = {}, []
    for name, value in laid.items():
        arrays[f"in_{name}_dram"] = value
        aps.append(nc.dram_tensor(f"in_{name}_dram", value.shape, _mybir.dt.from_np(value.dtype),
                                  kind="ExternalInput").ap())
    out = nc.dram_tensor("out_0_dram", x.shape, _mybir.dt.float32, kind="ExternalOutput").ap()
    build(nc, aps, out)
    r = _run(nc, [arrays], core_ids=[0])
    return r.results[0]["out_0_dram"]
```

```python
from contextlib import ExitStack

import concourse.bass as bass
from concourse import mybir

ALU = mybir.AluOpType
ACT = mybir.ActivationFunctionType
F32 = mybir.dt.float32
F32R = mybir.dt.float32r
F16 = mybir.dt.float16
BF16 = mybir.dt.bfloat16
I32 = mybir.dt.int32
U16 = mybir.dt.uint16

P = 128
KB = 256
EPS = 1e-5
FAR = 30000.0
BIG = 1.0e30
TINY = 1.0e-30


def gnn_kernel(nc, x, x_t, src_t, dst_t, attr_t, w0, b0, w1h_t, w1e_t, b1, w2_t, b2, wih_t, whh_t,
               bih, bhh, gamma, beta, run_mean, run_var, wqkv, wc, wn, b3, out):
    N, D = x.shape
    EA, E = attr_t.shape
    NB = N // P
    KD = D // P
    SUPER = 2
    TILES = E // P
    SUPERS = TILES // SUPER
    RING = 4
    NV = -(-(SUPERS + NB - 1) // RING) * RING
    TURNS = NV // RING
    NT = NV * SUPER
    CLEARED = 4 ** RING
    H = 8
    DH = D // H
    assert EA == P and TILES * P == E and TILES % SUPER == 0 and SUPER == 2 and N == 2 * 512 and D == 512

    p_dram = nc.dram_tensor("messages_dram", [N, D], F32, kind="Internal").ap()

    qk_dram = nc.dram_tensor("queries_keys_dram", [4, D, N], F32, kind="Internal").ap()

    with ExitStack() as ctx:
        def sb(name, shape, dt):
            return ctx.enter_context(nc.sbuf_tensor(name, shape, dt))

        def sem(name):
            return ctx.enter_context(nc.semaphore(name))

        base = -(-nc.sbuf_base // 64) * 64
        arena = sb("arena", [P, 190 * KB], F32)

        def fast(name, kb, shape):
            return nc.alloc_sbuf_tensor_at(name, shape, F32R, offset=base + int(kb * 1024))

        def at(kb, size_kb):
            return arena[:, int(kb * KB):int((kb + size_kb) * KB)]

        def rows(kb, n, width):
            return at(kb, n * width / KB).rearrange("p (a b) -> p a b", a=n)

        ct = rows(0, NB, N)
        xn = rows(32, NB, D)
        b0_s, b1_s = at(48, 2), at(50, 2)
        brz_s, bhh_rz = at(52, 4), at(56, 4)
        bin_s, bhn_s = at(60, 2), at(62, 2)
        bn_a, bn_b = at(64, 2), at(66, 2)
        mean_s, var_s = at(68, 2), at(70, 2)
        y_s = rows(72, 2, D)
        xt = rows(76, KD, N)
        sup = rows(92, NB, D)
        w0_s = rows(108, KD, D)
        adj_r = fast("adj_r", 116, [P, NB, N])
        sup_hi = fast("sup_hi", 164, [P, NB, D])
        sup_lo = fast("sup_lo", 92, [P, NB, D])
        oh_src = at(164, 16).bitcast(BF16).rearrange("p (v j n) -> p v j n", v=RING, j=SUPER)
        oh_dst = at(180, 2).bitcast(BF16).rearrange("p (k t n) -> p k t n", k=2, t=4)
        iota_i = at(186, 4).bitcast(I32)
        edge_i = at(126, 3)[:, 0:2 * TILES].bitcast(I32).rearrange("p (a t) -> p a t", a=2)
        ends_f, ends_v, plan_h = (at(kb, 2).bitcast(F16).rearrange("p (a t) -> p a t", a=2)[:, :, 0:NT]
                                  .rearrange("p a (v j) -> p a v j", j=SUPER) for kb in (129, 131, 133))
        tile_f = at(135, 1)[:, 0:NV]
        mask_h, plan_t = at(137, 1).bitcast(F16)[:, 0:NV], at(138, 2)[:, 0:NT].rearrange("p (v j) -> p v j", j=SUPER)
        step_f = at(184, 1)[:, 0:NV]
        deg_row = at(180, 4)[0:1, :]
        w1h_s, w1h_lo = rows(148, KD, D), fast("w1h_lo", 148, [P, KD, D])
        w1h_hi = [fast(f"w1h_hi_{k}", 108 + 2 * k, [P, D]) for k in range(KD)]
        h_hi, h_lo = ([fast(f"h_{n}_{u}", kb, [P, KD, P]) for u, kb in enumerate(kbs)] for n, kbs in
            (("hi", (180, 182)), ("lo", (184, 188))))
        p_s = rows(156, 4, D)
        w1e_s = at(186, 2)
        w2_s, w2_lo = rows(166, KD, D), fast("w2_lo", 166, [P, KD, D])
        w2_hi = [fast(f"w2_hi_{k}", kb, [P, D]) for k, kb in enumerate((72, 74, 48, 50))]
        agg = rows(92, NB, D)
        attr_s = rows(108, RING, SUPER * P)
        gath = at(112, 16).rearrange("p (v j n) -> p v j n", v=RING, j=SUPER)
        msg = [at(kb, SUPER * D / KB) for kb in (128, 132, 174, 178)]
        msg_hi = fast("msg_hi", 136, [P, 2, SUPER * D])
        msg_lo = fast("msg_lo", 144, [P, 2, SUPER * D])
        oh_edge = fast("oh_edge", 152, [P, 2, 4, P])
        whh_s = rows(138, KD, 3 * D)
        parts = ((0, 2), (1, 2), (0, 0), (0, 1), (1, 0), (1, 1), (2, 0))
        EARLY = 4
        whh_hi = {kc: fast(f"whh_hi_{n}", kb, [P, D]) for n, (kc, kb) in enumerate(zip(parts, (56, 58, 68, 70, 48, 50, 136)))}
        whh_lo = {(k, c): fast(f"whh_lo_{k}_{c}", 138 + 6 * k + 2 * c, [P, D]) for k, c in parts}
        hx_hi, hx_lo = ([fast(f"hx_{n}_{u}", kb, [P, KD, P]) for u, kb in enumerate(kbs)] for n, kbs in
            (("hi", (162, 172)), ("lo", (186, 188))))
        wih_a = rows(174, 2, 3 * D)
        wih_b = rows(108, 2, 3 * D)
        agg_hi, agg_lo = fast("agg_hi", 120, [P, KD, N]), fast("agg_lo", 174, [P, KD, N])
        m_t = rows(92, KD, N)
        indeg_all = at(162, 4)
        rz_s = rows(120, 2, 2 * D)
        n_s = rows(128, 2, D)
        d_s = rows(132, 2, D)
        x2_hi = fast("x2_hi", 76, [P, KD, N])
        x2_lo = fast("x2_lo", 104, [P, KD, N])
        stage = [fast(f"stage_{n}", kb, [P, 2, 512]) for n, kb in enumerate((64, 68, 120, 156))]
        q_h = [fast(f"q_h{n}", 92 + 12 * n, [P, N]) for n in range(2)]
        k_h = [fast(f"k_h{n}", 96 + 12 * n, [P, 2, N]) for n in range(2)]
        v_s = rows(124, NB, D)
        wq_s, wk_s, wv_s, wc_s, wn_s = (rows(kb, KD, D) for kb in (164, 140, 174, 156, 172))
        wq_lo, wk_lo, wv_lo, wc_lo, wn_lo = (fast(f"{n}_lo", kb, [P, KD, D]) for n, kb in
            (("wq", 164), ("wk", 140), ("wv", 174), ("wc", 156), ("wn", 172)))
        wq_hi, wk_hi, wv_hi, wc_hi, wn_hi = ([fast(f"{n}_hi_{k}", kb, [P, D]) for k, kb in enumerate(kbs)] for n, kbs in
            (("wq", (136, 162, 172, 186)), ("wk", (148, 150, 152, 154)), ("wv", (182, 184, 188, 160)),
             ("wc", (164, 166, 168, 170)), ("wn", (116, 118, 120, 122))))
        cnt_n = at(48, 16).bitcast(U16).rearrange("p (i n) -> p i n", i=NB)
        no_edge = at(140, 16).bitcast(BF16).rearrange("p (i n) -> p i n", i=NB)
        logit = rows(64, 2, N)
        prob = rows(164, 2, N)
        prob_t = rows(180, 2, N)
        att = rows(76, NB, D)
        x3_hi, x3_lo = fast("x3_hi", 92, [P, KD, N]), fast("x3_lo", 124, [P, KD, N])
        bet_hi, bet_lo = fast("bet_hi", 48, [P, NB, D]), fast("bet_lo", 140, [P, NB, D])
        ct_hi = [fast(f"ct_hi_{b}", kb, [P, N]) for b, kb in enumerate((76, 80, 84, 88, 108, 112, 180, 184))]
        ct_lo = [fast(f"ct_lo_{b}", 4 * b, [P, N]) for b in range(NB)]

        ident = sb("ident", [P, P], F32)
        ones = sb("ones", [P, P], F32)
        node_h = sb("node_h", [P, N], F16)
        node_f = sb("node_f", [P, P], F32)
        visit_f = sb("visit_f", [P, NV], F32)
        both_v = sb("both_v", [P, 2, NV, SUPER], F32)
        dst_v, src_v = both_v[:, 0, :, :], both_v[:, 1, :, :]
        src_i = sb("src_i", [P, NV, SUPER], I32)
        rel = sb("rel", [P, NV, SUPER], F32)
        blk = sb("blk", [P, NV], F32)
        end_f = sb("end_f", [P, NB], F32)
        end_i = sb("end_i", [P, NB], I32)
        turn_f = sb("turn_f", [P, TURNS], F32)
        turn_i = sb("turn_i", [P, TURNS], I32)
        last_i = sb("last_i", [P, NV], I32)
        ends_s = sb("ends_s", [P, 2, 2, 4], F32)
        zero_s = sb("zero_s", [P, 1], F32)
        ones_r = sb("ones_r", [P, 2], F32R)
        blk_i = sb("blk_i", [P, NV], I32)
        tile_i = sb("tile_i", [P, NV], I32)
        below = sb("below", [P, NB], F32)
        first_i = sb("first_i", [P, NB], I32)
        first_f = sb("first_f", [P, NB], F32)
        hits = sb("hits", [P, 1], F32)
        covered = sb("covered", [P, 1], F32)
        open_f = sb("open_f", [P, 1], F32)
        open_p = sb("open_p", [P, 1], F32)
        rounds_f = sb("rounds_f", [P, 1], F32)
        rounds_i = sb("rounds_i", [P, 1], I32)
        idx = sb("idx", [P, RING, SUPER], I32)
        eps_s = sb("eps_s", [P, 1], F32)
        dinv = sb("dinv", [P, NB], F32)
        indeg = sb("indeg", [P, NB], F32)
        outdeg = sb("outdeg", [P, NB], F32)
        r_out = sb("r_out", [P, NB], F32)
        stats = sb("stats", [P, 4 * NB, 6], F32)
        mv = sb("mv", [P, 4 * NB, 2], F32)
        std = sb("std", [P, 4 * NB], F32)
        rstd = sb("rstd", [P, 4 * NB], F32)
        wide = sb("wide", [P, NB], F32)
        wide_n = sb("wide_n", [P, 1], F32)
        wide_i = sb("wide_i", [P, 1], I32)
        b2_s = sb("b2_s", [P, KD], F32)
        b3_s = sb("b3_s", [P, D], F32)
        low = sb("low", [P, H * NB], F32)
        den = sb("den", [P, H * NB], F32)
        rden = sb("rden", [P, H * NB], F32)

        ps = ctx.enter_context(nc.psum_tensor("ps", [P, 8, 512], F32))

        ps_flat = ps[:, :, :].rearrange("p a n -> p (a n)")

        phase = sem("phase")
        s_edges, s_x, s_w0, s_bias, s_w1h, s_w1e, s_w2 = (sem(f"loaded_{n}") for n in
            ("edges", "x", "w0", "bias", "w1h", "w1e", "w2"))
        s_whh, s_wih, s_wq, s_wkv, s_wcn = (sem(f"loaded_{n}") for n in ("whh", "wih", "wq", "wkv", "wcn"))
        s_attr = [sem(f"attr_loaded_{u}") for u in range(RING)]
        s_gath = [sem(f"gathered_{u}") for u in range(RING)]
        s_pw = [sem(f"messages_stored_{u}") for u in range(4)]
        s_out = [sem(f"out_stored_{u}") for u in range(2)]
        s_xt = [sem(f"loaded_xt_{c}") for c in range(2)]
        const_set = sem("const_set")
        dve_step = sem("dve_step")
        pool_step = sem("pool_step")
        idx_set = sem("idx_set")
        xb_set = sem("xb_set")
        below_set, below_sum, hits_set, hits_sum = (sem(n) for n in ("below_set", "below_sum", "hits_set", "hits_sum"))
        plan_set = sem("plan_set")
        rounds_done = sem("rounds_done")
        ends_set = sem("ends_set")
        gather_step, hot_step, act_round = (sem(n) for n in ("gather_step", "hot_step", "act_round"))
        dst_hot = sem("dst_hot")
        sup_mm, sup_out = sem("sup_mm"), sem("sup_out")
        seed_mm, onehot_set, count_mm, count_free, ct_set, tables_set, edge_tables_set = (sem(n) for n in
            ("seed_mm", "onehot_set", "count_mm", "count_free", "ct_set", "tables_set", "edge_tables_set"))
        adj_set, deg_mm, dinv_set, sup_scaled = (sem(n) for n in ("adj_set", "deg_mm", "dinv_set", "sup_scaled"))
        sup_split = sem("sup_split")
        l0_mm, y_set, var_set, std_set, x_set = (sem(n) for n in ("l0_mm", "y_set", "var_set", "std_set", "x_set"))
        t_mm, t_out, p_mm, p_out = (sem(n) for n in ("t_mm", "t_out", "p_mm", "p_out"))
        attr_mm, pre_set, hi_set, lo_set, edge_hot, agg_mm, agg_free, agg_out = (sem(n) for n in
            ("attr_mm", "pre_set", "hi_set", "lo_set", "edge_hot", "agg_mm", "agg_free", "agg_out"))
        row_mm, row_out, mt_mm, mt_out, gate_mm, rz_pre, rz_set, n_pre, n_set, gate_free, bn_std = (sem(n) for n in
            ("row_mm", "row_out", "mt_mm", "mt_out", "gate_mm", "rz_pre", "rz_set", "n_pre", "n_set", "gate_free", "bn_std"))
        qkv_mm, qkv_out, cn_mm, cn_out = (sem(n) for n in ("qkv_mm", "qkv_out", "cn_mm", "cn_out"))
        qk_hi, qk_lo = sem("qk_hi"), sem("qk_lo")
        wide_set, x2_out, x3_out, bet_split = sem("wide_set"), sem("x2_out"), sem("x3_out"), sem("bet_split")
        wq_split, wk_half, wk_split, wn_split, wc_split = (sem(n) for n in
            ("wq_split", "wk_half", "wk_split", "wn_split", "wc_split"))
        w1h_half, w1h_split, h_half, h_split = (sem(n) for n in ("w1h_half", "w1h_split", "h_half", "h_split"))
        bn_set, whh_half, whh_split, whh_half_late, whh_split_late, hx_half, hx_split = (sem(n) for n in
            ("bn_set", "whh_half", "whh_split", "whh_half_late", "whh_split_late", "hx_half", "hx_split"))
        w2_half, w2_split, agg_out_t = sem("w2_half"), sem("w2_split"), sem("agg_out_t")
        s_wih_b = sem("loaded_wih_b")
        wq_half, wn_half, wc_half = sem("wq_half"), sem("wn_half"), sem("wc_half")
        ct_half, ct_split = sem("ct_half"), sem("ct_split")
        s_qk = [sem(f"queries_keys_stored_{n}") for n in range(4)]
        s_head = [sem(f"head_loaded_{n}") for n in range(2)]
        s_mm, s_low, s_exp, s_prob, s_tr, s_tout, s_pv, s_att = (sem(n) for n in
            ("score_mm", "low_set", "exp_set", "prob_set", "prob_tr", "prob_t_set", "pv_mm", "att_set"))
        bet_mm, bet_out, l3_mm, l3_y = (sem(n) for n in ("bet_mm", "bet_out", "l3_mm", "l3_y"))

        def end_phase(eng, n):
            eng.drain().then_inc(phase, 1)
            eng.wait_ge(phase, 4 * n)

        def group(g):
            return g // (2 * KD), g % (2 * KD) // 2, g % 2

        def three_passes(pe, bank, k, a_hi, a_lo, b_hi, b_lo, start, stop):
            pe.matmul(bank, a_hi, b_hi, start=start, stop=False)
            pe.matmul(bank, a_hi, b_lo, start=False, stop=False)
            return pe.matmul(bank, a_lo, b_hi, start=False, stop=stop)

        def rounds(eng, body):
            eng.wait_ge(plan_set, 1)
            n = eng.value_load(rounds_i[0:1, 0:1], min_val=1, max_val=NB)
            body(0)
            with eng.If(n > 1):
                with eng.Fori(1, NB) as r:
                    body(r)

        block = ctx.enter_context(nc.Block())

        @block.sync
        def _(sp):
            sp.dma_start(edge_i[:, 0, :], dst_t).then_inc(s_edges, 16)
            sp.dma_start(edge_i[:, 1, :], src_t).then_inc(s_edges, 16)
            sp.dma_start(w0_s, w0.rearrange("(k p) n -> p k n", p=P)).then_inc(s_w0, 16)
            for c in range(2):
                sp.dma_start(xt[:, :, c * 512:(c + 1) * 512], x_t[:, c * 512:(c + 1) * 512].rearrange("(k p) n -> p k n", p=P))\
                  .then_inc(s_xt[c], 16)
            sp.dma_start(xn, x.rearrange("(b p) n -> p b n", p=P)).then_inc(s_x, 16)
            for dest, vec in ((b0_s, b0), (b1_s, b1), (brz_s, bih[0:2 * D]), (bhh_rz, bhh[0:2 * D]),
                              (bin_s, bih[2 * D:3 * D]), (bhn_s, bhh[2 * D:3 * D]), (bn_a, gamma),
                              (bn_b, beta), (mean_s, run_mean), (var_s, run_var), (b3_s[:], b3)):
                sp.dma_start(dest, vec.partition_broadcast(P)).then_inc(s_bias, 16)
            sp.dma_start(w1h_s, w1h_t.rearrange("(k p) n -> p k n", p=P)).then_inc(s_w1h, 16)
            sp.wait_ge(const_set, 7)
            sp.dma_start(w1e_s, w1e_t).then_inc(s_w1e, 16)
            for i in range(NB):
                sp.wait_ge(p_out, i + 1)
                sp.dma_start(p_dram[i * P:(i + 1) * P, :], p_s[:, i % 4, :]).then_inc(s_pw[i % 4], 16)
            sp.wait_ge(phase, 8)
            sp.dma_start(w2_s, w2_t.rearrange("(k p) n -> p k n", p=P)).then_inc(s_w2, 16)

            def edge_round(r):
                with sp.Fori(0, TURNS) as turn:
                    for u in range(RING):
                        v = turn * RING + u
                        first = sp.value_load(tile_i[0:1, bass.ds(v, 1)], min_val=0, max_val=SUPERS - 1)
                        sp.wait_ge(attr_mm, r * NV + v + 1)
                        sp.dma_start(attr_s[:, u, :], attr_t[:, bass.ds(first * (SUPER * P), SUPER * P)])\
                          .then_inc(s_attr[u], 16)
            rounds(sp, edge_round)
            sp.wait_ge(phase, 12)
            sp.dma_start(b2_s[:], b2).then_inc(s_w1e, 16)
            sp.dma_start(whh_s, whh_t.rearrange("(k p) n -> p k n", p=P)).then_inc(s_whh, 16)
            sp.dma_start(wih_b, wih_t[2 * P:4 * P, :].rearrange("(k p) n -> p k n", p=P)).then_inc(s_wih_b, 16)
            sp.wait_ge(mt_mm, 2 * KD)
            sp.dma_start(wih_a, wih_t[0:2 * P, :].rearrange("(k p) n -> p k n", p=P)).then_inc(s_wih, 16)
            sp.wait_ge(mt_out, 2 * KD)
            sp.dma_start(wq_s, wqkv[:, 0:D].rearrange("(k p) n -> p k n", p=P)).then_inc(s_wq, 16)
            sp.wait_ge(gate_mm, NB)
            sp.dma_start(wk_s, wqkv[:, D:2 * D].rearrange("(k p) n -> p k n", p=P)).then_inc(s_wkv, 16)
            sp.dma_start(wv_s, wqkv[:, 2 * D:3 * D].rearrange("(k p) n -> p k n", p=P)).then_inc(s_wkv, 16)
            for g in range(4 * KD):
                a, m, c = group(g)
                sp.wait_ge(qk_lo, g + 1)
                sp.dma_start(qk_dram[2 * a:2 * a + 2, m * P:(m + 1) * P, c * 512:(c + 1) * 512]
                             .rearrange("a p n -> p a n"), stage[g % 4][:, :, :].bitcast(F32)).then_inc(s_qk[g % 4], 16)
            for h in range(H):
                for g in range(2 * KD + h // 2 * 2, 2 * KD + h // 2 * 2 + 2):
                    sp.wait_ge(s_qk[g % 4], 16 * (g // 4 + 1))
                if h == 1:
                    sp.wait_ge(qkv_mm, 4 * KD + NB)
                if h >= 2:
                    sp.wait_ge(s_mm, NB * (h - 1))
                f = slice(h * DH, (h + 1) * DH)
                for a in range(2):
                    half = slice(a * DH, (a + 1) * DH)
                    sp.dma_start(q_h[h % 2][half, :].bitcast(F32), qk_dram[a, f, :]).then_inc(s_head[h % 2], 16)
                    sp.dma_start(k_h[h % 2][half, :, :].bitcast(F32), qk_dram[2:4, f, :].rearrange("a p n -> p a n"))\
                      .then_inc(s_head[h % 2], 16)
                if h == 1:
                    sp.dma_start(wn_s, wn.rearrange("(k p) n -> p k n", p=P)).then_inc(s_wcn, 16)
                    sp.dma_start(wc_s, wc.rearrange("(k p) n -> p k n", p=P)).then_inc(s_wcn, 16)
            for i in range(NB):
                sp.wait_ge(x_set, 3 * NB + i + 1)
                sp.dma_start(out[i * P:(i + 1) * P, :], xn[:, i, :]).then_inc(s_out[i % 2], 16)
            for u in range(2):
                sp.wait_ge(s_out[u], 16 * (NB // 2))

        @block.gpsimd
        def _(pool):
            pool.memset(ident[:], 0.0).then_inc(pool_step, 1)
            pool.iota(iota_i, pattern=[[1, N]], base=0, channel_multiplier=0).then_inc(pool_step, 1)
            pool.memset(ones[:], 1.0).then_inc(const_set, 1)
            pool.memset(eps_s[:], EPS).then_inc(const_set, 1)
            pool.memset(zero_s[:], 0.0).then_inc(const_set, 1)
            pool.wait_ge(pool_step, 2)
            pool.affine_select(out=ident[:], in_=ident[:], compare_op=ALU.not_equal, fill=1.0, base=0,
                               pattern=[[-1, P]], channel_multiplier=1).then_inc(const_set, 1)
            pool.tensor_copy(node_f[:], iota_i[:, 0:P]).then_inc(const_set, 1)
            pool.tensor_copy(visit_f[:], iota_i[:, 0:NV]).then_inc(const_set, 1)
            pool.tensor_copy(node_h[:], iota_i).then_inc(const_set, 1)
            pool.wait_ge(s_x, 16)
            pool.wait_ge(s_bias, 11 * 16)
            for i in range(NB):
                pool.tensor_tensor(xn[:, i, :], xn[:, i, :], b0_s, ALU.add).then_inc(xb_set, 1)
            pool.tensor_tensor(brz_s, brz_s, bhh_rz, ALU.add).then_inc(xb_set, 1)

            def hot_round(r):
                pool.wait_ge(tables_set, r + 1)
                pool.sem_inc(hot_step, 1)

                with pool.Fori(0, TURNS) as turn:
                    for k in range(2):
                        v = turn * RING + 2 * k
                        pool.wait_ge(onehot_set, r * NV + v + 2)
                        pool.sem_inc(hot_step, 1)
                        pool.tensor_copy(ends_s[:, k, 0, :], rel[:, bass.ds(v, 2), :].rearrange("p v j -> p (v j)"))
                        pool.tensor_copy(ends_s[:, k, 1, :], src_v[:, bass.ds(v, 2), :].rearrange("p v j -> p (v j)"))\
                            .then_inc(ends_set, 1)
                        pool.wait_ge(count_mm, r * NV + v + 1)
                        pool.wait_ge(ends_set, (r * TURNS + turn) * 2 + k + 1)
                        pool.sem_inc(hot_step, 1)
                        for n in range(SUPER):
                            ins = pool.tensor_scalar(oh_dst[:, k, n, :], node_h[:, 0:P], ends_s[:, k, 0, n:n + 1], None,
                                                     ALU.is_equal)
                        ins.then_inc(dst_hot, 2)
            rounds(pool, hot_round)
            def split(whole, hi, lo, half_set, split_set):
                for k in range(KD):
                    pool.tensor_copy(hi[k][:], whole[:, k, :]).then_inc(half_set, 1)
                for k in range(KD):
                    pool.wait_ge(half_set, k + 1)
                    pool.tensor_tensor(lo[:, k, :], whole[:, k, :], hi[k][:].bitcast(F32), ALU.subtract)\
                        .then_inc(split_set, 1)
            end_phase(pool, 1)
            pool.wait_ge(s_w1h, 16)
            split(w1h_s, w1h_hi, w1h_lo, w1h_half, w1h_split)
            end_phase(pool, 2)
            for u in range(4):
                pool.wait_ge(s_pw[u], 32)

            def gather_round(r):
                with pool.Fori(0, TURNS) as turn:
                    for u in range(RING):
                        v = turn * RING + u
                        pool.wait_ge(pre_set, r * NV + v + 1)
                        pool.sem_inc(gather_step, 1)
                        pool.tensor_copy(idx[:, u, :], src_i[:, bass.ds(v, 1), :].rearrange("p a j -> p (a j)"))\
                            .then_inc(idx_set, 1)
                        pool.wait_ge(idx_set, r * NV + v + 1)
                        pool.sem_inc(gather_step, 1)
                        for j in range(SUPER):
                            pool.indirect_dma_start(
                                out=gath[:, u, j, :], out_offset=None, in_=p_dram,
                                in_offset=bass.IndirectOffsetOnAxis(ap=idx[:, u, j:j + 1], axis=0),
                            ).then_inc(s_gath[u], 16)
            rounds(pool, gather_round)

            pool.wait_ge(s_w2, 16)
            split(w2_s, w2_hi, w2_lo, w2_half, w2_split)
            end_phase(pool, 3)
            pool.wait_ge(s_whh, 16)
            pool.wait_ge(bn_set, 1)
            for n, (k, c) in enumerate(parts[:EARLY]):
                pool.tensor_copy(whh_hi[k, c][:], whh_s[:, k, c * D:(c + 1) * D]).then_inc(whh_half, 1)
                pool.wait_ge(whh_half, n + 1)
                pool.tensor_tensor(whh_lo[k, c][:], whh_s[:, k, c * D:(c + 1) * D], whh_hi[k, c][:].bitcast(F32), ALU.subtract)\
                    .then_inc(whh_split, 1)
            pool.wait_ge(mt_out, 2 * KD)
            for i in range(NB):
                if i >= 2:
                    pool.wait_ge(gate_mm, i - 1)
                s = slice(i * P, (i + 1) * P)
                pool.tensor_copy(hx_hi[i % 2][:], xt[:, :, s]).then_inc(hx_half, 1)
                pool.wait_ge(hx_half, i + 1)
                pool.tensor_tensor(hx_lo[i % 2][:], xt[:, :, s], hx_hi[i % 2][:].bitcast(F32), ALU.subtract).then_inc(hx_split, 1)
            pool.wait_ge(gate_mm, NB)
            pool.wait_ge(s_wq, 16)
            split(wq_s, wq_hi, wq_lo, wq_half, wq_split)
            end_phase(pool, 4)
            end_phase(pool, 5)
            pool.wait_ge(s_wcn, 32)
            split(wn_s, wn_hi, wn_lo, wn_half, wn_split)
            end_phase(pool, 6)
            split(wc_s, wc_hi, wc_lo, wc_half, wc_split)
            for b in range(NB):
                pool.wait_ge(ct_half, b + 1)
                pool.tensor_tensor(ct_lo[b][:], ct[:, b, :], ct_hi[b][:].bitcast(F32), ALU.subtract)\
                    .then_inc(ct_split, 1)

        @block.scalar
        def _(act):
            def layer_std(n):
                act.wait_ge(var_set, n + 1)
                act.activation(std[:, n:n + 1], mv[:, n, 1:2], ACT.Sqrt, bias=eps_s[:, 0:1]).then_inc(std_set, 1)

            def turned(n, dest, bank):
                act.wait_ge(t_mm, n + 1)
                i = n % NB
                act.activation(dest[:, :, i * P:(i + 1) * P],
                               ps[:, bank, :].rearrange("p (k n) -> p k n", k=KD), ACT.Copy).then_inc(t_out, 1)

            for i in range(NB):
                act.wait_ge(sup_mm, i + 1)
                act.activation(sup[:, i, :], ps[:, i % 4, :], ACT.Copy).then_inc(sup_out, 1)
            def place(b):
                return ps[:, 2 * (b % 4):2 * (b % 4) + 2, :].rearrange("p a n -> p (a n)")

            act.wait_ge(seed_mm, 1)
            for b in range(4):
                act.activation(place(b), zero_s[:, 0:1].broadcast_to([P, N]), ACT.Copy).then_inc(count_free, 1)
            act.wait_ge(plan_set, 1)
            for b in range(NB):
                end = act.value_load(end_i[0:1, b:b + 1], min_val=0, max_val=NB * NV)
                act.wait_ge(count_mm, end + RING)
                act.activation(ct[:, b, :], place(b), ACT.Copy, accum_out=indeg[:, b:b + 1]).then_inc(ct_set, 1)
                act.activation(adj_r[:, b, :], place(b), ACT.Sign).then_inc(adj_set, 1)
                if b < 4:
                    act.wait_ge(ct_set, b + 1)
                    act.wait_ge(adj_set, b + 1)
                    act.activation(place(b), zero_s[:, 0:1].broadcast_to([P, N]), ACT.Copy).then_inc(count_free, 1)
            end_phase(act, 1)
            for c in range(2):
                act.wait_ge(row_mm, c + 1)
                act.activation(deg_row[0:1, c * 512:(c + 1) * 512], ps[0:1, 4 + c, :], ACT.Sqrt).then_inc(row_out, 1)
            act.wait_ge(dinv_set, 1)
            for b in range(NB):
                act.activation(sup_hi[:, b, :], sup[:, b, :], ACT.Copy, scale=dinv[:, b:b + 1]).then_inc(sup_scaled, 1)
            for i in range(NB + 2):
                if i < NB:
                    layer_std(i)
                if i >= 2:
                    n = i - 2
                    turned(n, xt, 4 + n % 2)
                    if n >= 2:
                        act.wait_ge(p_mm, n - 1)
                    act.activation(h_hi[n % 2][:], ps[:, 4 + n % 2, :].rearrange("p (k n) -> p k n", k=KD), ACT.Copy)\
                       .then_inc(h_half, 1)
            end_phase(act, 2)

            act.wait_ge(seed_mm, 2)
            for b in range(4):
                act.activation(ps[:, 4 + b, :], zero_s[:, 0:1].broadcast_to([P, D]), ACT.Copy).then_inc(agg_free, 1)

            def relu_round(r):
                def flush(v, b):
                    act.wait_ge(agg_mm, r * NV + v + (1 + RING))
                    act.sem_inc(act_round, 1)
                    bank = ps[:, bass.ds(b % 4 + 4, 1), :].rearrange("p a n -> p (a n)")
                    act.activation(arena[:, bass.ds(b * D + 92 * KB, D)], bank, ACT.Copy).then_inc(agg_out, 1)
                    act.wait_ge(agg_out, b + 1)
                    act.sem_inc(act_round, 1)
                    act.activation(bank, zero_s[:, 0:1].broadcast_to([P, D]), ACT.Copy).then_inc(agg_free, 1)

                with act.Fori(0, TURNS) as turn:
                    for u in range(RING):
                        v = turn * RING + u
                        act.wait_ge(pre_set, r * NV + v + (1 + RING))
                        act.wait_ge(agg_mm, r * NV + v + (RING - 1))
                        act.activation(msg_hi[:, u % 2, :], msg[u], ACT.Relu).then_inc(hi_set, 1)
                        ended = act.value_load(last_i[0:1, bass.ds(v, 1)], min_val=0, max_val=NB)
                        with act.If(ended > 0):
                            flush(v - 2, ended - 1)
                final = act.value_load(blk_i[0:1, NV - 1:NV], min_val=0, max_val=NB - 1)
                flush(NV - 1, final + r)
            rounds(act, relu_round)
            end_phase(act, 3)
            for b in range(NB):
                turned(NB + b, agg_hi, b % 2)
            act.activation(var_s, var_s, ACT.Sqrt, bias=eps_s[:, 0:1]).then_inc(bn_std, 1)
            for c in range(2):
                act.wait_ge(row_mm, c + 3)
                act.activation(indeg_all[:, c * 512:(c + 1) * 512], ps[:, 2 + c, :], ACT.Copy).then_inc(row_out, 1)
            act.wait_ge(mt_mm, 2 * KD)
            act.wait_ge(s_whh, 16)
            for k, c in parts[EARLY:]:
                act.activation(whh_hi[k, c][:], whh_s[:, k, c * D:(c + 1) * D], ACT.Copy).then_inc(whh_half_late, 1)
            for i in range(NB + 1):
                if i < NB:
                    act.wait_ge(rz_pre, i + 1)
                    act.activation(rz_s[:, i % 2, :], rz_s[:, i % 2, :], ACT.Sigmoid).then_inc(rz_set, 1)
                    act.wait_ge(n_pre, i + 1)
                    act.activation(n_s[:, i % 2, :], n_s[:, i % 2, :], ACT.Tanh).then_inc(n_set, 1)
                if i == NB:
                    for n in range(4):
                        turned(2 * NB + n, x2_hi, n)
                if i:
                    layer_std(NB + i - 1)
            end_phase(act, 4)
            for i in range(4, NB):
                turned(2 * NB + i, x2_hi, i % 4)
            act.wait_ge(s_wkv, 32)
            for whole, hi in ((wk_s, wk_hi), (wv_s, wv_hi)):
                for k in range(KD):
                    act.activation(hi[k][:], whole[:, k, :], ACT.Copy).then_inc(wk_half, 1)
            for g in range(4 * KD + NB):
                act.wait_ge(qkv_mm, g + 1)
                bank = ps[:, 6 + g % 2, :]
                if g < 4 * KD:
                    if g >= 4:
                        act.wait_ge(s_qk[g % 4], 16 * (g // 4))
                    act.activation(stage[g % 4][:, 0, :], bank, ACT.Copy,
                                   scale=-float(DH) ** -0.5 if g < 2 * KD else 1.0).then_inc(qk_hi, 1)
                else:
                    act.activation(v_s[:, g - 4 * KD, :], bank, ACT.Copy).then_inc(qkv_out, 1)
                if g < NB:
                    act.wait_ge(cn_mm, g + 1)
                    act.activation(cnt_n[:, g, :], ps[:, 2 + 2 * (g % 2):4 + 2 * (g % 2), :].rearrange("p a n -> p (a n)"),
                                   ACT.Copy, accum_out=outdeg[:, g:g + 1]).then_inc(cn_out, 1)
            end_phase(act, 5)

            def exps(u):
                act.wait_ge(s_low, u + 1)
                act.activation(logit[:, u % 2, :], logit[:, u % 2, :], ACT.Exp, bias=low[:, u:u + 1], scale=-1.0)\
                   .then_inc(s_exp, 1)

            def prob_out(u):
                for c in range(2):
                    act.wait_ge(s_tr, 2 * u + c + 1)
                    if u >= 2:
                        act.wait_ge(s_pv, u - 1)
                    act.activation(prob_t[:, u % 2, c * 512:(c + 1) * 512], ps[:, 4 + c, :], ACT.Copy)\
                       .then_inc(s_tout, 1)
            U = H * NB
            for u in range(U + 2):
                if u < U:
                    exps(u)
                if u >= 2:
                    prob_out(u - 2)
            end_phase(act, 6)
            for i in range(NB + 3):
                if i < NB:
                    layer_std(2 * NB + i)
                if 1 <= i <= NB:
                    turned(3 * NB + i - 1, x3_hi, (i - 1) % 2)
                if i >= 3:
                    act.wait_ge(bet_mm, i - 2)
                    act.activation(bet_hi[:, i - 3, :], ps[:, 2 + (i - 3) % 2, :], ACT.Copy).then_inc(bet_out, 1)
            for b in range(NB):
                act.activation(ct_hi[b][:], ct[:, b, :], ACT.Copy).then_inc(ct_half, 1)
            for i in range(NB):
                layer_std(3 * NB + i)

        @block.tensor
        def _(pe):
            def turn_block(n, source, bank):
                for k in range(KD):
                    mm = pe.transpose(ps[:, bank, k * P:(k + 1) * P], source[:, n % NB, k * P:(k + 1) * P], ident[:])
                mm.then_inc(t_mm, 1)

            pe.wait_ge(const_set, 7)
            pe.wait_ge(below_set, NB - 1)
            pe.matmul(ps[:, 6, 0:NB - 1], ones[:], below[:, 0:NB - 1], start=True, stop=True).then_inc(below_sum, 1)
            pe.wait_ge(s_w0, 16)
            for i in range(NB):
                if i % 4 == 0:
                    pe.wait_ge(s_xt[i // 4], 16)
                if i >= 4:
                    pe.wait_ge(sup_out, i - 3)
                if i == 5:
                    pe.wait_ge(hits_set, 1)
                    pe.matmul(ps[:, 7, 0:1], ones[:], hits[:], start=True, stop=True).then_inc(hits_sum, 1)
                for k in range(KD):
                    mm = pe.matmul(ps[:, i % 4, :], xt[:, k, i * P:(i + 1) * P], w0_s[:, k, :],
                                   start=(k == 0), stop=(k == KD - 1))
                mm.then_inc(sup_mm, 1)
            pe.sem_inc(count_mm, RING)
            pe.wait_ge(sup_out, NB)
            pe.wait_ge(hits_sum, 2)
            for bank in range(8):
                mm = pe.matmul(ps[:, bank, :], node_h[:, 0:P], node_h[:, 0:512], start=True, stop=True)
            mm.then_inc(seed_mm, 1)

            def count_round(r):
                ahead = pe.snap(r * CLEARED + r % 4 * sum(4 ** u for u in range(RING)))
                with pe.Fori(0, TURNS) as turn:
                    turn_plan = pe.snap(pe.value_load(turn_i[0:1, bass.ds(turn, 1)], min_val=CLEARED,
                                                      max_val=CLEARED * NB + CLEARED - 1) + ahead)
                    g = pe.snap((r * TURNS + turn) * RING)
                    pe.wait_ge(count_free, turn_plan // CLEARED)
                    for u in range(RING):
                        place = pe.snap(turn_plan // (4 ** u) % 4 * N)
                        pe.wait_ge(onehot_set, g + (u + 1 + RING))
                        if u % 2 == 0:
                            pe.wait_ge(dst_hot, g + (u + 2))
                        for j in range(SUPER):
                            for c in range(2):
                                mm = pe.matmul(ps_flat[:, bass.ds(place + c * 512, 512)],
                                               oh_dst[:, u // 2, u % 2 * SUPER + j, :],
                                               oh_src[:, u, j, c * 512:(c + 1) * 512],
                                               start=False, stop=False, skip_group_check=True)
                        mm.then_inc(count_mm, 1)
            rounds(pe, count_round)
            end_phase(pe, 1)

            pe.wait_ge(adj_set, 2 * NB)
            for c in range(2):
                for b in range(NB):
                    mm = pe.matmul(ps[0:2, 4 + c, :], ones_r[:], adj_r[:, b, c * 512:(c + 1) * 512],
                                   start=(b == 0), stop=(b == NB - 1))
                mm.then_inc(row_mm, 1)
            for i in range(NB):
                if i % 4 == 0:
                    pe.wait_ge(row_out, i // 4 + 1)
                pe.transpose(ps[:, 7, i:i + 1], deg_row[0:1, i * P:(i + 1) * P], ident[0:1, 0:1])
            pe.wait_ge(wide_set, 1)
            pe.matmul(ps[:, 7, NB:NB + 1], ones[:], wide_n[:], start=True, stop=True).then_inc(deg_mm, 1)
            pe.wait_ge(s_w1h, 16)
            for i in range(NB + 4):
                if i < NB:
                    if i >= 4:
                        pe.wait_ge(y_set, i - 3)
                    for b in range(NB):
                        if i == 0:
                            pe.wait_ge(sup_split, b + 1)
                        for part in (sup_hi, sup_lo):
                            mm = pe.matmul(ps[:, i % 4, :], adj_r[:, b, i * P:(i + 1) * P], part[:, b, :],
                                           start=(b == 0 and part is sup_hi), stop=(b == NB - 1 and part is sup_lo))
                    mm.then_inc(l0_mm, 1)
                if 2 <= i < NB + 2:
                    n = i - 2
                    pe.wait_ge(x_set, n + 1)
                    if n >= 2:
                        pe.wait_ge(h_split, n - 1)
                    turn_block(n, xn, 4 + n % 2)
                if i >= 4:
                    n = i - 4
                    pe.wait_ge(h_split, n + 1)
                    pe.wait_ge(w1h_split, KD)
                    if n >= 2:
                        pe.wait_ge(p_out, n - 1)
                    for k in range(KD):
                        mm = three_passes(pe, ps[:, 6 + n % 2, :], k, h_hi[n % 2][:, k, :], h_lo[n % 2][:, k, :],
                                          w1h_hi[k][:], w1h_lo[:, k, :], start=(k == 0), stop=(k == KD - 1))
                    mm.then_inc(p_mm, 1)
            end_phase(pe, 2)

            pe.sem_inc(attr_mm, RING)
            pe.sem_inc(agg_mm, RING)
            pe.wait_ge(s_w1e, 16)
            for bank in range(4, 8):
                mm = pe.matmul(ps[:, bank, :], node_h[:, 0:P], node_h[:, 0:512], start=True, stop=True)
            mm.then_inc(seed_mm, 1)

            def edge_round(r):
                def attr_products(turn, u):
                    g = r * NV + turn * RING + u
                    slot = u % RING
                    pe.wait_ge(s_attr[slot], (r * TURNS + turn + u // RING) * 16 + 16)
                    pe.wait_ge(pre_set, g + (RING - 1))
                    for j in range(SUPER):
                        mm = pe.matmul(ps[:, 2 * (u % 2) + j, :], attr_s[:, slot, j * P:(j + 1) * P], w1e_s,
                                       start=True, stop=True)
                    mm.then_inc(attr_mm, 1)

                def body(turn, last):
                    for u in range(RING):
                        if u + 3 < RING or not last:
                            attr_products(turn, u + 3)
                        v = turn * RING + u
                        b = pe.snap(pe.value_load(blk_i[0:1, bass.ds(v, 1)], min_val=0, max_val=NB - 1) + r)
                        pe.wait_ge(agg_free, b + 1)
                        if u % 2 == 0:
                            pe.wait_ge(edge_hot, (r * TURNS + turn) * 2 + u // 2 + 1)
                        pe.wait_ge(lo_set, r * NV + v + 1)
                        for j in range(SUPER):
                            for part in (msg_hi, msg_lo):
                                mm = pe.matmul(ps[:, bass.ds(b % 4 + 4, 1), :].rearrange("p a n -> p (a n)"),
                                               oh_edge[:, u // 2, u % 2 * SUPER + j, :], part[:, u % 2, j * D:(j + 1) * D],
                                               start=False, stop=False, skip_group_check=True)
                        mm.then_inc(agg_mm, 1)
                for u in range(3):
                    attr_products(0, u)
                with pe.Fori(0, TURNS - 1) as turn:
                    body(turn, False)
                body(TURNS - 1, True)
            rounds(pe, edge_round)
            end_phase(pe, 3)

            for b in range(NB):
                if b >= 2:
                    pe.wait_ge(agg_out_t, b - 1)
                turn_block(NB + b, agg, b % 2)
            for b in range(NB):
                mm = pe.matmul(ps[:, 2 + b // 4, (b % 4) * P:(b % 4 + 1) * P], indeg[:, b:b + 1].broadcast_to([P, P]), ident[:],
                               start=True, stop=True)
                if b % 4 == 3:
                    mm.then_inc(row_mm, 1)
            pe.wait_ge(w2_split, KD)
            for g in range(2 * KD):
                c, m = g // KD, g % KD
                pe.wait_ge(agg_out_t, 4 * c + 4)
                if g >= 4:
                    pe.wait_ge(mt_out, g - 3)
                f, n = slice(m * P, (m + 1) * P), slice(c * 512, (c + 1) * 512)
                for k in range(KD):
                    mm = three_passes(pe, ps[:, 4 + g % 4, :], k, w2_hi[k][:, f], w2_lo[:, k, f], agg_hi[:, k, n],
                                      agg_lo[:, k, n], start=(k == 0), stop=(k == KD - 1))
                mm.then_inc(mt_mm, 1)
            pe.wait_ge(s_whh, 16)
            pe.wait_ge(s_wih_b, 16)
            pe.wait_ge(mt_out, 2 * KD)
            for i in range(NB):
                if i >= 2:
                    pe.wait_ge(gate_free, i - 1)
                q = 4 * (i % 2)
                s = slice(i * P, (i + 1) * P)
                for n, (k, c) in enumerate([(k, 2) for k in (3, 2, 0, 1)] + [(k, c) for k in (3, 0, 1, 2) for c in range(2)]):
                    bank, start, stop = ps[:, q + c + (c == 2), :], k == 3, k == 1 and c == 2
                    if n == 2:
                        pe.wait_ge(hx_split, i + 1)
                        pe.wait_ge(whh_split, EARLY)
                    if i == 0 and (k, c) == (1, 0):
                        pe.wait_ge(whh_split_late, len(parts) - EARLY)
                    if (k, c) in parts:
                        three_passes(pe, bank, k, hx_hi[i % 2][:, k, :], hx_lo[i % 2][:, k, :], whh_hi[k, c][:], whh_lo[k, c][:],
                                     start=start, stop=stop)
                    else:
                        pe.matmul(bank, xt[:, k, s], whh_s[:, k, c * D:(c + 1) * D], start=start, stop=stop)
                for k in (2, 3, 0, 1):
                    if i == 0 and k == 0:
                        pe.wait_ge(s_wih, 16)
                    wih = wih_a if k < 2 else wih_b
                    for c in range(3):
                        mm = pe.matmul(ps[:, q + c, :], m_t[:, k, s], wih[:, k % 2, c * D:(c + 1) * D],
                                       start=(k == 2 and c == 2), stop=(k == 1))
                mm.then_inc(gate_mm, 1)
            pe.wait_ge(gate_free, NB - 1)
            for i in range(NB):
                if i == 4:
                    end_phase(pe, 4)
                pe.wait_ge(x_set, NB + i + 1)
                if i >= 4:
                    pe.wait_ge(x2_out, i - 3)
                turn_block(2 * NB + i, xn, i % 4)
            for g in range(4 * KD + NB):
                if 2 <= g < 4 * KD + 2:
                    pe.wait_ge(qk_lo, g - 1)
                if g >= 4 * KD + 2:
                    pe.wait_ge(qkv_out, g - 4 * KD - 1)
                if g == 0:
                    pe.wait_ge(wq_split, KD)
                if g == 2 * KD:
                    pe.wait_ge(wk_split, KD)
                if g == 4 * KD:
                    pe.wait_ge(wk_split, 2 * KD)
                if g < 2:
                    pe.wait_ge(x2_out, 4 * g + 4)
                for k in range(KD):
                    if g < 4 * KD:
                        a, m, c = group(g)
                        hi, lo = ((wq_hi, wq_lo), (wk_hi, wk_lo))[a]
                        f, n = slice(m * P, (m + 1) * P), slice(c * 512, (c + 1) * 512)
                        mm = three_passes(pe, ps[:, 6 + g % 2, :], k, hi[k][:, f], lo[:, k, f], x2_hi[:, k, n], x2_lo[:, k, n],
                                          start=(k == 0), stop=(k == KD - 1))
                    else:
                        n = slice((g - 4 * KD) * P, (g - 4 * KD + 1) * P)
                        mm = three_passes(pe, ps[:, 6 + g % 2, :], k, x2_hi[:, k, n], x2_lo[:, k, n], wv_hi[k][:], wv_lo[:, k, :],
                                          start=(k == 0), stop=(k == KD - 1))
                mm.then_inc(qkv_mm, 1)
                if g < NB:
                    if g >= 2:
                        pe.wait_ge(cn_out, g - 1)
                    else:
                        pe.wait_ge(x2_out, NB)
                    for b in range(NB):
                        mm = pe.transpose(ps[:, 2 + 2 * (g % 2) + b // 4, (b % 4) * P:(b % 4 + 1) * P],
                                          ct[:, b, g * P:(g + 1) * P], ident[:])
                    mm.then_inc(cn_mm, 1)
            end_phase(pe, 5)

            def scores(u):
                h, i = u // NB, u % NB
                if u >= 2:
                    pe.wait_ge(s_low, u - 1)
                if i == 0:
                    pe.wait_ge(s_head[h % 2], 64 * (h // 2 + 1))
                for c in range(2):
                    for a in range(2):
                        mm = pe.matmul(ps[:, 2 * (u % 2) + c, :], q_h[h % 2][:, i * P:(i + 1) * P],
                                       k_h[h % 2][:, a, c * 512:(c + 1) * 512], start=(a == 0), stop=(a == 1))
                mm.then_inc(s_mm, 1)

            def turn_probs(u):
                pe.wait_ge(s_prob, u + 1)
                for b in range(NB):
                    if b % 4 == 0 and u >= 1:
                        pe.wait_ge(s_tout, 2 * u - 1 + b // 4)
                    mm = pe.transpose(ps[:, 4 + b // 4, (b % 4) * P:(b % 4 + 1) * P],
                                      prob[:, u % 2, b * P:(b + 1) * P], ident[:])
                    if b % 4 == 3:
                        mm.then_inc(s_tr, 1)

            def weigh(u):
                h, i = u // NB, u % NB
                if i == 0 and h >= 2:
                    pe.wait_ge(s_att, h - 1)
                for b in range(NB):
                    if b % 4 == 0:
                        pe.wait_ge(s_tout, 2 * u + 1 + b // 4)
                    mm = pe.matmul(ps[:, 6 + h % 2, i * DH:(i + 1) * DH], prob_t[:, u % 2, b * P:(b + 1) * P],
                                   v_s[:, b, h * DH:(h + 1) * DH], start=(b == 0), stop=(b == NB - 1))
                mm.then_inc(s_pv, 1)
            U = H * NB
            for u in range(U + 3):
                if u < U:
                    scores(u)
                if 2 <= u < U + 2:
                    turn_probs(u - 2)
                if u >= 3:
                    weigh(u - 3)
            end_phase(pe, 6)

            pe.wait_ge(wn_split, KD)
            for i in range(NB + 2):
                if i < NB:
                    pe.wait_ge(x_set, 2 * NB + i + 1)
                    if i >= 2:
                        pe.wait_ge(x3_out, i - 1)
                    turn_block(3 * NB + i, xn, i % 2)
                if i >= 2:
                    n = i - 2
                    pe.wait_ge(x3_out, n + 1)
                    if n >= 2:
                        pe.wait_ge(bet_split, n - 1)
                    s = slice(n * P, (n + 1) * P)
                    for k in range(KD):
                        mm = three_passes(pe, ps[:, 2 + n % 2, :], k, x3_hi[:, k, s], x3_lo[:, k, s], wn_hi[k][:], wn_lo[:, k, :],
                                          start=(k == 0), stop=(k == KD - 1))
                    mm.then_inc(bet_mm, 1)
            pe.wait_ge(wc_split, KD)
            many = pe.value_load(wide_i[0:1, 0:1], min_val=0, max_val=NB * P)
            for i in range(NB):
                if i >= 2:
                    pe.wait_ge(l3_y, i - 1)
                s = slice(i * P, (i + 1) * P)
                for k in range(KD):
                    three_passes(pe, ps[:, 4 + 2 * (i % 2), :], k, x3_hi[:, k, s], x3_lo[:, k, s], wc_hi[k][:], wc_lo[:, k, :],
                                 start=(k == 0), stop=(k == KD - 1))
                gathered = ps[:, 5 + 2 * (i % 2), :]
                for b in range(NB):
                    if i == 0:
                        pe.wait_ge(bet_split, b + 1)
                        pe.wait_ge(ct_half, b + 1)
                    pe.matmul(gathered, ct_hi[b][:, s], bet_hi[:, b, :], start=(b == 0), stop=False)
                with pe.If(many > 0):
                    pe.wait_ge(ct_split, NB)
                    for b in range(NB):
                        pe.matmul(gathered, ct_lo[b][:, s], bet_hi[:, b, :], start=False, stop=False)
                for b in range(NB):
                    mm = pe.matmul(gathered, ct_hi[b][:, s], bet_lo[:, b, :], start=False, stop=(b == NB - 1))
                mm.then_inc(l3_mm, 1)

        @block.vector
        def _(dve):
            done = [0]

            def link(ins):
                done[0] += 1
                ins.then_inc(dve_step, 1)
                dve.wait_ge(dve_step, done[0])

            def norm_stats(n):
                link(dve.bn_stats(stats[:, n, :], y_s[:, n % 2, :]))
                dve.bn_aggr(mv[:, n, :], stats[:, n, :]).then_inc(var_set, 1)

            def norm_apply(n):
                dve.wait_ge(std_set, n + 1)
                link(dve.reciprocal(rstd[:, n:n + 1], std[:, n:n + 1]))
                dve.tensor_scalar(xn[:, n % NB, :], y_s[:, n % 2, :], mv[:, n, 0:1], rstd[:, n:n + 1],
                                  ALU.subtract, ALU.mult).then_inc(x_set, 1)

            flat = lambda t: t[:, :, :].rearrange("p v j -> p (v j)")
            dve.memset(flat(ends_f[:, 0])[:, TILES:NT], FAR)
            dve.memset(flat(ends_f[:, 1])[:, TILES:NT], 0.0)
            dve.wait_ge(s_edges, 32)
            for a in range(2):
                ins = dve.tensor_copy(flat(ends_f[:, a])[:, 0:TILES], edge_i[:, a, :])
            link(ins)
            for b in range(1, NB):
                dve.tensor_scalar(flat(plan_h[:, b % 2]), flat(ends_f[:, 0]), float(b * P), 0.0, ALU.is_lt, ALU.add,
                                  accum_out=below[:, b - 1:b]).then_inc(below_set, 1)
                dve.wait_ge(below_set, max(1, b - 1))
            dve.wait_ge(below_set, NB - 1)
            dve.wait_ge(below_sum, 1)
            link(dve.tensor_copy(first_i[:, 0:NB - 1], ps[:, 6, 0:NB - 1]))
            link(dve.tensor_scalar(first_i[:, 0:NB - 1], first_i[:, 0:NB - 1], (SUPER * P).bit_length() - 1, None,
                                   ALU.logical_shift_right))
            link(dve.tensor_copy(first_f[:, 0:NB - 1], first_i[:, 0:NB - 1]))
            dve.wait_ge(const_set, 7)
            link(dve.scalar_tensor_tensor(first_f[:, 0:NB - 1], first_f[:, 0:NB - 1], float(SUPERS - 1), visit_f[:, 1:NB],
                                          ALU.min, ALU.add))
            link(dve.tensor_scalar(blk[:], visit_f[:], first_f[:, 0:1], None, ALU.is_ge))
            for b in range(2, NB):
                link(dve.scalar_tensor_tensor(blk[:], visit_f[:], first_f[:, b - 1:b], blk[:], ALU.is_ge, ALU.add))
            dve.memset(ends_v[:, :, 0:NB, :], 0.0)
            for b in range(NB):
                link(dve.tensor_scalar(mask_h, blk[:], float(b), None, ALU.is_equal))
                mask = mask_h[:, b:NV].unsqueeze(2).broadcast_to([P, NV - b, SUPER])
                whose = plan_h if b else ends_v
                for a in range(2):
                    ins = dve.tensor_tensor(whose[:, a, b:NV, :], ends_f[:, a, 0:NV - b, :], mask, ALU.mult)
                link(ins)
                if b:
                    for a in range(2):
                        ins = dve.tensor_tensor(ends_v[:, a, b:NV, :], ends_v[:, a, b:NV, :], plan_h[:, a, b:NV, :], ALU.add)
                    link(ins)
            blk_b = blk[:].unsqueeze(2).broadcast_to([P, NV, SUPER])
            link(dve.scalar_tensor_tensor(rel[:], blk_b, -float(P), ends_v[:, 0], ALU.mult, ALU.add))
            link(dve.tensor_scalar(flat(plan_t), flat(rel), 0.0, None, ALU.is_ge))
            dve.scalar_tensor_tensor(flat(plan_t), flat(rel), float(P), flat(plan_t), ALU.is_lt, ALU.mult,
                                     accum_out=hits[:]).then_inc(hits_set, 1)
            dve.wait_ge(hits_sum, 1)
            link(dve.tensor_scalar(covered[:], ps[:, 7, 0:1], float(E), None, ALU.is_equal))
            link(dve.tensor_scalar(open_f[:], covered[:], -1.0, 1.0, ALU.mult, ALU.add))
            dve.tensor_scalar(open_p[:], open_f[:], -float(P), None, ALU.mult)
            link(dve.tensor_scalar(rounds_f[:], open_f[:], float(NB - 1), 1.0, ALU.mult, ALU.add))
            dve.tensor_copy(rounds_i[:], rounds_f[:])
            for a in range(2):
                ins = dve.tensor_scalar(flat(ends_v[:, a]), flat(ends_v[:, a]), covered[:, 0:1], None, ALU.mult)
            link(ins)
            for a in range(2):
                dve.scalar_tensor_tensor(both_v[:, a, :, :], ends_f[:, a], open_f[:, 0:1], ends_v[:, a], ALU.mult, ALU.add)
            link(dve.tensor_scalar(end_f[:, 0:NB - 1], first_f[:, 0:NB - 1], covered[:, 0:1], None, ALU.mult))
            dve.tensor_scalar(end_f[:, NB - 1:NB], covered[:], float(NV), None, ALU.mult)
            link(dve.tensor_scalar(first_f[:], visit_f[:, 1:NB + 1], open_f[:, 0:1], float(NV), ALU.mult, ALU.mult))
            link(dve.tensor_tensor(end_f[:], end_f[:], first_f[:], ALU.add))
            dve.tensor_copy(end_i[:], end_f[:])
            link(dve.tensor_scalar(blk[:], blk[:], covered[:, 0:1], None, ALU.mult))

            def edge_tables():
                link(dve.memset(step_f[:, 0:2], 0.0))
                link(dve.tensor_tensor(step_f[:, 2:NV], blk[:, 1:NV - 1], blk[:, 0:NV - 2], ALU.subtract))
                link(dve.scalar_tensor_tensor(step_f[:, 2:NV], blk[:, 0:NV - 2], 1.0, step_f[:, 2:NV], ALU.add, ALU.mult))
                link(dve.tensor_copy(last_i[:], step_f))
                link(dve.tensor_copy(blk_i[:], blk[:]))
                link(dve.tensor_tensor(step_f, visit_f[:], blk[:], ALU.subtract))
                link(dve.tensor_scalar(step_f, step_f, float(SUPERS - 1), None, ALU.min))
                link(dve.tensor_copy(tile_i[:], step_f))
                link(dve.tensor_copy(src_i[:], src_v))

            by_turn = lambda t: t[:, 0:NV].rearrange("p (n u) -> p n u", u=RING)
            link(dve.tensor_scalar(tile_f, blk[:], 4.0, -4.0, ALU.is_ge, ALU.mult))
            link(dve.tensor_tensor(tile_f, tile_f, blk[:], ALU.add))
            link(dve.tensor_scalar(turn_f[:], by_turn(blk)[:, :, RING - 1], 1.0, float(CLEARED), ALU.add, ALU.mult))
            for u in range(RING):
                link(dve.scalar_tensor_tensor(turn_f[:], by_turn(tile_f)[:, :, u], float(4 ** u), turn_f[:],
                                              ALU.mult, ALU.add))
            link(dve.tensor_copy(turn_i[:], turn_f[:]))
            link(dve.tensor_copy(ones_r[:], ones[:, 0:2]))

            def start_tables():
                link(dve.scalar_tensor_tensor(rel[:], blk_b, -float(P), dst_v, ALU.mult, ALU.add))

            def next_tables(tables_set, steps):
                dve.tensor_scalar(rel[:], rel[:], open_p[:, 0:1], None, ALU.add).then_inc(tables_set, 1)
                dve.wait_ge(tables_set, steps + 2)
                dve.sem_inc(rounds_done, 1)

            start_tables()
            dve.sem_inc(hits_sum, 1)
            dve.sem_inc(tables_set, 1)
            dve.sem_inc(onehot_set, RING)
            dve.sem_inc(plan_set, 1)

            def count_round(r):
                with dve.Fori(0, TURNS) as turn:
                    for n in range(RING):
                        if n % 2 == 0:
                            dve.wait_ge(ends_set, (r * TURNS + turn) * 2 + n // 2 + 1)
                        dve.wait_ge(count_mm, r * NV + turn * RING + n + 1)
                        for j in range(SUPER):
                            t = n % 2 * SUPER + j
                            if n % 2:
                                dve.tensor_scalar(oh_dst[:, n // 2, t, :], node_h[:, 0:P],
                                                  ends_s[:, n // 2, 0, t:t + 1], None, ALU.is_equal)
                            ins = dve.tensor_scalar(oh_src[:, n, j, :], node_h[:], ends_s[:, n // 2, 1, t:t + 1], None,
                                                    ALU.is_equal)
                        ins.then_inc(onehot_set, 1)
                dve.wait_ge(dst_hot, r * NV + NV)
                dve.wait_ge(onehot_set, r * NV + NV + RING)
                next_tables(tables_set, r)
            rounds(dve, count_round)
            end_phase(dve, 1)

            for b in range(NB):
                diag = adj_r[:, b, b * P:(b + 1) * P]
                dve.tensor_tensor(diag, diag.bitcast(F32), ident[:], ALU.add).then_inc(adj_set, 1)
            dve.tensor_scalar(wide[:], indeg[:], 4096.0, 0.0, ALU.is_gt, ALU.add, accum_out=wide_n[:]).then_inc(wide_set, 1)
            edge_tables()
            dve.wait_ge(deg_mm, 1)
            dve.reciprocal(dinv[:], ps[:, 7, 0:NB]).then_inc(dinv_set, 1)
            dve.tensor_copy(wide_i[:], ps[:, 7, NB:NB + 1])
            dve.wait_ge(dinv_set, 1)
            for b in range(NB):
                dve.wait_ge(sup_scaled, b + 1)
                dve.scalar_tensor_tensor(sup_lo[:, b, :], sup[:, b, :], dinv[:, b:b + 1], sup_hi[:, b, :].bitcast(F32),
                                         ALU.mult, ALU.subtract).then_inc(sup_split, 1)
            dve.wait_ge(xb_set, NB + 1)

            def messages(n):
                dve.wait_ge(p_mm, n + 1)
                if n >= 4:
                    dve.wait_ge(s_pw[n % 4], 16)
                dve.tensor_tensor(p_s[:, n % 4, :], ps[:, 6 + n % 2, :], b1_s, ALU.add).then_inc(p_out, 1)

            for i in range(NB + 4):
                if i < NB:
                    dve.wait_ge(l0_mm, i + 1)
                    if i >= 2:
                        dve.wait_ge(x_set, i - 1)
                    dve.scalar_tensor_tensor(y_s[:, i % 2, :], ps[:, i % 4, :], dinv[:, i:i + 1], xn[:, i, :],
                                             ALU.mult, ALU.add).then_inc(y_set, 1)
                    dve.wait_ge(y_set, i + 1)
                    norm_stats(i)
                if 1 <= i <= NB:
                    norm_apply(i - 1)
                if 3 <= i < NB + 3:
                    n = i - 3
                    dve.wait_ge(h_half, n + 1)
                    dve.tensor_tensor(h_lo[n % 2][:], ps[:, 4 + n % 2, :].rearrange("p (k n) -> p k n", k=KD),
                                      h_hi[n % 2][:].bitcast(F32), ALU.subtract).then_inc(h_split, 1)
                if i >= 4:
                    messages(i - 4)
            end_phase(dve, 2)

            start_tables()
            dve.sem_inc(edge_tables_set, 1)
            dve.sem_inc(pre_set, RING)

            def edge_round(r):
                def one_hots(turn, k):
                    v = turn * RING + 2 * k
                    dve.wait_ge(agg_mm, r * NV + v + 2)
                    where = rel[:, bass.ds(v, 2), :]
                    dve.tensor_tensor(oh_edge[:, k, :, :], node_f[:].unsqueeze(1).broadcast_to([P, 4, P]),
                                      where.rearrange("p v j -> p (v j)").unsqueeze(2).broadcast_to([P, 4, P]),
                                      ALU.is_equal).then_inc(edge_hot, 1)

                def add(turn, u):
                    dve.wait_ge(attr_mm, r * NV + turn * RING + u + (1 + RING))
                    dve.wait_ge(s_gath[u % RING], (r * TURNS + turn + u // RING) * 32 + 32)
                    dve.tensor_tensor(msg[u % RING], ps[:, 2 * (u % 2):2 * (u % 2) + 2, :].rearrange("p a n -> p (a n)"),
                                      gath[:, u % RING, :, :].rearrange("p j n -> p (j n)"), ALU.add).then_inc(pre_set, 1)

                def low_part(turn, u):
                    dve.wait_ge(hi_set, r * NV + turn * RING + u + 1)
                    dve.scalar_tensor_tensor(msg_lo[:, u % 2, :], msg[u], 0.0, msg_hi[:, u % 2, :].bitcast(F32),
                                             ALU.max, ALU.subtract).then_inc(lo_set, 1)

                def body(turn, last):
                    for u in range(RING):
                        if u % 2 == 0:
                            one_hots(turn, u // 2)
                        low_part(turn, u)
                        if u + 2 < RING or not last:
                            add(turn, u + 2)
                add(0, 0)
                add(0, 1)
                with dve.Fori(0, TURNS - 1) as turn:
                    body(turn, False)
                body(TURNS - 1, True)
                dve.wait_ge(edge_hot, r * (TURNS * 2) + TURNS * 2)
                next_tables(edge_tables_set, r)

            rounds(dve, edge_round)
            end_phase(dve, 3)

            def turned_low(n, x_hi, x_lo, bank, x_out):
                dve.wait_ge(t_out, n + 1)
                i = n % NB
                c = slice(i * P, (i + 1) * P)
                dve.tensor_tensor(x_lo[:, :, c], ps[:, bank, :].rearrange("p (k n) -> p k n", k=KD),
                                  x_hi[:, :, c].bitcast(F32), ALU.subtract).then_inc(x_out, 1)

            for b in range(NB):
                turned_low(NB + b, agg_hi, agg_lo, b % 2, agg_out_t)
            dve.wait_ge(bn_std, 1)
            link(dve.reciprocal(var_s, var_s))
            link(dve.tensor_tensor(bn_a, bn_a, var_s, ALU.mult))
            link(dve.tensor_tensor(mean_s, mean_s, bn_a, ALU.mult))
            link(dve.tensor_tensor(bn_b, bn_b, mean_s, ALU.subtract))
            dve.sem_inc(bn_set, 1)
            dve.wait_ge(s_w1e, 32)
            for g in range(2 * KD):
                c, m = g // KD, g % KD
                dve.wait_ge(row_out, c + 3)
                dve.wait_ge(mt_mm, g + 1)
                dve.scalar_tensor_tensor(m_t[:, m, c * 512:(c + 1) * 512], indeg_all[:, c * 512:(c + 1) * 512], b2_s[:, m:m + 1],
                                         ps[:, 4 + g % 4, :], ALU.mult, ALU.add).then_inc(mt_out, 1)
            for n, (k, c) in enumerate(parts[EARLY:]):
                dve.wait_ge(whh_half_late, n + 1)
                dve.tensor_tensor(whh_lo[k, c][:], whh_s[:, k, c * D:(c + 1) * D], whh_hi[k, c][:].bitcast(F32), ALU.subtract)\
                   .then_inc(whh_split_late, 1)
            for i in range(NB + 1):
                if i < NB:
                    q = 4 * (i % 2)
                    rz, new, dif = rz_s[:, i % 2, :], n_s[:, i % 2, :], d_s[:, i % 2, :]
                    dve.wait_ge(gate_mm, i + 1)
                    dve.tensor_tensor(rz, ps[:, q:q + 2, :].rearrange("p a n -> p (a n)"), brz_s, ALU.add)\
                       .then_inc(rz_pre, 1)
                    link(dve.tensor_tensor(new, ps[:, q + 3, :], bhn_s, ALU.add))
                    link(dve.tensor_tensor(dif, ps[:, q + 2, :], bin_s, ALU.add))
                    dve.sem_inc(gate_free, 1)
                    dve.wait_ge(rz_set, i + 1)
                    link(dve.tensor_tensor(new, new, rz[:, 0:D], ALU.mult))
                    dve.tensor_tensor(new, new, dif, ALU.add).then_inc(n_pre, 1)
                    dve.wait_ge(n_set, i + 1)
                    link(dve.tensor_tensor(dif, xn[:, i, :], new, ALU.subtract))
                    link(dve.tensor_tensor(dif, dif, rz[:, D:2 * D], ALU.mult))
                    link(dve.tensor_tensor(dif, dif, new, ALU.add))
                    link(dve.tensor_tensor(dif, dif, bn_a, ALU.mult))
                    link(dve.tensor_tensor(dif, dif, bn_b, ALU.add))
                    link(dve.scalar_tensor_tensor(y_s[:, i % 2, :], xn[:, i, :], 2.0, dif, ALU.mult, ALU.add))
                    norm_stats(NB + i)
                if i:
                    norm_apply(NB + i - 1)
            end_phase(dve, 4)

            for i in range(NB):
                turned_low(2 * NB + i, x2_hi, x2_lo, i % 4, x2_out)
            for n, (whole, hi, lo) in enumerate(((wk_s, wk_hi, wk_lo), (wv_s, wv_hi, wv_lo))):
                for k in range(KD):
                    dve.wait_ge(wk_half, n * KD + k + 1)
                    dve.tensor_tensor(lo[:, k, :], whole[:, k, :], hi[k][:].bitcast(F32), ALU.subtract).then_inc(wk_split, 1)
            for g in range(4 * KD):
                dve.wait_ge(qk_hi, g + 1)
                part = stage[g % 4]
                dve.scalar_tensor_tensor(part[:, 1, :], ps[:, 6 + g % 2, :], -float(DH) ** -0.5 if g < 2 * KD else 1.0,
                                         part[:, 0, :].bitcast(F32), ALU.mult, ALU.subtract).then_inc(qk_lo, 1)
            dve.wait_ge(cn_out, NB)
            dve.wait_ge(qkv_mm, 4 * KD)
            for i in range(NB):
                dve.tensor_scalar(no_edge[:, i, :], cnt_n[:, i, :], 0.0, BIG, ALU.is_equal, ALU.mult)
            end_phase(dve, 5)

            def lowest(u):
                dve.wait_ge(s_mm, u + 1)
                if u >= 2:
                    dve.wait_ge(s_prob, u - 1)
                dve.tensor_tensor_reduce(out=logit[:, u % 2, :],
                                         in0=ps[:, 2 * (u % 2):2 * (u % 2) + 2, :].rearrange("p a n -> p (a n)"),
                                         in1=no_edge[:, u % NB, :], scale=1.0, scalar=3.0e38, op0=ALU.add,
                                         op1=ALU.min, accum_out=low[:, u:u + 1]).then_inc(s_low, 1)

            def probs(u):
                dve.wait_ge(s_exp, u + 1)
                if u >= 2:
                    dve.wait_ge(s_tr, 2 * u - 2)
                dve.scalar_tensor_tensor(prob[:, u % 2, :], logit[:, u % 2, :], 1.0, cnt_n[:, u % NB, :], ALU.mult,
                                         ALU.mult, accum_out=den[:, u:u + 1]).then_inc(s_prob, 1)

            def head_out(h):
                dve.wait_ge(s_pv, NB * (h + 1))
                c = slice(h * NB, (h + 1) * NB)
                link(dve.tensor_scalar(rden[:, c], den[:, c], TINY, None, ALU.max))
                link(dve.reciprocal(rden[:, c], rden[:, c]))
                dve.tensor_tensor(att[:, :, h * DH:(h + 1) * DH], ps[:, 6 + h % 2, :].rearrange("p (i f) -> p i f", i=NB),
                                  rden[:, c].unsqueeze(2).broadcast_to([P, NB, DH]), ALU.mult).then_inc(s_att, 1)
            U = H * NB
            for u in range(U + 1):
                if u < U:
                    lowest(u)
                if u >= 1:
                    probs(u - 1)
                if u >= NB + 4 and (u - 4) % NB == 0:
                    head_out((u - 4) // NB - 1)
            head_out(H - 1)
            dve.wait_ge(s_att, H)
            end_phase(dve, 6)

            for i in range(NB + 5):
                if i < NB:
                    n = 2 * NB + i
                    if i >= 2:
                        dve.wait_ge(x_set, n - 1)
                    link(dve.tensor_tensor(y_s[:, i % 2, :], xn[:, i, :], att[:, i, :], ALU.add))
                    norm_stats(n)
                if 1 <= i <= NB:
                    norm_apply(2 * NB + i - 1)
                if 2 <= i < NB + 2:
                    turned_low(3 * NB + i - 2, x3_hi, x3_lo, i % 2, x3_out)
                if i >= 5:
                    n = i - 5
                    dve.wait_ge(bet_out, n + 1)
                    dve.tensor_tensor(bet_lo[:, n, :], ps[:, 2 + n % 2, :], bet_hi[:, n, :].bitcast(F32), ALU.subtract)\
                       .then_inc(bet_split, 1)
            link(dve.reciprocal(r_out[:], outdeg[:]))
            for i in range(NB + 1):
                if i < NB:
                    n = 3 * NB + i
                    dve.wait_ge(l3_mm, i + 1)
                    if i >= 2:
                        dve.wait_ge(x_set, n - 1)
                    y = y_s[:, i % 2, :]
                    dve.wait_ge(x_set, 2 * NB + i + 1)
                    link(dve.scalar_tensor_tensor(y, ps[:, 5 + 2 * (i % 2), :], r_out[:, i:i + 1], xn[:, i, :],
                                                  ALU.mult, ALU.add))
                    link(dve.tensor_tensor(y, y, b3_s[:], ALU.add))
                    dve.tensor_tensor(y, y, ps[:, 4 + 2 * (i % 2), :], ALU.add).then_inc(l3_y, 1)
                    dve.wait_ge(l3_y, i + 1)
                    norm_stats(n)
                if i:
                    norm_apply(3 * NB + i - 1)


def build(nc, aps, out):
    gnn_kernel(nc, *aps, out)


def kernel(**inputs):
    import numpy as _np
    import concourse.bacc as _bacc
    from concourse import mybir as _mybir
    from concourse.bass_utils import run_bass_kernel_spmd as _run

    def a(name):
        return _np.asarray(inputs[name])

    def c(v):
        return _np.ascontiguousarray(v)

    x, w1 = a("x"), a("L1_gnn_W1")
    hd = x.shape[1]
    tiles = a("src").shape[0] // 128
    laid = {
        "x": c(x),
        "x_t": c(x.T),
        "src_t": c(a("src").reshape(tiles, 128).T),
        "dst_t": c(a("dst").reshape(tiles, 128).T),
        "attr_t": c(a("edge_attr_128").T),
        "w0": c(a("L0_gnn_weight")),
        "b0": c(a("L0_gnn_bias")),
        "w1h_t": c(w1[:, :hd].T),
        "w1e_t": c(w1[:, hd:].T),
        "b1": c(a("L1_gnn_b1")),
        "w2_t": c(a("L1_gnn_W2").T),
        "b2": c(a("L1_gnn_b2").reshape(-1, 128).T),
        "wih_t": c(a("L1_gnn_W_ih").T),
        "whh_t": c(a("L1_gnn_W_hh").T),
        "bih": c(a("L1_gnn_b_ih")),
        "bhh": c(a("L1_gnn_b_hh")),
        "gamma": c(a("L1_gnn_gamma")),
        "beta": c(a("L1_gnn_beta")),
        "run_mean": c(a("L1_gnn_run_mean")),
        "run_var": c(a("L1_gnn_run_var")),
        "wqkv": c(a("L2_gnn_W")),
        "wc": c(a("L3_gnn_wc")),
        "wn": c(a("L3_gnn_wn")),
        "b3": c(a("L3_gnn_bias")),
    }
    nc = _bacc.Bacc("TRN2", target_bir_lowering=False, num_devices=1)
    arrays, aps = {}, []
    for name, value in laid.items():
        arrays[f"in_{name}_dram"] = value
        aps.append(nc.dram_tensor(f"in_{name}_dram", value.shape, _mybir.dt.from_np(value.dtype),
                                  kind="ExternalInput").ap())
    out = nc.dram_tensor("out_0_dram", x.shape, _mybir.dt.float32, kind="ExternalOutput").ap()
    build(nc, aps, out)
    r = _run(nc, [arrays], core_ids=[0])
    return r.results[0]["out_0_dram"]
```
